# Optimizing a Trainium2 kernel written in Bass

```python
import numpy as np
import jax
import jax.numpy as jnp

def _softmax(x, axis=-1):
    return jax.nn.softmax(x, axis=axis)

def _gelu(x):
    return jax.nn.gelu(x, approximate=True)

def _silu(x):
    return jax.nn.silu(x)

def _sigmoid(x):
    return jax.nn.sigmoid(x)

def _layernorm(x, axis=-1, eps=1e-05):
    m = jnp.mean(x, axis=axis, keepdims=True)
    v = jnp.var(x, axis=axis, keepdims=True)
    return (x - m) / jnp.sqrt(v + eps)

def _scatter_add(tgt, idx, src, axis=0):
    return tgt.at[idx].add(src)

def _segment_sum(src, seg, n):
    return jax.ops.segment_sum(src, seg, n)
kernel_name = 'mk_prb_d2_jaxref_r8_e8fcba'

def setup_inputs(seed: int=0):
    np.random.seed(seed)
    _w = jnp.asarray

    def _L0_attn_setup():
        import jax, jax.numpy as jnp
        import numpy as np
        D_MODEL = 128
        N_HEADS = 16
        D_HEAD = 64
        BATCH = 4
        SEQ = 256
        NEG = -1000000000.0
        key = jax.random.key(seed)
        k1, k2, k3, k4, k5 = jax.random.split(key, 5)
        x = jax.random.normal(k1, (BATCH, SEQ, D_MODEL), dtype=jnp.float32)
        std = 0.02
        wq = jax.random.normal(k2, (N_HEADS, D_HEAD, D_MODEL), dtype=jnp.float32) * std
        wk = jax.random.normal(k3, (N_HEADS, D_HEAD, D_MODEL), dtype=jnp.float32) * std
        wv = jax.random.normal(k4, (N_HEADS, D_HEAD, D_MODEL), dtype=jnp.float32) * std
        wo = jax.random.normal(k5, (D_MODEL, N_HEADS * D_HEAD), dtype=jnp.float32) * std
        return {'x': x, 'wq': wq, 'wk': wk, 'wv': wv, 'wo': wo}
    _L0_attn_in = _L0_attn_setup()

    def _L0_ffn_setup():
        import jax, jax.numpy as jnp
        import numpy as np
        D_MODEL = 128
        D_FF = 512
        N_EXPERTS = 8
        D_EXPERT = D_FF // N_EXPERTS
        TOP_K = 2
        LB_WEIGHT = 0.01
        B, S = (4, 256)

        def _top_k_softmax(logits, k):
            vals, _ = jax.lax.top_k(logits, k)
            thresh = vals[..., -1:]
            masked = jnp.where(logits >= thresh, logits, -jnp.inf)
            return jax.nn.softmax(masked, axis=-1)
        key = jax.random.key(seed)
        ks = jax.random.split(key, 8)
        x = jax.random.normal(ks[0], (B, S, D_MODEL), dtype=jnp.float32)
        w1 = jax.random.normal(ks[1], (N_EXPERTS, D_MODEL, D_EXPERT), dtype=jnp.float32) * (1.0 / np.sqrt(D_MODEL))
        b1 = jnp.zeros((N_EXPERTS, D_EXPERT), dtype=jnp.float32)
        w2 = jax.random.normal(ks[2], (N_EXPERTS, D_EXPERT, D_MODEL), dtype=jnp.float32) * (1.0 / np.sqrt(D_EXPERT))
        b2 = jnp.zeros((N_EXPERTS, D_MODEL), dtype=jnp.float32)
        centroids = jax.random.normal(ks[3], (N_EXPERTS, D_MODEL), dtype=jnp.float32) * 0.02
        w_route = jax.random.normal(ks[4], (N_EXPERTS, D_MODEL), dtype=jnp.float32) * (1.0 / np.sqrt(D_MODEL))
        return {'x': x, 'w1': w1, 'b1': b1, 'w2': w2, 'b2': b2, 'centroids': centroids, 'w_route': w_route}
    _L0_ffn_in = _L0_ffn_setup()

    def _L1_attn_setup():
        import jax, jax.numpy as jnp
        import numpy as np
        D_MODEL = 128
        D_STATE = 64
        HEADDIM = 64
        EXPAND = 2
        D_INNER = D_MODEL * EXPAND
        NHEADS = D_INNER // HEADDIM
        D_IN_PROJ = 2 * D_INNER + 2 * D_STATE + NHEADS
        BATCH, SEQLEN = (4, 512)

        def layernorm(x, w, b, eps=1e-05):
            mu = jnp.mean(x, axis=-1, keepdims=True)
            var = jnp.mean(jnp.square(x - mu), axis=-1, keepdims=True)
            return (x - mu) * jax.lax.rsqrt(var + eps) * w + b

        def _selective_scan(x_multi, A, Bm, Cm, dt):
            Bb, L, H, P = x_multi.shape
            N = Bm.shape[-1]
            dA = jnp.minimum(jnp.exp(dt * A[None, None, :]), 0.99)

            def step(h, inp):
                x_t, B_t, C_t, dA_t = inp
                dBx = jnp.einsum('bhp,bn->bhpn', x_t, B_t)
                h = jnp.clip(dA_t[:, :, None, None] * h + dBx, -10.0, 10.0)
                y_t = jnp.einsum('bn,bhpn->bhp', C_t, h)
                return (h, y_t)
            h0 = jnp.zeros((Bb, H, P, N), dtype=x_multi.dtype)
            xs = (jnp.moveaxis(x_multi, 1, 0), jnp.moveaxis(Bm, 1, 0), jnp.moveaxis(Cm, 1, 0), jnp.moveaxis(dA, 1, 0))
            _, y = jax.lax.scan(step, h0, xs)
            return jnp.moveaxis(y, 0, 1)
        key = jax.random.key(seed)
        ks = jax.random.split(key, 5)
        x = jax.random.normal(ks[0], (BATCH, SEQLEN, D_MODEL), dtype=jnp.float32)
        in_proj_w = jax.random.normal(ks[1], (D_IN_PROJ, D_MODEL), dtype=jnp.float32) * 0.5 * np.sqrt(2.0 / (D_IN_PROJ + D_MODEL))
        out_proj_w = jax.random.normal(ks[2], (D_MODEL, D_INNER), dtype=jnp.float32) * 0.5 * np.sqrt(2.0 / (D_MODEL + D_INNER))
        A_log = jnp.log(jnp.arange(1, NHEADS + 1, dtype=jnp.float32))
        dt_bias = jax.random.normal(ks[3], (NHEADS,), dtype=jnp.float32) * 0.01 + 0.1
        Dparam = jnp.ones((NHEADS,), dtype=jnp.float32)
        return {'x': x, 'in_proj_w': in_proj_w, 'out_proj_w': out_proj_w, 'A_log': A_log, 'dt_bias': dt_bias, 'Dparam': Dparam, 'ln_w': jnp.ones((D_INNER,), jnp.float32), 'ln_b': jnp.zeros((D_INNER,), jnp.float32), 'ni_w': jnp.ones((D_MODEL,), jnp.float32), 'ni_b': jnp.zeros((D_MODEL,), jnp.float32), 'no_w': jnp.ones((D_MODEL,), jnp.float32), 'no_b': jnp.zeros((D_MODEL,), jnp.float32)}
    _L1_attn_in = _L1_attn_setup()

    def _L1_ffn_setup():
        import jax, jax.numpy as jnp
        import numpy as np
        DIM = 128
        DEPTH = 6
        HEADS = 16
        DIM_HEAD = 64
        WINDOW = 32
        INNER = HEADS * DIM_HEAD
        DIM_INNER = int(DIM * 4 * 2 / 3)
        QK_SCALE = 8.0

        def shift_tokens(t):
            a, s = jnp.split(t, 2, -1)
            s = jnp.pad(s, ((0, 0), (1, 0), (0, 0)))[:, :-1]
            return jnp.concatenate([a, s], -1)

        def l2norm(t):
            return t / jnp.maximum(jnp.linalg.norm(t, axis=-1, keepdims=True), 1e-12)

        def rotate_half(x):
            x1, x2 = jnp.split(x, 2, -1)
            return jnp.concatenate([-x2, x1], -1)

        def rotary_tables(n):
            half = jnp.arange(0, DIM_HEAD, 2, dtype=jnp.float32)
            inv_freq = 1.0 / 10000.0 ** (half / DIM_HEAD)
            t = jnp.arange(n, dtype=jnp.float32)
            freqs = t[:, None] * inv_freq[None, :]
            freqs = jnp.concatenate([freqs, freqs], -1)
            base_scale = (half + 0.4 * DIM_HEAD) / (1.4 * DIM_HEAD)
            power = (t - n // 2) / (WINDOW // 2)
            scale = base_scale[None, :] ** power[:, None]
            scale = jnp.concatenate([scale, scale], -1)
            return (freqs, scale)

        def local_attention(q, k, v):
            b, h, n, d = q.shape
            w = WINDOW
            nw = n // w
            bq = q.reshape(b, h, nw, w, d)
            bk = k.reshape(b, h, nw, w, d)
            bv = v.reshape(b, h, nw, w, d)

            def look(t):
                p = jnp.pad(t, ((0, 0), (0, 0), (1, 0), (0, 0), (0, 0)))
                return jnp.concatenate([p[:, :, :nw], p[:, :, 1:]], axis=3)
            bk2, bv2 = (look(bk), look(bv))
            seq = jnp.arange(n).reshape(nw, w)
            seq_p = jnp.pad(seq, ((1, 0), (0, 0)), constant_values=-1)
            jt = jnp.concatenate([seq_p[:nw], seq_p[1:]], axis=1)
            it = seq[:, :, None]
            jb = jt[:, None, :]
            mask = (it < jb) | (it > jb + w) | (jb == -1)
            sim = jnp.einsum('bhwie,bhwje->bhwij', bq, bk2) * QK_SCALE
            sim = jnp.where(mask, -jnp.finfo(sim.dtype).max, sim)
            attn = jax.nn.softmax(sim, -1)
            out = jnp.einsum('bhwij,bhwje->bhwie', attn, bv2)
            return out.reshape(b, h, n, d)

        def attn_layer(x, Wqkv, qs, ksc, Wo):
            b, n, _ = x.shape
            qkv = x @ Wqkv
            q, k, v = jnp.split(qkv, 3, -1)
            sh = lambda t: t.reshape(b, n, HEADS, DIM_HEAD).transpose(0, 2, 1, 3)
            q, k, v = (sh(q), sh(k), sh(v))
            q = l2norm(q) * qs
            k = l2norm(k) * ksc
            freqs, scale = rotary_tables(n)
            cos, sin = (jnp.cos(freqs), jnp.sin(freqs))
            q = q * cos * scale + rotate_half(q) * sin * scale
            inv = 1.0 / scale
            k = k * cos * inv + rotate_half(k) * sin * inv
            out = local_attention(q, k, v)
            out = out.transpose(0, 2, 1, 3).reshape(b, n, INNER)
            return out @ Wo

        def ffn_layer(x, g, bln, W1, b1, W2, b2):
            mu = x.mean(-1, keepdims=True)
            var = ((x - mu) ** 2).mean(-1, keepdims=True)
            xn = (x - mu) / jnp.sqrt(var + 1e-05) * g + bln
            hg = xn @ W1 + b1
            a, gate = jnp.split(hg, 2, -1)
            return a * jax.nn.gelu(gate, approximate=False) @ W2 + b2
        key = jax.random.key(seed)
        ks = jax.random.split(key, 8)
        B, N = (2, 256)
        init = lambda k, shape: jax.random.normal(k, shape, jnp.float32) * 0.02
        return {'x': jax.random.normal(ks[0], (B, N, DIM), jnp.float32), 'Wqkv': init(ks[1], (DEPTH, DIM, 3 * INNER)), 'q_scale': jnp.ones((DEPTH, DIM_HEAD), jnp.float32), 'k_scale': jnp.ones((DEPTH, DIM_HEAD), jnp.float32), 'Wo': init(ks[2], (DEPTH, INNER, DIM)), 'ln_g': jnp.ones((DEPTH, DIM), jnp.float32), 'ln_b': jnp.zeros((DEPTH, DIM), jnp.float32), 'W1': init(ks[3], (DEPTH, DIM, 2 * DIM_INNER)), 'b1': jnp.zeros((DEPTH, 2 * DIM_INNER), jnp.float32), 'W2': init(ks[4], (DEPTH, DIM_INNER, DIM)), 'b2': jnp.zeros((DEPTH, DIM), jnp.float32)}
    _L1_ffn_in = _L1_ffn_setup()
    _d = {'L0_attn_x': _L0_attn_in['x'], 'L0_attn_wq': _L0_attn_in['wq'], 'L0_attn_wk': _L0_attn_in['wk'], 'L0_attn_wv': _L0_attn_in['wv'], 'L0_attn_wo': _L0_attn_in['wo'], 'L0_ffn_w1': _L0_ffn_in['w1'], 'L0_ffn_b1': _L0_ffn_in['b1'], 'L0_ffn_w2': _L0_ffn_in['w2'], 'L0_ffn_b2': _L0_ffn_in['b2'], 'L0_ffn_centroids': _L0_ffn_in['centroids'], 'L0_ffn_w_route': _L0_ffn_in['w_route'], 'L1_attn_in_proj_w': _L1_attn_in['in_proj_w'], 'L1_attn_out_proj_w': _L1_attn_in['out_proj_w'], 'L1_attn_A_log': _L1_attn_in['A_log'], 'L1_attn_dt_bias': _L1_attn_in['dt_bias'], 'L1_attn_Dparam': _L1_attn_in['Dparam'], 'L1_attn_ln_w': _L1_attn_in['ln_w'], 'L1_attn_ln_b': _L1_attn_in['ln_b'], 'L1_attn_ni_w': _L1_attn_in['ni_w'], 'L1_attn_ni_b': _L1_attn_in['ni_b'], 'L1_attn_no_w': _L1_attn_in['no_w'], 'L1_attn_no_b': _L1_attn_in['no_b'], 'L1_ffn_Wqkv': _L1_ffn_in['Wqkv'], 'L1_ffn_q_scale': _L1_ffn_in['q_scale'], 'L1_ffn_k_scale': _L1_ffn_in['k_scale'], 'L1_ffn_Wo': _L1_ffn_in['Wo'], 'L1_ffn_ln_g': _L1_ffn_in['ln_g'], 'L1_ffn_ln_b': _L1_ffn_in['ln_b'], 'L1_ffn_W1': _L1_ffn_in['W1'], 'L1_ffn_b1': _L1_ffn_in['b1'], 'L1_ffn_W2': _L1_ffn_in['W2'], 'L1_ffn_b2': _L1_ffn_in['b2']}
    _x0 = _d['L0_attn_x']
    _d['L0_attn_x'] = jax.random.normal(jax.random.fold_in(jax.random.key(seed), 1), (16, 256, 128), dtype=_x0.dtype)
    del _x0
    return _d

def reference(L0_attn_x, L0_attn_wq, L0_attn_wk, L0_attn_wv, L0_attn_wo, L0_ffn_w1, L0_ffn_b1, L0_ffn_w2, L0_ffn_b2, L0_ffn_centroids, L0_ffn_w_route, L1_attn_in_proj_w, L1_attn_out_proj_w, L1_attn_A_log, L1_attn_dt_bias, L1_attn_Dparam, L1_attn_ln_w, L1_attn_ln_b, L1_attn_ni_w, L1_attn_ni_b, L1_attn_no_w, L1_attn_no_b, L1_ffn_Wqkv, L1_ffn_q_scale, L1_ffn_k_scale, L1_ffn_Wo, L1_ffn_ln_g, L1_ffn_ln_b, L1_ffn_W1, L1_ffn_b1, L1_ffn_W2, L1_ffn_b2):

    def _L0_attn_ref(x, wq, wk, wv, wo):
        import jax, jax.numpy as jnp
        import numpy as np
        D_MODEL = 128
        N_HEADS = 16
        D_HEAD = 64
        BATCH = 4
        SEQ = 256
        NEG = -1000000000.0
        b, s, _ = x.shape
        scale = jnp.sqrt(jnp.asarray(D_HEAD, x.dtype))
        q = jnp.einsum('bsd,hed->bhse', x, wq)
        k = jnp.einsum('bsd,hed->bhse', x, wk)
        v = jnp.einsum('bsd,hed->bhse', x, wv)
        scores = jnp.einsum('bhse,bhte->bhst', q, k) / scale
        causal_mask = jnp.triu(jnp.ones((s, s), dtype=bool), k=1)
        scores = jnp.where(causal_mask, jnp.asarray(NEG, scores.dtype), scores)
        weights = jax.nn.softmax(scores, axis=-1)
        heads = jnp.einsum('bhst,bhte->bhse', weights, v)
        concat = heads.transpose(0, 2, 1, 3).reshape(b, s, N_HEADS * D_HEAD)
        return concat @ wo.T

    def _L0_ffn_ref(x, w1, b1, w2, b2, centroids, w_route):
        import jax, jax.numpy as jnp
        import numpy as np
        D_MODEL = 128
        D_FF = 512
        N_EXPERTS = 8
        D_EXPERT = D_FF // N_EXPERTS
        TOP_K = 2
        LB_WEIGHT = 0.01
        B, S = (4, 256)

        def _top_k_softmax(logits, k):
            vals, _ = jax.lax.top_k(logits, k)
            thresh = vals[..., -1:]
            masked = jnp.where(logits >= thresh, logits, -jnp.inf)
            return jax.nn.softmax(masked, axis=-1)
        eps = 1e-12
        x_norm = x / jnp.maximum(jnp.linalg.norm(x, axis=-1, keepdims=True), eps)
        c_norm = centroids / jnp.maximum(jnp.linalg.norm(centroids, axis=-1, keepdims=True), eps)
        cos_scores = jnp.einsum('bsd,ed->bse', x_norm, c_norm)
        route_scores = jnp.einsum('bsd,ed->bse', x, w_route)
        logits = cos_scores + route_scores
        gates = _top_k_softmax(logits, TOP_K)
        h = jax.nn.gelu(jnp.einsum('bsd,edh->bseh', x, w1) + b1, approximate=False)
        expert_out = jnp.einsum('bseh,ehd->bsed', h, w2) + b2
        out = jnp.einsum('bse,bsed->bsd', gates, expert_out)
        return out

    def _L1_attn_ref(x, in_proj_w, out_proj_w, A_log, dt_bias, Dparam, ln_w, ln_b, ni_w, ni_b, no_w, no_b):
        import jax, jax.numpy as jnp
        import numpy as np
        D_MODEL = 128
        D_STATE = 64
        HEADDIM = 64
        EXPAND = 2
        D_INNER = D_MODEL * EXPAND
        NHEADS = D_INNER // HEADDIM
        D_IN_PROJ = 2 * D_INNER + 2 * D_STATE + NHEADS
        BATCH, SEQLEN = (4, 512)

        def layernorm(x, w, b, eps=1e-05):
            mu = jnp.mean(x, axis=-1, keepdims=True)
            var = jnp.mean(jnp.square(x - mu), axis=-1, keepdims=True)
            return (x - mu) * jax.lax.rsqrt(var + eps) * w + b

        def _selective_scan(x_multi, A, Bm, Cm, dt):
            Bb, L, H, P = x_multi.shape
            N = Bm.shape[-1]
            dA = jnp.minimum(jnp.exp(dt * A[None, None, :]), 0.99)

            def step(h, inp):
                x_t, B_t, C_t, dA_t = inp
                dBx = jnp.einsum('bhp,bn->bhpn', x_t, B_t)
                h = jnp.clip(dA_t[:, :, None, None] * h + dBx, -10.0, 10.0)
                y_t = jnp.einsum('bn,bhpn->bhp', C_t, h)
                return (h, y_t)
            h0 = jnp.zeros((Bb, H, P, N), dtype=x_multi.dtype)
            xs = (jnp.moveaxis(x_multi, 1, 0), jnp.moveaxis(Bm, 1, 0), jnp.moveaxis(Cm, 1, 0), jnp.moveaxis(dA, 1, 0))
            _, y = jax.lax.scan(step, h0, xs)
            return jnp.moveaxis(y, 0, 1)
        Bb, L, Dm = x.shape
        x_norm = layernorm(x, ni_w, ni_b)
        zxbcdt = jnp.einsum('bld,ed->ble', x_norm, in_proj_w)
        z = zxbcdt[..., :D_INNER]
        x_ssm = zxbcdt[..., D_INNER:2 * D_INNER]
        Bm = zxbcdt[..., 2 * D_INNER:2 * D_INNER + D_STATE]
        Cm = zxbcdt[..., 2 * D_INNER + D_STATE:2 * D_INNER + 2 * D_STATE]
        dt = zxbcdt[..., 2 * D_INNER + 2 * D_STATE:]
        dt = jnp.clip(jax.nn.softplus(dt + dt_bias[None, None, :]), 0.001, 0.1)
        A = -jnp.exp(A_log)
        x_multi = x_ssm.reshape(Bb, L, NHEADS, HEADDIM)
        y = _selective_scan(x_multi, A, Bm, Cm, dt)
        y = y + x_multi * Dparam[None, None, :, None]
        y = y.reshape(Bb, L, D_INNER)
        y = y * jax.nn.silu(z)
        y = layernorm(y, ln_w, ln_b)
        y = jnp.einsum('ble,de->bld', y, out_proj_w)
        y = jnp.clip(y, -10.0, 10.0)
        y = layernorm(y, no_w, no_b)
        return y

    def _L1_ffn_ref(x, Wqkv, q_scale, k_scale, Wo, ln_g, ln_b, W1, b1, W2, b2):
        import jax, jax.numpy as jnp
        import numpy as np
        DIM = 128
        DEPTH = 6
        HEADS = 16
        DIM_HEAD = 64
        WINDOW = 32
        INNER = HEADS * DIM_HEAD
        DIM_INNER = int(DIM * 4 * 2 / 3)
        QK_SCALE = 8.0

        def shift_tokens(t):
            a, s = jnp.split(t, 2, -1)
            s = jnp.pad(s, ((0, 0), (1, 0), (0, 0)))[:, :-1]
            return jnp.concatenate([a, s], -1)

        def l2norm(t):
            return t / jnp.maximum(jnp.linalg.norm(t, axis=-1, keepdims=True), 1e-12)

        def rotate_half(x):
            x1, x2 = jnp.split(x, 2, -1)
            return jnp.concatenate([-x2, x1], -1)

        def rotary_tables(n):
            half = jnp.arange(0, DIM_HEAD, 2, dtype=jnp.float32)
            inv_freq = 1.0 / 10000.0 ** (half / DIM_HEAD)
            t = jnp.arange(n, dtype=jnp.float32)
            freqs = t[:, None] * inv_freq[None, :]
            freqs = jnp.concatenate([freqs, freqs], -1)
            base_scale = (half + 0.4 * DIM_HEAD) / (1.4 * DIM_HEAD)
            power = (t - n // 2) / (WINDOW // 2)
            scale = base_scale[None, :] ** power[:, None]
            scale = jnp.concatenate([scale, scale], -1)
            return (freqs, scale)

        def local_attention(q, k, v):
            b, h, n, d = q.shape
            w = WINDOW
            nw = n // w
            bq = q.reshape(b, h, nw, w, d)
            bk = k.reshape(b, h, nw, w, d)
            bv = v.reshape(b, h, nw, w, d)

            def look(t):
                p = jnp.pad(t, ((0, 0), (0, 0), (1, 0), (0, 0), (0, 0)))
                return jnp.concatenate([p[:, :, :nw], p[:, :, 1:]], axis=3)
            bk2, bv2 = (look(bk), look(bv))
            seq = jnp.arange(n).reshape(nw, w)
            seq_p = jnp.pad(seq, ((1, 0), (0, 0)), constant_values=-1)
            jt = jnp.concatenate([seq_p[:nw], seq_p[1:]], axis=1)
            it = seq[:, :, None]
            jb = jt[:, None, :]
            mask = (it < jb) | (it > jb + w) | (jb == -1)
            sim = jnp.einsum('bhwie,bhwje->bhwij', bq, bk2) * QK_SCALE
            sim = jnp.where(mask, -jnp.finfo(sim.dtype).max, sim)
            attn = jax.nn.softmax(sim, -1)
            out = jnp.einsum('bhwij,bhwje->bhwie', attn, bv2)
            return out.reshape(b, h, n, d)

        def attn_layer(x, Wqkv, qs, ksc, Wo):
            b, n, _ = x.shape
            qkv = x @ Wqkv
            q, k, v = jnp.split(qkv, 3, -1)
            sh = lambda t: t.reshape(b, n, HEADS, DIM_HEAD).transpose(0, 2, 1, 3)
            q, k, v = (sh(q), sh(k), sh(v))
            q = l2norm(q) * qs
            k = l2norm(k) * ksc
            freqs, scale = rotary_tables(n)
            cos, sin = (jnp.cos(freqs), jnp.sin(freqs))
            q = q * cos * scale + rotate_half(q) * sin * scale
            inv = 1.0 / scale
            k = k * cos * inv + rotate_half(k) * sin * inv
            out = local_attention(q, k, v)
            out = out.transpose(0, 2, 1, 3).reshape(b, n, INNER)
            return out @ Wo

        def ffn_layer(x, g, bln, W1, b1, W2, b2):
            mu = x.mean(-1, keepdims=True)
            var = ((x - mu) ** 2).mean(-1, keepdims=True)
            xn = (x - mu) / jnp.sqrt(var + 1e-05) * g + bln
            hg = xn @ W1 + b1
            a, gate = jnp.split(hg, 2, -1)
            return a * jax.nn.gelu(gate, approximate=False) @ W2 + b2
        for i in range(DEPTH):
            x = attn_layer(shift_tokens(x), Wqkv[i], q_scale[i], k_scale[i], Wo[i]) + x
            x = ffn_layer(shift_tokens(x), ln_g[i], ln_b[i], W1[i], b1[i], W2[i], b2[i]) + x
        return x
    x = L0_attn_x
    xn = _layernorm(x, axis=-1)
    x = x + _L0_attn_ref(xn, L0_attn_wq, L0_attn_wk, L0_attn_wv, L0_attn_wo) + _L0_ffn_ref(xn, L0_ffn_w1, L0_ffn_b1, L0_ffn_w2, L0_ffn_b2, L0_ffn_centroids, L0_ffn_w_route)
    xn = _layernorm(x, axis=-1)
    x = x + _L1_attn_ref(xn, L1_attn_in_proj_w, L1_attn_out_proj_w, L1_attn_A_log, L1_attn_dt_bias, L1_attn_Dparam, L1_attn_ln_w, L1_attn_ln_b, L1_attn_ni_w, L1_attn_ni_b, L1_attn_no_w, L1_attn_no_b) + _L1_ffn_ref(xn, L1_ffn_Wqkv, L1_ffn_q_scale, L1_ffn_k_scale, L1_ffn_Wo, L1_ffn_ln_g, L1_ffn_ln_b, L1_ffn_W1, L1_ffn_b1, L1_ffn_W2, L1_ffn_b2)
    return x

_drawn_inputs = setup_inputs


def setup_inputs(seed=0):
    import zlib

    import numpy as np

    out = dict(_drawn_inputs(seed))
    spreads = {'L0_ffn_b1': (0.0, 0.1),
     'L0_ffn_b2': (0.0, 0.1),
     'L1_attn_Dparam': (1.0, 0.6),
     'L1_attn_ln_w': (1.0, 0.6),
     'L1_attn_ln_b': (0.0, 0.8),
     'L1_attn_ni_w': (1.0, 0.2),
     'L1_attn_ni_b': (0.0, 0.42),
     'L1_attn_no_w': (1.0, 0.6),
     'L1_attn_no_b': (0.0, 0.777),
     'L1_ffn_q_scale': (1.0, 0.6),
     'L1_ffn_k_scale': (1.0, 0.6),
     'L1_ffn_ln_g': (1.0, 0.6),
     'L1_ffn_ln_b': (0.0, 0.8),
     'L1_ffn_b1': (0.0, 0.8),
     'L1_ffn_b2': (0.0, 0.1)}
    factors = {'L0_attn_wq': 8.0, 'L0_attn_wk': 8.0, 'L1_ffn_W1': 4.269, 'L1_ffn_W2': 4.184}
    for name, (base, spread) in spreads.items():
        noise = np.random.default_rng([zlib.crc32(name.encode()), seed]).standard_normal(out[name].shape)
        drawn = base * np.exp(spread * noise) if base else spread * noise
        out[name] = jnp.asarray(drawn.astype(out[name].dtype))
    for name, factor in factors.items():
        out[name] = (out[name] * factor).astype(out[name].dtype)
    return out
```

```python
from contextlib import ExitStack

import numpy as np

import concourse.bass as bass
from concourse import mybir

F32 = mybir.dt.float32
BF16 = mybir.dt.bfloat16
I32 = mybir.dt.int32
ALU = mybir.AluOpType
ACT = mybir.ActivationFunctionType
AX = mybir.AxisListType

P = 128
D = 128
NB = 16
S = 256
T = S // P
H = 16
DH = 64
INNER = H * DH
HALF = 8
NE = 8
DE = 64
EH = NE * DE
DEPTH = 6
WINDOW = 32
FI = int(D * 4 * 2 / 3)
FC = [(0, 128), (128, 128), (256, FI - 256)]
SH = 4
DI = SH * 64
NS = 64
EPS = 1e-5
LN_CAP = float(np.log(0.99))
GUARD = 95.0
STEPS = 16
MASKED = -1e30

CAUSAL = [(0, 128), (0, 256)]
LOCAL = [(0, 128), (96, 160)]


def program(nc, a, out):
    ctx = ExitStack()
    with ctx:
        def sb(name, shape, dt=F32):
            return ctx.enter_context(nc.sbuf_tensor(name, shape, dt))

        def sem(name):
            return ctx.enter_context(nc.semaphore(name))

        bank = {n: ctx.enter_context(nc.psum_tensor(n, [P, 512], F32))
                for n in ("pj0", "pj1", "tp0", "tp1", "sc0", "sc1", "ov0", "ov1")}
        pj = [bank["pj0"], bank["pj1"]]
        tp = [bank["tp0"], bank["tp1"]]
        sc = [bank["sc0"], bank["sc1"]]
        ov = [bank["ov0"], bank["ov1"]]

        x = sb("x", [P, NB * T, D])
        y = sb("y", [P, NB * T, D])
        ident = sb("ident", [P, P])
        ident_bf = sb("ident_bf", [P, P], BF16)
        causal_bf = sb("causal_bf", [P, 384], BF16)
        local_bf = sb("local_bf", [P, 288], BF16)
        triu = sb("triu", [P, P])
        later = sb("later", [P, P])
        ones = sb("ones", [P, P])
        rot = sb("rot", [P, 4, T, DH])
        w_big = sb("w_big", [P, 3 * INNER])
        w_o = sb("w_o", [P, 8, D])
        w_moe1 = sb("w_moe1", [P, EH])
        w_moe2 = sb("w_moe2", [P, 4, D])
        b_moe1 = sb("b_moe1", [1, EH])
        b_moe2 = sb("b_moe2", [NE, D])
        route = sb("route", [P, 2 * NE])
        cent = sb("cent", [NE, D])
        w_in = sb("w_in", [P, 2 * DI + 2 * NS + SH])
        w_out = sb("w_out", [P, 2, D])
        ni = sb("ni", [P, 2])
        lnw = sb("lnw", [P, 2, 2])
        now = sb("now", [P, 2, D])
        hp = sb("hp", [P, 3, SH])
        neg_a = sb("neg_a", [P, SH])
        qk_scale = sb("qk_scale", [P, DEPTH, 2, DH])
        ln_gb = sb("ln_gb", [P, DEPTH, 2])
        w_f1 = sb("w_f1", [P, 2 * FI])
        w_f2 = sb("w_f2", [P, 3, D])
        b_f1 = sb("b_f1", [P, DEPTH, 6])
        b_f2 = sb("b_f2", [1, DEPTH, D])
        b_f2_now = sb("b_f2_now", [1, D])
        tabs = sb("tabs", [P, 4, T, DH])
        cur = sb("cur", [P, T, D])
        mid = sb("mid", [P, T, D])
        xn = sb("xn", [P, T, D])
        xn2 = sb("xn2", [P, T, D])
        xt = sb("xt", [P, S])
        xt2 = sb("xt2", [P, S])
        qt = sb("qt", [P, H // 2, S])
        kt = sb("kt", [P, H // 2, S])
        v = sb("v", [P, T, INNER])
        sq = sb("sq", [P, 2, 512])
        rq = sb("rq", [P, 8, 512])
        rb = sb("rb", [P, 2, 512])
        ss = sb("ss", [P, 2 * T * 2, HALF])
        prob = sb("prob", [P, 2, 512])
        pt = sb("pt", [P, 2, 384])
        nm = sb("nm", [P, H, T])
        rs = sb("rs", [P, T, H])
        rinv = sb("rinv", [P, T, H])
        o = sb("o", [P, T, INNER])
        ot = sb("ot", [P, 8, S])
        hid = sb("hid", [P, 3, S])
        gel = sb("gel", [P, 2, S])
        st = sb("st", [P, T, 6])
        mv = sb("mv", [P, T, 2])
        sm = sb("sm", [P, T, 8])
        lg = sb("lg", [P, T, 8 * 8])
        gate_t = sb("gate_t", [NE, S])
        o2 = o[:, :, :].rearrange("p t n -> p (t n)")
        v2 = v[:, :, :].rearrange("p t n -> p (t n)")
        qt2 = qt[:, :, :].rearrange("p t n -> p (t n)")
        kt2 = kt[:, :, :].rearrange("p t n -> p (t n)")
        rq2 = rq[:, :, :].rearrange("p t n -> p (t n)")
        c_sz = o2[:, 0:512].rearrange("p (t n) -> p t n", t=T)
        c_x = o2[:, 512:1024].rearrange("p (t n) -> p t n", t=T)
        c_y = o2[:, 1024:1536].rearrange("p (t n) -> p t n", t=T)
        c_yn = o2[:, 1536:2048].rearrange("p (t n) -> p t n", t=T)
        c_sq = v2[:, 0:1024].rearrange("p (t h n) -> p t h n", t=T, h=SH)
        c_bcd = v2[:, 1024:1024 + T * 132].rearrange("p (t n) -> p t n", t=T)
        c_bt = v2[0:NS, 1536:1792]
        c_ct = v2[0:NS, 1792:2048]
        c_dec = qt2[:, 0:1536].rearrange("p (h n) -> p h n", h=SH)
        c_gm = kt2[:, 0:1536].rearrange("p (h n) -> p h n", h=SH)
        c_lb = rq2[:, 0:1024].rearrange("p (g n) -> p g n", g=8)
        c_arg = rq2[:, 1024:2048].rearrange("p (g n) -> p g n", g=8)
        c_g = rq2[:, 2048:2432]
        c_yt = rq2[:, 2560:3072].rearrange("p (c n) -> p c n", c=2)
        dts = sb("dts", [P, 10, 8])
        dec_all = sb("dec_all", [P, 8])
        gmx = sb("gmx", [P, T, 12])
        flag = sb("flag", [P, 2])
        flag1 = sb("flag1", [1, 2])
        eps_c = sb("eps_c", [P, 4])
        bias_col = sb("bias_col", [P, 8])
        xsh = sb("xsh", [P, S])
        carrier = sb("carrier", [P, 2])
        e_bc = sb("e_bc", [P, STEPS, 2 * NS])
        e_dec = sb("e_dec", [P, STEPS, 2])
        e_x = sb("e_x", [P, 2, STEPS])
        e_y = sb("e_y", [P, 2, STEPS])
        e_h = sb("e_h", [P, 2, NS])
        e_t = sb("e_t", [P, NS])
        d_bcd = nc.dram_tensor("scratch_bcd", (S, 132), F32).ap()
        d_dec = nc.dram_tensor("scratch_dec", (S, SH), F32).ap()
        d_x = nc.dram_tensor("scratch_x", (S, DI), F32).ap()
        d_y = nc.dram_tensor("scratch_y", (S, DI), F32).ap()

        first_in, consts_in, w2_in, xrest_in = sem("first_in"), sem("consts_in"), sem("w2_in"), sem("xrest_in")
        layer_in, out_done = sem("layer_in"), sem("out_done")
        tabs_done = sem("tabs_done")
        prep, prep_t, prep_ok = sem("prep"), sem("prep_t"), sem("prep_ok")
        slow = sem("slow")
        x_final = sem("x_final")

        def signals(prefix, names):
            return {n: sem(prefix + n) for n in names.split()}

        core = "scores max_done exp_done pt_tr pt_done pv_done o_done o_tr ot_done wo_done dve_link act_link state_done "
        A = signals("a_", core + "mean_done xnorm_done xn_done tr_x xt_done qkt_done qk_done tr_v v_done route_ps "
                    "sumsq_in sumsq gate_in gate_exp lg_done gate_tr gatet_done moe_h moe_gelu moe_gated moe_tr moet_done")
        C = signals("c_", "mean0 rstd0 mean1 rstd1 mean2 rstd2 mean3 rstd3 xn_done tr_x xt_done zx bcd bct zx_out bcd_out "
                    "bct_out sq_out dt_in dt_exp soft lb_done cums lrow arg_done dec1 dec_done g_ps gm_done guard_ps "
                    "gmx_done flag_tr flag_out scan_ok y_ps y_out yn_done yn_tr yt_done o_ps x_done dve_link act_link")
        B = signals("b_", core + "cur_in tr_x xt_done proj sq_done ssq_done ssum_done r_done rot_b rot_sum rot_done "
                    "qkt_ready qkt_done v_done mid_done mid_tr midt_done back_tr mean rstd xn2_done xn2_tr xt2_done "
                    "hid_ps hid_gelu hid_done f_done gb_act")
        prep_a, slow_dma, prob_clear = sem("prep_a"), sem("slow_dma"), sem("prob_clear")

        block = ctx.enter_context(nc.Block())

        def chain(eng, s, it, per):
            n = [0]

            def link(ins):
                n[0] += 1
                ins.then_inc(s, 1)
                eng.wait_ge(s, it * per + n[0])
                return ins
            link.n, link.sem, link.it = n, s, it
            link.per = per
            return link

        def hold(dve, s, n):
            dve.wait_ge(s, n)
            dve.tensor_copy(carrier[:, 0:1], eps_c[:, 0:1])

        def tile_cols(span):
            return [(0, span[0][1]), (span[0][1], span[0][1] + span[1][1])]

        def pe_attention(eng, G, it, span, mask):
            cols = tile_cols(span)
            width = cols[1][1]
            local = span is LOCAL

            def scores(h):
                b = DH * (h % 2)
                eng.wait_ge(G["exp_done"], it * H + max(h - 1, 0))
                eng.matmul(sc[h % 2][:, 0:width], ident_bf[:, :], mask[:, :], start=True, stop=False)
                for t in range(T):
                    k0, kn = span[t]
                    m = eng.matmul(sc[h % 2][:, cols[t][0]:cols[t][1]], qt[b:b + DH, h // 2, P * t:P * t + P],
                                   kt[b:b + DH, h // 2, k0:k0 + kn], start=False, stop=(t == T - 1))
                m.then_inc(G["scores"], 1)

            def turn(h):
                eng.wait_ge(G["exp_done"], it * H + h + 1)
                eng.wait_ge(G["pt_done"], it * H + max(h - 1, 0))
                q = prob[:, h % 2, :]
                eng.transpose(tp[h % 2][:, 0:128], q[:, 0:128], ident[:, :])
                m = eng.transpose(tp[h % 2][:, 128:256], q[:, 384:512], ident[:, :])
                if local:
                    m = eng.transpose(tp[h % 2][:, 256:256 + WINDOW], q[0:WINDOW, 256:384], ident[0:WINDOW, 0:WINDOW])
                else:
                    m = eng.transpose(tp[h % 2][:, 256:384], q[:, 256:384], ident[:, :])
                m.then_inc(G["pt_tr"], 1)

            def weigh(h):
                eng.wait_ge(G["pt_done"], it * H + h + 1)
                if h % HALF == 0:
                    eng.wait_ge(G["o_done"], it * 2 + h // HALF)
                q = pt[:, h % 2, :]
                c = DH * (h % HALF)
                vv = [v[:, t, h * DH:h * DH + DH] for t in range(T)]
                eng.matmul(ov[0][:, c:c + DH], q[:, 0:128], vv[0], start=True, stop=True)
                eng.matmul(ov[1][:, c:c + DH], q[:, 128:256], vv[1], start=True, stop=False)
                eng.matmul(ov[1][:, c:c + DH], q[:, 256:384], vv[0], start=False, stop=True).then_inc(G["pv_done"], 1)

            scores(0)
            scores(1)
            for h in range(H):
                turn(h)
                if h + 2 < H:
                    scores(h + 2)
                weigh(h)
            for g in range(4):
                t, hf = g // 2, g % 2
                if g == 0:
                    eng.wait_ge(G["o_done"], it * 2 + 2)
                eng.wait_ge(G["pt_done"], it * H + H)
                if g >= 2:
                    eng.wait_ge(G["ot_done"], it * 4 + g - 1)
                for j in range(4):
                    m = eng.transpose(tp[g % 2][:, 128 * j:128 * j + 128],
                                      o[:, t, 512 * hf + 128 * j:512 * hf + 128 * j + 128], ident[:, :])
                m.then_inc(G["o_tr"], 1)
            eng.wait_ge(G["ot_done"], it * 4 + 4)
            for t in range(T):
                for c in range(8):
                    m = eng.matmul(pj[0][:, D * t:D * t + D], ot[:, c, P * t:P * t + P], w_o[:, c, :],
                                   start=(c == 0), stop=(c == 7 and local))
                if local:
                    m.then_inc(G["wo_done"], 1)
                else:
                    for c in range(4):
                        eng.matmul(pj[0][:, D * t:D * t + D], hid_moe(c, t), w_moe2[:, c, :], start=False, stop=False)
                    eng.matmul(pj[0][:, D * t:D * t + D], gate_t[:, P * t:P * t + P], b_moe2[:, :],
                               start=False, stop=True).then_inc(G["wo_done"], 1)

        def hid_moe(c, t):
            return rq[:, 4 + c, P * t:P * t + P]

        def dve_attention(eng, G, it, span):
            cols = tile_cols(span)
            local = span is LOCAL

            def top(h):
                eng.wait_ge(G["scores"], it * H + h + 1)
                for t in range(T):
                    m = eng.tensor_reduce(nm[:, h, t:t + 1], sc[h % 2][:, cols[t][0]:cols[t][1]], AX.X, ALU.max,
                                          negate=True)
                m.then_inc(G["max_done"], 1)

            def copy(h):
                eng.wait_ge(G["pt_tr"], it * H + h + 1)
                eng.wait_ge(G["pv_done"], it * H + max(h - 1, 0))
                n = 256 + (WINDOW if local else P)
                eng.tensor_copy(pt[:, h % 2, 0:n], tp[h % 2][:, 0:n]).then_inc(G["pt_done"], 1)

            def norm(hf):
                eng.wait_ge(G["pv_done"], it * H + HALF * (hf + 1))
                link(eng.reciprocal(rinv[:, :, HALF * hf:HALF * hf + HALF], rs[:, :, HALF * hf:HALF * hf + HALF]))
                for t in range(T):
                    m = eng.tensor_tensor(
                        o[:, t, 512 * hf:512 * hf + 512].rearrange("p (h e) -> p h e", h=HALF),
                        ov[t][:, :].rearrange("p (h e) -> p h e", h=HALF),
                        rinv[:, t, HALF * hf:HALF * hf + HALF].unsqueeze(2).broadcast_to((P, HALF, DH)), ALU.mult)
                m.then_inc(G["o_done"], 1)

            link = dve_attention.link
            top(0)
            top(1)
            for h in range(H):
                copy(h)
                if h + 2 < H:
                    top(h + 2)
                if h == HALF:
                    norm(0)
            norm(1)
            for g in (1, 3):
                eng.wait_ge(G["o_tr"], it * 4 + g + 1)
                if g == 3:
                    eng.wait_ge(G["ot_done"], it * 4 + 3)
                else:
                    eng.wait_ge(G["ot_done"], it * 4 + 1)
                t, hf = g // 2, g % 2
                eng.tensor_copy(ot[:, 4 * hf:4 * hf + 4, P * t:P * t + P],
                                tp[g % 2][:, :].rearrange("p (c n) -> p c n", c=4)).then_inc(G["ot_done"], 1)

        def act_attention(act, G, it, span):
            cols = tile_cols(span)
            for h in range(H):
                act.wait_ge(G["max_done"], it * H + h + 1)
                act.wait_ge(G["pt_tr"], it * H + max(h - 1, 0))
                for t in range(T):
                    n = span[t][1]
                    at = [0, 512 - n][t]
                    m = act.activation(prob[:, h % 2, at:at + n], sc[h % 2][:, cols[t][0]:cols[t][1]], ACT.Exp,
                                       bias=nm[:, h, t:t + 1], accum_out=rs[:, t, h:h + 1])
                m.then_inc(G["exp_done"], 1)
            for g in (0, 2):
                act.wait_ge(G["o_tr"], it * 4 + g + 1)
                if g == 2:
                    act.wait_ge(G["ot_done"], it * 4 + 2)
                t, hf = g // 2, g % 2
                act.activation(ot[:, 4 * hf:4 * hf + 4, P * t:P * t + P],
                               tp[g % 2][:, :].rearrange("p (c n) -> p c n", c=4), ACT.Copy).then_inc(G["ot_done"], 1)

        def stats(eng, link, src, t):
            for n, c in enumerate(src):
                m = eng.bn_stats(st[:, t, :], c)
            m.then_inc(link.sem, 1)
            link.n[0] += 1
            hold(eng, link.sem, link.it * link.per + link.n[0])
            return eng.bn_aggr(mv[:, t, :], st[:, t, :])

        def rstd(act, link, t):
            link(act.activation(sm[:, t, 1:2], mv[:, t, 1:2], ACT.Ln, bias=eps_c[:, 0:1]))
            return act.activation(sm[:, t, 0:1], sm[:, t, 1:2], ACT.Exp, scale=-0.5)

        def W2_LOADS():
            yield triu[:, :], a["triu"]
            yield later[:, :], a["later"]
            yield rot[:, :, :, :], a["rot"].rearrange("k (t p) e -> p k t e", p=P)
            yield w_in[:, :], a["w_in"]
            yield w_out[:, :, :], a["w_out"].rearrange("(c p) n -> p c n", p=P)
            yield ni[:, 0:1], a["ni_w"].rearrange("(p a) -> p a", a=1)
            yield ni[:, 1:2], a["ni_b"].rearrange("(p a) -> p a", a=1)
            yield lnw[:, :, 0], a["ln_w"].rearrange("(c p) -> p c", p=P)
            yield lnw[:, :, 1], a["ln_b"].rearrange("(c p) -> p c", p=P)
            yield now[:, 0, :], a["no_w"].rearrange("(a n) -> a n", a=1).broadcast_to((P, D))
            yield now[:, 1, :], a["no_b"].rearrange("(a n) -> a n", a=1).broadcast_to((P, D))
            for n, k in enumerate(("A_log", "dt_bias", "Dparam")):
                yield hp[:, n, :], a[k].rearrange("(a n) -> a n", a=1).broadcast_to((P, SH))
            for n, k in enumerate(("q_scale", "k_scale")):
                yield qk_scale[:, :, n, :], a[k].rearrange("(a l) e -> a l e", a=1).broadcast_to((P, DEPTH, DH))
            yield ln_gb[:, :, 0], a["f_g"]
            yield ln_gb[:, :, 1], a["f_b"]
            for c in range(6):
                f0, fn = FC[c % 3]
                f0 += FI * (c // 3)
                yield b_f1[0:fn, :, c], a["b_f1"][f0:f0 + fn, :]
            yield b_f2[:, :, :], a["b_f2"].rearrange("(a l) n -> a l n", a=1)
        N_W2 = len(list(W2_LOADS()))
        N_CONST, N_FIRST, N_LAYER = 6, 5, 6

        N_TABS = T * 2 + T * 2 * 2 + 1

        def exact_scan(pool):
            with nc.allow_non_contiguous_dma("rare path"):
                def moved(ins):
                    ins.then_inc(slow_dma, 16)
                    pool.wait_ge(slow_dma, 16)
                    pool.dma_reset(range(slow_dma.num, slow_dma.num + 1))
                    pool.sem_clear(slow_dma)

                def did(ins):
                    ins.then_inc(slow, 1)
                    pool.wait_ge(slow, 1)
                    pool.sem_clear(slow)

                for t in range(T):
                    moved(pool.dma_start(d_bcd[P * t:P * t + P, :], c_bcd[:, t, :]))
                    moved(pool.dma_start(d_dec[P * t:P * t + P, :], dec_all[:, SH * t:SH * t + SH]))
                    moved(pool.dma_start(d_x[P * t:P * t + P, :], c_x[:, t, :]))
                did(pool.memset(e_h[:, :, :], 0.0))
                with pool.Fori(0, S // STEPS) as n:
                    at = n * STEPS
                    for i in range(STEPS):
                        moved(pool.dma_start(e_bc[:, i:i + 1, :],
                                             d_bcd[bass.ds(at + i, 1), 0:2 * NS].unsqueeze(0).broadcast_to((P, 1, 2 * NS))))
                    for hh in range(2):
                        for e in range(2):
                            h = 2 * hh + e
                            moved(pool.dma_start(e_dec[64 * e:64 * e + 64, :, hh],
                                                 d_dec[bass.ds(at, STEPS), h].unsqueeze(0).broadcast_to((64, STEPS))))
                        moved(pool.dma_start(e_x[:, hh, :], d_x[bass.ds(at, STEPS), P * hh:P * hh + P].rearrange("s p -> p s")))
                    for i in range(STEPS):
                        for hh in range(2):
                            hs = e_h[:, hh, :]
                            did(pool.tensor_scalar(e_t[:, :], e_bc[:, i, 0:NS], e_x[:, hh, i:i + 1], None, ALU.mult))
                            did(pool.tensor_scalar(hs, hs, e_dec[:, i, hh:hh + 1], None, ALU.mult))
                            did(pool.tensor_tensor(hs, hs, e_t[:, :], ALU.add))
                            did(pool.tensor_scalar(hs, hs, -10.0, 10.0, ALU.max, ALU.min))
                            did(pool.tensor_tensor(e_t[:, :], hs, e_bc[:, i, NS:2 * NS], ALU.mult))
                            w = NS // 2
                            while w >= 1:
                                dst = e_t[:, 0:w] if w > 1 else e_y[:, hh, i:i + 1]
                                did(pool.tensor_tensor(dst, e_t[:, 0:w], e_t[:, w:2 * w], ALU.add))
                                w //= 2
                    for hh in range(2):
                        moved(pool.dma_start(d_y[bass.ds(at, STEPS), P * hh:P * hh + P].rearrange("s p -> p s"), e_y[:, hh, :]))
                for t in range(T):
                    moved(pool.dma_start(c_y[:, t, :], d_y[P * t:P * t + P, :]))
        def pe_layer(pe, it):
            pe.wait_ge(B["cur_in"], it + 1)
            for t in range(T):
                m = pe.transpose(tp[0][:, P * t:P * t + P], cur[:, t, :], ident[:, :])
            m.then_inc(B["tr_x"], 1)
            pe.wait_ge(B["xt_done"], it + 1)
            for g in range(12):
                t, c = (g // 4, g % 4) if g < 8 else ((g - 8) // 2, 4 + (g - 8) % 2)
                if g >= 2:
                    done, n = (B["rot_b"], it * 8 + g - 1) if g <= 9 else (B["v_done"], it * 4 + g - 9)
                    pe.wait_ge(done, n)
                m = pe.matmul(pj[g % 2][:, :], xsh[:, P * t:P * t + P], w_big[:, 512 * c:512 * c + 512], start=True, stop=True)
                m.then_inc(B["proj"], 1)
            for g in range(8):
                t, c = g // 4, g % 4
                pe.wait_ge(B["rot_done"], it * 8 + g + 1)
                if g >= 2:
                    pe.wait_ge(B["qkt_done"], it * 8 + g - 1)
                for j in range(4):
                    m = pe.transpose(tp[g % 2][:, P * j:P * j + P], rq[:, g, P * j:P * j + P], ident[:, :])
                m.then_inc(B["qkt_ready"], 1)
            pe.wait_ge(B["qkt_done"], it * 8 + 8)
            pe.wait_ge(B["v_done"], it * 4 + 4)
            pe_attention(pe, B, it, LOCAL, local_bf)
            pe.wait_ge(B["mid_done"], it * T + T)
            for t in range(T):
                m = pe.transpose(tp[0][:, P * t:P * t + P], mid[:, t, :], ident[:, :])
            m.then_inc(B["mid_tr"], 1)
            pe.wait_ge(B["midt_done"], it + 1)
            for t in range(T):
                m = pe.transpose(tp[1][:, P * t:P * t + P], xsh[:, P * t:P * t + P], ident[:, :])
            m.then_inc(B["back_tr"], 1)
            pe.wait_ge(B["xn2_done"], it * T + T)
            for t in range(T):
                m = pe.transpose(tp[0][:, P * t:P * t + P], xn2[:, t, :], ident[:, :])
            m.then_inc(B["xn2_tr"], 1)
            pe.wait_ge(B["xt2_done"], it + 1)
            for c, (f0, fn) in enumerate(FC):
                if c >= 2:
                    pe.wait_ge(B["hid_done"], it * 3 + c - 1)
                for n in range(2):
                    m = pe.matmul(sc[c % 2][0:fn, S * n:S * n + S], w_f1[:, FI * n + f0:FI * n + f0 + fn], xt2[:, :],
                                  start=True, stop=True)
                m.then_inc(B["hid_ps"], 1)
            pe.wait_ge(B["hid_done"], it * 3 + 3)
            for t in range(T):
                for c, (f0, fn) in enumerate(FC):
                    pe.matmul(pj[1][:, D * t:D * t + D], hid[0:fn, c, P * t:P * t + P], w_f2[0:fn, c, :],
                              start=(c == 0), stop=False)
                m = pe.matmul(pj[1][:, D * t:D * t + D], ones[0:1, :], b_f2_now[:, :], start=False, stop=True)
            m.then_inc(B["f_done"], 1)

        LN_A, LN_B, LN_C_TOTAL = 19, 4, 37

        def shifted(dve, dst, src, done):
            dve.tensor_copy(dst[0:64, :], src[0:64, 0:S])
            dve.tensor_copy(dst[64:128, 1:S], src[64:128, 0:S - 1]).then_inc(done, 1)

        def dve_layer(dve, it, b, n_link):
            link = chain(dve, B["dve_link"], it, n_link)
            dve_attention.link = link
            dve.wait_ge(B["tr_x"], it + 1)
            shifted(dve, xsh, tp[0], B["xt_done"])
            for g in range(8):
                t, c = g // 4, g % 4
                k = 2 * (c // 2)
                src = pj[g % 2][:, :].rearrange("p (h e) -> p h e", h=HALF)
                heads = (P, HALF, 32)
                dve.wait_ge(B["sq_done"], it * 8 + g + 1)
                dve.tensor_reduce(ss[:, g, :], sq[:, g % 2, :].rearrange("p (h e) -> p h e", h=HALF), AX.X, ALU.add
                                  ).then_inc(B["ssq_done"], 1)
                dve.tensor_tensor(rq[:, g, :].rearrange("p (h e) -> p h e", h=HALF), src,
                                  tabs[:, k, t, :].unsqueeze(1).broadcast_to((P, HALF, DH)), ALU.mult)
                dve.wait_ge(B["ssq_done"], it * 8 + g + 1)
                dve.tensor_scalar(ss[:, g, :], ss[:, g, :], 1e-24, None, ALU.max).then_inc(B["ssum_done"], 1)
                if g >= 2:
                    dve.wait_ge(B["rot_sum"], it * 8 + g - 1)
                dst = rb[:, g % 2, :].rearrange("p (h e) -> p h e", h=HALF)
                dve.tensor_tensor(dst[:, :, 0:32], src[:, :, 32:64],
                                  tabs[:, k + 1, t, 0:32].unsqueeze(1).broadcast_to(heads), ALU.mult)
                dve.tensor_tensor(dst[:, :, 32:64], src[:, :, 0:32],
                                  tabs[:, k + 1, t, 32:64].unsqueeze(1).broadcast_to(heads), ALU.mult
                                  ).then_inc(B["rot_b"], 1)
                if g >= 1:
                    scale_heads(dve, it, g - 1)
            scale_heads(dve, it, 7)
            for g in (1, 3, 5, 7):
                dve.wait_ge(B["qkt_ready"], it * 8 + g + 1)
                dve.wait_ge(B["qkt_done"], it * 8 + g)
                turned(g, lambda o_, i_: dve.tensor_copy(o_, i_)).then_inc(B["qkt_done"], 1)
            dve_attention(dve, B, it, LOCAL)
            for t in range(T):
                dve.wait_ge(B["wo_done"], it * T + T)
                m = dve.tensor_tensor(mid[:, t, :], cur[:, t, :], pj[0][:, D * t:D * t + D], ALU.add)
                m.then_inc(B["mid_done"], 1)
            dve.wait_ge(B["mid_tr"], it + 1)
            shifted(dve, xsh, tp[0], B["midt_done"])
            dve.wait_ge(B["back_tr"], it + 1)
            for t in range(T):
                stats(dve, link, [tp[1][:, P * t:P * t + P]], t).then_inc(B["mean"], 1)
            for t in range(T):
                dve.wait_ge(B["rstd"], it * T + t + 1)
                dve.tensor_scalar(xn2[:, t, :], tp[1][:, P * t:P * t + P], mv[:, t, 0:1], sm[:, t, 0:1],
                                  ALU.subtract, ALU.mult).then_inc(B["xn2_done"], 1)
            dve.wait_ge(B["xn2_tr"], it + 1)
            dve.tensor_scalar(xt2[:, :], tp[0][:, 0:S], bias_col[:, 0:1], bias_col[:, 1:2],
                              ALU.mult, ALU.add).then_inc(B["xt2_done"], 1)
            for c, (f0, fn) in enumerate(FC):
                dve.wait_ge(B["hid_gelu"], it * 3 + c + 1)
                dve.scalar_tensor_tensor(hid[0:fn, c, :], sc[c % 2][0:fn, 0:S], bias_col[0:fn, 2 + c:3 + c],
                                         gel[0:fn, c % 2, :], ALU.add, ALU.mult).then_inc(B["hid_done"], 1)
            dve.wait_ge(B["f_done"], it + 1)
            dve.tensor_tensor(y[:, bass.ds(b * T, T), :], mid[:, :, :],
                              pj[1][:, 0:2 * D].rearrange("p (t n) -> p t n", t=T), ALU.add
                              ).then_inc(B["state_done"], 1)
            assert link.n[0] == n_link, link.n


        def scale_heads(dve, it, g):
            dve.wait_ge(B["rot_sum"], it * 8 + g + 1)
            dve.wait_ge(B["r_done"], it * 8 + g + 1)
            q = rq[:, g, :].rearrange("p (h e) -> p h e", h=HALF)
            dve.tensor_tensor(q, q, ss[:, g, :].unsqueeze(2).broadcast_to((P, HALF, DH)), ALU.mult).then_inc(B["rot_done"], 1)

        def turned(g, copy):
            t, c = g // 4, g % 4
            dst = (qt if c < 2 else kt)[:, 4 * (c % 2):4 * (c % 2) + 4, P * t:P * t + P]
            return copy(dst, tp[g % 2][:, :].rearrange("p (c n) -> p c n", c=4))

        def act_layer(act, it, n_link):
            link = chain(act, B["act_link"], it, n_link)
            act.preload_act_table_set("natural_log_exp_and_others")
            for g in range(8):
                act.wait_ge(B["proj"], it * 12 + g + 1)
                if g >= 2:
                    act.wait_ge(B["ssum_done"], it * 8 + g - 1)
                act.activation(sq[:, g % 2, :], pj[g % 2][:, :], ACT.Square).then_inc(B["sq_done"], 1)
                if g >= 1:
                    factor(act, link, it, g - 1)
            factor(act, link, it, 7)
            for g in range(4):
                act.wait_ge(B["proj"], it * 12 + 8 + g + 1)
                act.activation(v[:, g // 2, 512 * (g % 2):512 * (g % 2) + 512], pj[g % 2][:, :], ACT.Copy).then_inc(B["v_done"], 1)
            for g in (0, 2, 4, 6):
                act.wait_ge(B["qkt_ready"], it * 8 + g + 1)
                act.wait_ge(B["qkt_done"], it * 8 + g)
                turned(g, lambda o_, i_: act.activation(o_, i_, ACT.Copy)).then_inc(B["qkt_done"], 1)
            act_attention(act, B, it, LOCAL)
            for t in range(T):
                act.wait_ge(B["mean"], it * T + t + 1)
                rstd(act, link, t).then_inc(B["rstd"], 1)
            act.preload_act_table_set("gelu_and_others")
            for c, (f0, fn) in enumerate(FC):
                act.wait_ge(B["hid_ps"], it * 3 + c + 1)
                if c >= 2:
                    act.wait_ge(B["hid_done"], it * 3 + c - 1)
                act.activation(gel[0:fn, c % 2, :], sc[c % 2][0:fn, S:2 * S], ACT.Gelu, bias=bias_col[0:fn, 5 + c:6 + c]
                               ).then_inc(B["hid_gelu"], 1)
            assert link.n[0] == n_link, link.n

        def factor(act, link, it, g):
            act.wait_ge(B["ssum_done"], it * 8 + g + 1)
            link(act.activation(ss[:, g, :], ss[:, g, :], ACT.Ln, scale=2.0 ** 20))
            act.activation(ss[:, g, :], ss[:, g, :], ACT.Exp, scale=-0.5, bias=eps_c[:, 1:2]).then_inc(B["r_done"], 1)


        @block.sync
        def _(sp):
            xin = a["x"].rearrange("b (t p) d -> p (b t) d", p=P)
            for dst, src in ((x[:, 0:T, :], xin[:, 0:T, :]), (w_big[:, :], a["w_qkv0"]), (ident[:, :], a["ident"]),
                             (cent[:, :], a["cent"]), (route[:, NE:2 * NE], a["w_route"])):
                sp.dma_start(dst, src).then_inc(first_in, 16)
            for dst, src in ((o[:, 0, 0:672], a["masks"]),
                             (w_o[:, :, :], a["w_o0"].rearrange("(c p) n -> p c n", p=P)),
                             (w_moe1[:, :], a["w_moe1"]), (w_moe2[:, :, :], a["w_moe2"].rearrange("(c p) n -> p c n", p=P)),
                             (b_moe1[:, :], a["b_moe1"]), (b_moe2[:, :], a["b_moe2"])):
                sp.dma_start(dst, src).then_inc(consts_in, 16)
            sp.dma_start(x[:, T:NB * T, :], xin[:, T:NB * T, :]).then_inc(xrest_in, 16)
            with nc.allow_non_contiguous_dma("small per-partition columns"):
                for dst, src in W2_LOADS():
                    sp.dma_start(dst, src).then_inc(w2_in, 16)
            sp.wait_ge(A["wo_done"], NB * T)
            with sp.Fori(0, DEPTH) as l:
                sp.wait_ge(B["state_done"], l * NB)
                sp.dma_start(w_big[:, :], a["w_qkv"][bass.ds(l, 1), :, :].rearrange("a p n -> p (a n)")).then_inc(layer_in, 16)
                sp.dma_start(w_o[:, :, :], a["w_o"][bass.ds(l, 1), :, :].rearrange("a (c p) n -> p (a c) n", p=P)
                             ).then_inc(layer_in, 16)
                sp.dma_start(w_f1[:, :], a["w_f1"][bass.ds(l, 1), :, :].rearrange("a p n -> p (a n)")).then_inc(layer_in, 16)
                for c, (f0, fn) in enumerate(FC):
                    sp.dma_start(w_f2[0:fn, c, :], a["w_f2"][bass.ds(l, 1), f0:f0 + fn, :].rearrange("a p n -> p (a n)")
                                 ).then_inc(layer_in, 16)
            sp.wait_ge(x_final, NB)
            sp.dma_start(out.rearrange("b (t p) d -> p (b t) d", p=P), x[:, :, :]).then_inc(out_done, 16)
            sp.wait_ge(out_done, 16)

        @block.gpsimd
        def _(pool):
            pool.memset(ones[:, :], 1.0).then_inc(prep, 1)
            pool.memset(xsh[:, :], 0.0).then_inc(prep, 1)
            pool.memset(eps_c[:, 0:1], EPS).then_inc(prep, 1)
            pool.memset(eps_c[:, 1:2], float(10 * np.log(2.0))).then_inc(prep, 1)
            with pool.Fori(0, NB) as it:
                for t in range(T):
                    pool.wait_ge(A["lg_done"], it * T + t + 1)
                    pool.wait_ge(A["moe_gelu"], it * T + t + 1)
                    pool.tensor_tensor(rq[:, t, :].rearrange("p (e n) -> p e n", e=NE),
                                       rq[:, t, :].rearrange("p (e n) -> p e n", e=NE),
                                       lg[:, t, 56:64].unsqueeze(2).broadcast_to((P, NE, DE)), ALU.mult
                                       ).then_inc(A["moe_gated"], 1)
            with pool.Fori(0, NB) as it:
                pool.wait_ge(C["flag_out"], it + 1)
                pool.wait_ge(C["y_out"], it * T + T)
                pool.wait_ge(C["dec1"], it + 1)
                pool.tensor_tensor(carrier[:, 1:2], eps_c[:, 0:1], eps_c[:, 0:1], ALU.add)
                bound = pool.value_load(flag1[0:1, 0:1].bitcast(I32))
                with pool.If(bound > int(np.float32(GUARD).view(np.int32))):
                    exact_scan(pool)
                pool.memset(flag1[0:1, 1:2], 0.0).then_inc(C["scan_ok"], 1)
            pool.wait_ge(A["state_done"], NB)
            pool.memset(prob[:, :, 256:352], 0.0).then_inc(prob_clear, 1)
            pool.memset(pt[:, :, 256 + WINDOW:384], 0.0).then_inc(prob_clear, 1)
            with pool.Fori(0, DEPTH) as l:
                pool.wait_ge(w2_in, 16 * N_W2)
                pool.wait_ge(B["state_done"], l * NB)
                for k in range(4):
                    sc_ = qk_scale[:, bass.ds(l, 1), k // 2, :]
                    for t in range(T):
                        if k % 2 == 0:
                            pool.tensor_tensor(tabs[:, k, t, :].unsqueeze(1), rot[:, k, t, :].unsqueeze(1), sc_, ALU.mult
                                               ).then_inc(tabs_done, 1)
                        else:
                            for lo, hi in ((0, 32), (32, 0)):
                                pool.tensor_tensor(tabs[:, k, t, lo:lo + 32].unsqueeze(1),
                                                   rot[:, k, t, lo:lo + 32].unsqueeze(1), sc_[:, :, hi:hi + 32], ALU.mult
                                                   ).then_inc(tabs_done, 1)
                pool.tensor_copy(b_f2_now[:, :].unsqueeze(1), b_f2[:, bass.ds(l, 1), :]).then_inc(tabs_done, 1)
                with pool.Fori(0, NB) as b:
                    it = l * NB + b
                    pool.wait_ge(B["state_done"], it)
                    pool.tensor_copy(cur[:, :, :], y[:, bass.ds(b * T, T), :]).then_inc(B["cur_in"], 1)
                    for g in range(8):
                        pool.wait_ge(B["rot_b"], it * 8 + g + 1)
                        pool.tensor_tensor(rq[:, g, :], rq[:, g, :], rb[:, g % 2, :], ALU.add).then_inc(B["rot_sum"], 1)
            pool.wait_ge(B["state_done"], DEPTH * NB)
            for b in range(NB):
                pool.tensor_tensor(x[:, b * T:b * T + T, :], x[:, b * T:b * T + T, :], y[:, b * T:b * T + T, :],
                                   ALU.add).then_inc(x_final, 1)

        @block.tensor
        def _(pe):
            pe.wait_ge(prep_ok, 2)
            pe.wait_ge(first_in, 16 * N_FIRST)
            pe.transpose(tp[0][:, 0:NE], cent[:, :], ident[0:NE, 0:NE]).then_inc(prep_t, 1)
            pe.wait_ge(prep_ok, 3)
            pe.wait_ge(prep, 4)
            pe.wait_ge(consts_in, 16 * N_CONST)
            with pe.Fori(0, NB) as it:
                pe.wait_ge(A["xn_done"], it * T + T)
                pe.wait_ge(A["ot_done"], it * 4)
                for t in range(T):
                    m = pe.transpose(tp[0][:, P * t:P * t + P], xn[:, t, :], ident[:, :])
                m.then_inc(A["tr_x"], 1)
                pe.wait_ge(A["xt_done"], it + 1)
                pe.wait_ge(A["state_done"], it)
                for p in range(H // 2):
                    if p >= 2:
                        pe.wait_ge(A["qk_done"], it * 8 + p - 1)
                    for n in range(2):
                        m = pe.matmul(pj[p % 2][:, S * n:S * n + S], w_big[:, INNER * n + P * p:INNER * n + P * p + P],
                                      xt[:, :], start=True, stop=True)
                    m.then_inc(A["qkt_done"], 1)
                for g in range(4):
                    t, c = g // 2, g % 2
                    pe.wait_ge(A["qk_done"], it * 8 + 7 + min(g, 1))
                    if g >= 2:
                        pe.wait_ge(A["v_done"], it * 4 + g - 1)
                    pe.matmul(pj[g % 2][:, :], xt[:, P * t:P * t + P],
                              w_big[:, 2 * INNER + 512 * c:2 * INNER + 512 * c + 512], start=True, stop=True
                              ).then_inc(A["tr_v"], 1)
                for t in range(T):
                    m = pe.matmul(tp[1][:, 16 * t:16 * t + 16], xt[:, P * t:P * t + P], route[:, :], start=True, stop=True)
                m.then_inc(A["route_ps"], 1)
                for t in range(T):
                    pe.wait_ge(A["v_done"], it * 4 + 3 + t)
                    pe.matmul(pj[t][:, :], xt[:, P * t:P * t + P], w_moe1[:, :], start=True, stop=False)
                    pe.matmul(pj[t][:, :], ones[0:1, :], b_moe1[:, :], start=False, stop=True).then_inc(A["moe_h"], 1)
                for t in range(T):
                    pe.wait_ge(A["moe_gated"], it * T + t + 1)
                    if t == 0:
                        pe.wait_ge(A["lg_done"], it * T + T)
                    for c in range(4):
                        m = pe.transpose(tp[t][:, P * c:P * c + P], rq[:, t, P * c:P * c + P], ident[:, :])
                    m.then_inc(A["moe_tr"], 1)
                pe.wait_ge(A["moet_done"], it * T + T)
                for t in range(T):
                    m = pe.transpose(tp[0][0:NE, P * t:P * t + P], lg[:, t, 56:64], ident[:, :])
                m.then_inc(A["gate_tr"], 1)
                pe.wait_ge(A["gatet_done"], it + 1)
                pe_attention(pe, A, it, CAUSAL, causal_bf)
            pe.wait_ge(w2_in, 16 * N_W2)
            pe.wait_ge(A["state_done"], NB)
            with pe.Fori(0, NB) as it:
                pe.wait_ge(C["xn_done"], it * T + T)
                pe.wait_ge(C["yt_done"], it * T)
                for t in range(T):
                    m = pe.transpose(tp[0][:, P * t:P * t + P], xn[:, t, :], ident[:, :])
                m.then_inc(C["tr_x"], 1)
                pe.wait_ge(C["xt_done"], it + 1)
                pe.wait_ge(C["x_done"], it)
                for t in range(T):
                    pe.matmul(pj[t][:, :], xt[:, P * t:P * t + P], w_in[:, 0:512], start=True, stop=True).then_inc(C["zx"], 1)
                    pe.matmul(tp[t][:, 256:256 + 132], xt[:, P * t:P * t + P], w_in[:, 512:644],
                              start=True, stop=True).then_inc(C["bcd"], 1)
                for n in range(2):
                    m = pe.matmul(sc[0][0:NS, S * n:S * n + S], w_in[:, 512 + NS * n:512 + NS * n + NS], xt[:, :],
                                  start=True, stop=True)
                m.then_inc(C["bct"], 1)
                pe.wait_ge(C["soft"], it + 1)
                pe.wait_ge(C["bcd_out"], it * T + T)
                pe.matmul(tp[0][:, 0:8], triu[:, :], dts[:, 8, :], start=True, stop=True)
                pe.matmul(tp[0][:, 8:16], ones[:, :], dts[:, 8, :], start=True, stop=True).then_inc(C["cums"], 1)
                pe.wait_ge(C["lb_done"], it + 1)
                for g in range(8):
                    m = pe.matmul(ov[g // 4][:, P * (g % 4):P * (g % 4) + P], c_lb[:, g, :], triu[:, :], start=True, stop=True)
                    if g % 4 == 3:
                        m.then_inc(C["lrow"], 1)
                pe.wait_ge(C["bct_out"], it + 1)
                for n, (s_, t_) in enumerate(((0, 0), (0, 1), (1, 1))):
                    m = pe.matmul(sc[1][:, P * n:P * n + P], c_bt[:, P * s_:P * s_ + P], c_ct[:, P * t_:P * t_ + P],
                                  start=True, stop=True)
                m.then_inc(C["g_ps"], 1)
                pe.wait_ge(C["dec_done"], it * 3 + 3)
                pe.wait_ge(C["sq_out"], it * T + T)
                pe.wait_ge(C["zx_out"], it * T + T)
                for h in range(SH):
                    pe.matmul(pj[0][:, P * h:P * h + P], c_dec[:, h, 0:P], c_sq[:, 0, h, :], start=True, stop=True)
                    pe.matmul(pj[1][:, P * h:P * h + P], c_dec[:, h, P:2 * P], c_sq[:, 0, h, :], start=True, stop=False)
                    m = pe.matmul(pj[1][:, P * h:P * h + P], c_dec[:, h, 2 * P:3 * P], c_sq[:, 1, h, :], start=False, stop=True)
                m.then_inc(C["guard_ps"], 1)
                pe.wait_ge(C["gm_done"], it + 1)
                for h in range(SH):
                    c = slice(64 * h, 64 * h + 64)
                    pe.matmul(ov[0][:, c], c_gm[:, h, 0:P], c_x[:, 0, c], start=True, stop=True)
                    pe.matmul(ov[1][:, c], c_gm[:, h, P:2 * P], c_x[:, 0, c], start=True, stop=False)
                    m = pe.matmul(ov[1][:, c], c_gm[:, h, 2 * P:3 * P], c_x[:, 1, c], start=False, stop=True)
                m.then_inc(C["y_ps"], 1)
                pe.wait_ge(C["gmx_done"], it + 1)
                pe.wait_ge(C["soft"], it + 1)
                pe.wait_ge(C["arg_done"], it * 8 + 8)
                pe.transpose(tp[0][0:1, 0:P], flag[:, 0:1], ident[:, :]).then_inc(C["flag_tr"], 1)
                pe.wait_ge(C["yn_done"], it * T + T)
                pe.wait_ge(C["flag_out"], it + 1)
                for t in range(T):
                    for c in range(2):
                        m = pe.transpose(tp[t][:, P * c:P * c + P], c_yn[:, t, P * c:P * c + P], ident[:, :])
                    m.then_inc(C["yn_tr"], 1)
                pe.wait_ge(C["yt_done"], it * T + T)
                for t in range(T):
                    for c in range(2):
                        m = pe.matmul(pj[0][:, D * t:D * t + D], c_yt[:, c, P * t:P * t + P], w_out[:, c, :],
                                      start=(c == 0), stop=(c == 1))
                m.then_inc(C["o_ps"], 1)
            pe.wait_ge(C["x_done"], NB)
            pe.wait_ge(prob_clear, 2)
            with pe.Fori(0, DEPTH) as l:
                with pe.Fori(0, NB) as b:
                    pe.wait_ge(tabs_done, (l + 1) * N_TABS)
                    pe.wait_ge(layer_in, (l + 1) * 16 * N_LAYER)
                    pe_layer(pe, l * NB + b)

        @block.vector
        def _(dve):
            dve.wait_ge(first_in, 16 * N_FIRST)
            dve.wait_ge(consts_in, 16 * N_CONST)
            dve.tensor_copy(ident_bf[:, :], ident[:, :])
            dve.tensor_copy(causal_bf[:, :], o[:, 0, 0:384])
            dve.tensor_copy(local_bf[:, :], o[:, 0, 384:672]).then_inc(prep_ok, 1)
            dve.wait_ge(prep_t, 1)
            dve.tensor_copy(route[:, 0:NE], tp[0][:, 0:NE]).then_inc(prep_ok, 1)
            dve.wait_ge(first_in, 16 * N_FIRST)
            dve.wait_ge(xrest_in, 16)
            with dve.Fori(0, NB) as it:
                link = chain(dve, A["dve_link"], it, LN_A)
                dve_attention.link = link
                for t in range(T):
                    xs = x[:, bass.ds(it * T + t, 1), :]
                    stats(dve, link, [xs.rearrange("p a n -> p (a n)")], t).then_inc(A["mean_done"], 1)
                for t in range(T):
                    xs = x[:, bass.ds(it * T + t, 1), :].rearrange("p a n -> p (a n)")
                    dve.wait_ge(A["xnorm_done"], it * T + t + 1)
                    dve.tensor_scalar(xn[:, t, :], xs, mv[:, t, 0:1], sm[:, t, 0:1], ALU.subtract, ALU.mult
                                      ).then_inc(A["xn_done"], 1)
                dve.wait_ge(A["tr_x"], it + 1)
                dve.tensor_copy(xt[:, :], tp[0][:, 0:S]).then_inc(A["xt_done"], 1)
                dve.wait_ge(A["xn_done"], it * T + T)
                for t in range(T):
                    dve.tensor_tensor_reduce(sq[:, t, 0:D], xn[:, t, :], xn[:, t, :], 1.0, 0.0, ALU.mult, ALU.add,
                                             sm[:, t, 5:6])
                link(dve.tensor_copy(lg[:, 0, 43:44], eps_c[:, 0:1]))
                dve.tensor_scalar(sm[:, :, 2:3], sm[:, :, 5:6], 1e-24, None, ALU.max).then_inc(A["sumsq_in"], 1)
                for p in range(1, H // 2, 2):
                    dve.wait_ge(A["qkt_done"], it * 8 + p + 1)
                    dve.wait_ge(A["qk_done"], it * 8 + p)
                    dve.tensor_scalar(qt[:, p, :], pj[1][:, 0:S], 0.125, None, ALU.mult)
                    dve.tensor_copy(kt[:, p, :], pj[1][:, S:2 * S]).then_inc(A["qk_done"], 1)
                for g in (1, 3):
                    dve.wait_ge(A["tr_v"], it * 4 + g + 1)
                    dve.wait_ge(A["v_done"], it * 4 + g)
                    dve.tensor_copy(v[:, g // 2, 512:1024], pj[1][:, :]).then_inc(A["v_done"], 1)
                dve.wait_ge(A["route_ps"], it + 1)
                dve.wait_ge(A["sumsq"], it * T + T)
                for t in range(T):
                    q = lg[:, t, :]
                    link(dve.tensor_scalar(q[:, 32:40], tp[1][:, 16 * t:16 * t + 8], sm[:, t, 4:5], None, ALU.mult))
                    link(dve.tensor_tensor(q[:, 0:8], q[:, 32:40], tp[1][:, 16 * t + 8:16 * t + 16], ALU.add))
                    hold(dve, A["dve_link"], it * LN_A + link.n[0])
                    link(dve.max(q[:, 8:16], q[:, 0:8]))
                    link(dve.tensor_scalar(q[:, 40:41], q[:, 8:9], -1.0, None, ALU.mult))
                    dve.tensor_scalar(q[:, 24:32], q[:, 0:8], q[:, 9:10], None, ALU.is_ge).then_inc(A["gate_in"], 1)
                for t in range(T):
                    q = lg[:, t, :]
                    dve.wait_ge(A["gate_exp"], it * T + t + 1)
                    link(dve.tensor_tensor(q[:, 24:32], q[:, 24:32], q[:, 16:24], ALU.mult))
                    link(dve.tensor_reduce(q[:, 41:42], q[:, 24:32], AX.X, ALU.add))
                    link(dve.reciprocal(q[:, 42:43], q[:, 41:42]))
                    dve.tensor_scalar(q[:, 56:64], q[:, 24:32], q[:, 42:43], None, ALU.mult).then_inc(A["lg_done"], 1)
                for t in range(T):
                    dve.wait_ge(A["moe_tr"], it * T + t + 1)
                    dve.tensor_copy(rq[:, 4:8, P * t:P * t + P], tp[t][:, :].rearrange("p (c n) -> p c n", c=4)
                                    ).then_inc(A["moet_done"], 1)
                dve.wait_ge(A["gate_tr"], it + 1)
                dve.tensor_copy(gate_t[:, :], tp[0][0:NE, 0:S]).then_inc(A["gatet_done"], 1)
                dve_attention(dve, A, it, CAUSAL)
                dve.wait_ge(A["wo_done"], it * T + T)
                xs = x[:, bass.ds(it * T, T), :]
                dve.tensor_tensor(xs, xs, pj[0][:, 0:T * D].rearrange("p (t n) -> p t n", t=T), ALU.add
                                  ).then_inc(A["state_done"], 1)
                assert link.n[0] == LN_A, link.n
            dve.wait_ge(w2_in, 16 * N_W2)
            with dve.Fori(0, NB) as it:
                link = chain(dve, C["dve_link"], it, LN_C_TOTAL)
                for t in range(T):
                    xs = x[:, bass.ds(it * T + t, 1), :].rearrange("p a n -> p (a n)")
                    stats(dve, link, [xs], t).then_inc(C["mean0"], 1)
                for t in range(T):
                    xs = x[:, bass.ds(it * T + t, 1), :].rearrange("p a n -> p (a n)")
                    ys = y[:, bass.ds(it * T + t, 1), :].rearrange("p a n -> p (a n)")
                    dve.wait_ge(C["rstd0"], it * T + t + 1)
                    link(dve.tensor_scalar(ys, xs, mv[:, t, 0:1], sm[:, t, 0:1], ALU.subtract, ALU.mult))
                    hold(dve, C["dve_link"], it * LN_C_TOTAL + link.n[0])
                    stats(dve, link, [ys], t).then_inc(C["mean1"], 1)
                for t in range(T):
                    ys = y[:, bass.ds(it * T + t, 1), :].rearrange("p a n -> p (a n)")
                    dve.wait_ge(C["rstd1"], it * T + t + 1)
                    dve.tensor_scalar(xn[:, t, :], ys, mv[:, t, 0:1], sm[:, t, 0:1], ALU.subtract, ALU.mult
                                      ).then_inc(C["xn_done"], 1)
                for t in range(T):
                    dve.wait_ge(C["bcd"], it * T + t + 1)
                    dve.tensor_copy(c_bcd[:, t, :], tp[t][:, 256:388]).then_inc(C["bcd_out"], 1)
                dve.wait_ge(C["bcd_out"], it * T + T)
                dve.tensor_tensor(dts[:, 0, :].rearrange("p (t h) -> p t h", t=T), c_bcd[:, :, 128:132],
                                  hp[:, 1, :].unsqueeze(1).broadcast_to((P, T, SH)), ALU.add).then_inc(C["dt_in"], 1)
                dve.wait_ge(C["dt_exp"], it + 1)
                d = [dts[:, i, :] for i in range(10)]
                link(dve.tensor_scalar(d[1], d[1], 1.0, None, ALU.min))
                link(dve.tensor_scalar(d[2], d[1], 2.0, None, ALU.add))
                link(dve.reciprocal(d[3], d[2]))
                link(dve.tensor_tensor(d[2], d[1], d[3], ALU.mult))
                link(dve.tensor_tensor(d[3], d[2], d[2], ALU.mult))
                link(dve.tensor_scalar(d[4], d[3], 2.0 / 7, 2.0 / 5, ALU.mult, ALU.add))
                link(dve.tensor_tensor(d[4], d[4], d[3], ALU.mult))
                link(dve.tensor_scalar(d[4], d[4], 2.0 / 3, None, ALU.add))
                link(dve.tensor_tensor(d[4], d[4], d[3], ALU.mult))
                link(dve.tensor_scalar(d[4], d[4], 2.0, None, ALU.add))
                link(dve.tensor_tensor(d[4], d[4], d[2], ALU.mult))
                link(dve.tensor_scalar(d[4], d[4], 0.001, 0.1, ALU.max, ALU.min))
                link(dve.tensor_tensor(d[5].rearrange("p (t h) -> p t h", t=T), d[4].rearrange("p (t h) -> p t h", t=T),
                                       neg_a[:, :].unsqueeze(1).broadcast_to((P, T, SH)), ALU.mult))
                dve.tensor_scalar(d[8], d[5], LN_CAP, None, ALU.min).then_inc(C["soft"], 1)
                dve.wait_ge(C["soft"], it + 1)
                dve.tensor_copy(c_lb[:, :, :], d[8].unsqueeze(2).broadcast_to((P, 8, P))).then_inc(C["lb_done"], 1)
                dve.wait_ge(C["cums"], it + 1)
                dve.tensor_copy(d[6], tp[0][:, 0:8])
                link(dve.tensor_copy(d[7], tp[0][:, 8:16]))
                link(dve.tensor_tensor(d[9], d[7], d[6], ALU.subtract))
                for g in range(8):
                    dve.wait_ge(C["lrow"], it * 2 + g // 4 + 1)
                    dve.scalar_tensor_tensor(c_arg[:, g, :], ov[g // 4][:, P * (g % 4):P * (g % 4) + P], dts[:, 6, g:g + 1],
                                             later[:, :], ALU.subtract, ALU.add).then_inc(C["arg_done"], 1)
                dve.wait_ge(C["g_ps"], it + 1)
                link(dve.tensor_copy(c_g, sc[1][:, 0:384]))
                dve.wait_ge(C["dec_done"], it * 3 + 3)
                dve.tensor_tensor(c_gm[:, :, :], c_dec[:, :, :], c_g.unsqueeze(1).broadcast_to((P, SH, 384)), ALU.mult
                                  ).then_inc(C["gm_done"], 1)
                dve.wait_ge(C["guard_ps"], it + 1)
                for t in range(T):
                    link(dve.tensor_reduce(gmx[:, t, 0:8], pj[t][:, :].rearrange("p (h n) -> p h n", n=64), AX.X, ALU.max))
                link(dve.tensor_tensor(gmx[:, :, 8:12], gmx[:, :, 0:8:2], gmx[:, :, 1:8:2], ALU.mult))
                dve.tensor_reduce(flag[:, 0:1], gmx[:, :, 8:12], AX.XY, ALU.max).then_inc(C["gmx_done"], 1)
                dve.wait_ge(C["flag_tr"], it + 1)
                dve.wait_ge(C["scan_ok"], it)
                dve.tensor_reduce(flag1[0:1, 0:1], tp[0][0:1, 0:P], AX.X, ALU.max).then_inc(C["flag_out"], 1)
                dve.wait_ge(C["y_ps"], it + 1)
                for t in range(T):
                    dve.tensor_copy(c_y[:, t, :], ov[t][:, 0:DI]).then_inc(C["y_out"], 1)
                dve.wait_ge(C["zx_out"], it * T + T)
                for t in range(T):
                    dve.tensor_tensor(c_yn[:, t, :].rearrange("p (h n) -> p h n", h=SH),
                                      c_x[:, t, :].rearrange("p (h n) -> p h n", h=SH),
                                      hp[:, 2, :].unsqueeze(2).broadcast_to((P, SH, 64)), ALU.mult)
                dve.wait_ge(C["scan_ok"], it + 1)
                link(dve.tensor_copy(flag[:, 1:2], eps_c[:, 0:1]))
                link(dve.tensor_tensor(c_yn[:, :, :], c_yn[:, :, :], c_y[:, :, :], ALU.add))
                link(dve.tensor_tensor(c_yn[:, :, :], c_yn[:, :, :], c_sz[:, :, :], ALU.mult))
                for t in range(T):
                    stats(dve, link, [c_yn[:, t, :]], t).then_inc(C["mean2"], 1)
                for t in range(T):
                    dve.wait_ge(C["rstd2"], it * T + t + 1)
                    dve.tensor_scalar(c_yn[:, t, :], c_yn[:, t, :], mv[:, t, 0:1], sm[:, t, 0:1], ALU.subtract, ALU.mult
                                      ).then_inc(C["yn_done"], 1)
                dve.wait_ge(C["o_ps"], it + 1)
                link(dve.tensor_scalar(xn[:, :, :].rearrange("p t n -> p (t n)"), pj[0][:, 0:2 * D], 10.0, -10.0, ALU.min, ALU.max))
                for t in range(T):
                    stats(dve, link, [xn[:, t, :]], t).then_inc(C["mean3"], 1)
                for t in range(T):
                    dve.wait_ge(C["rstd3"], it * T + t + 1)
                    link(dve.tensor_scalar(xn[:, t, :], xn[:, t, :], mv[:, t, 0:1], sm[:, t, 0:1], ALU.subtract, ALU.mult))
                link(dve.tensor_tensor(xn[:, :, :], xn[:, :, :], now[:, 0, :].unsqueeze(1).broadcast_to((P, T, D)), ALU.mult))
                link(dve.tensor_tensor(xn[:, :, :], xn[:, :, :], now[:, 1, :].unsqueeze(1).broadcast_to((P, T, D)), ALU.add))
                xs = x[:, bass.ds(it * T, T), :]
                dve.tensor_tensor(xs, xs, xn[:, :, :], ALU.add).then_inc(C["x_done"], 1)
                assert link.n[0] == LN_C_TOTAL, link.n
            with dve.Fori(0, DEPTH) as l:
                with dve.Fori(0, NB) as b:
                    dve.wait_ge(tabs_done, (l + 1) * N_TABS)
                    dve.wait_ge(B["gb_act"], l + 1)
                    dve_layer(dve, l * NB + b, b, LN_B)

        @block.scalar
        def _(act):
            LA_A, LA_B, LA_C = 4, 10, 8
            act.wait_ge(first_in, 16 * N_FIRST)
            act.wait_ge(prep, 4)
            act.activation(lg[0:NE, 0, 0:1], cent[:, 0:1], ACT.Copy).then_inc(prep_a, 1)
            act.wait_ge(prep_a, 1)
            act.activation(rb[0:NE, 0, 0:D], cent[:, :], ACT.Square, accum_out=eps_c[0:NE, 2:3]).then_inc(prep_a, 1)
            act.wait_ge(prep_a, 2)
            act.activation(eps_c[0:NE, 3:4], eps_c[0:NE, 2:3], ACT.Ln, scale=2.0 ** 20).then_inc(prep_a, 1)
            act.wait_ge(prep_a, 3)
            act.activation(eps_c[0:NE, 2:3], eps_c[0:NE, 3:4], ACT.Exp, scale=-0.5, bias=eps_c[0:NE, 1:2]).then_inc(prep_a, 1)
            act.wait_ge(prep_a, 4)
            act.activation(cent[:, :], cent[:, :], ACT.Copy, scale=eps_c[0:NE, 2:3]).then_inc(prep_ok, 1)
            with act.Fori(0, NB) as it:
                link = chain(act, A["act_link"], it, LA_A)
                act.preload_act_table_set("natural_log_exp_and_others")
                for t in range(T):
                    act.wait_ge(A["mean_done"], it * T + t + 1)
                    rstd(act, link, t).then_inc(A["xnorm_done"], 1)
                for t in range(T):
                    act.wait_ge(A["sumsq_in"], it + 1)
                    link(act.activation(sm[:, t, 3:4], sm[:, t, 2:3], ACT.Ln, scale=2.0 ** 20))
                    act.activation(sm[:, t, 4:5], sm[:, t, 3:4], ACT.Exp, scale=-0.5, bias=eps_c[:, 1:2]).then_inc(A["sumsq"], 1)
                for p in range(0, H // 2, 2):
                    act.wait_ge(A["qkt_done"], it * 8 + p + 1)
                    act.wait_ge(A["qk_done"], it * 8 + p)
                    act.activation(qt[:, p, :], pj[0][:, 0:S], ACT.Copy, scale=0.125)
                    act.activation(kt[:, p, :], pj[0][:, S:2 * S], ACT.Copy).then_inc(A["qk_done"], 1)
                for g in (0, 2):
                    act.wait_ge(A["tr_v"], it * 4 + g + 1)
                    act.wait_ge(A["v_done"], it * 4 + g)
                    act.activation(v[:, g // 2, 0:512], pj[0][:, :], ACT.Copy).then_inc(A["v_done"], 1)
                for t in range(T):
                    q = lg[:, t, :]
                    act.wait_ge(A["gate_in"], it * T + t + 1)
                    act.activation(q[:, 16:24], q[:, 0:8], ACT.Exp, bias=q[:, 40:41]).then_inc(A["gate_exp"], 1)
                for t in range(T):
                    act.wait_ge(A["moe_h"], it * T + t + 1)
                    act.activation(rq[:, t, :], pj[t][:, :], ACT.Gelu).then_inc(A["moe_gelu"], 1)
                act.preload_act_table_set("natural_log_exp_and_others")
                act_attention(act, A, it, CAUSAL)
                assert link.n[0] == LA_A, link.n
            act.wait_ge(w2_in, 16 * N_W2)
            act.activation(neg_a[:, :], hp[:, 0, :], ACT.Exp).then_inc(prep_a, 1)
            act.wait_ge(prep_a, 5)
            act.activation(neg_a[:, :], neg_a[:, :], ACT.Copy, scale=-1.0).then_inc(prep_ok, 1)
            with act.Fori(0, NB) as it:
                link = chain(act, C["act_link"], it, LA_C)
                act.preload_act_table_set("natural_log_exp_and_others")
                for mean, done in ((C["mean0"], C["rstd0"]), (C["mean1"], C["rstd1"])):
                    for t in range(T):
                        act.wait_ge(mean, it * T + t + 1)
                        rstd(act, link, t).then_inc(done, 1)
                act.wait_ge(C["tr_x"], it + 1)
                act.activation(xt[:, :], tp[0][:, 0:S], ACT.Identity, scale=ni[:, 0:1], bias=ni[:, 1:2]).then_inc(C["xt_done"], 1)
                for t in range(T):
                    act.wait_ge(C["zx"], it * T + t + 1)
                    act.activation(c_x[:, t, :], pj[t][:, 256:512], ACT.Copy)
                    act.activation(c_sq[:, t, :, 0:64], pj[t][:, 256:512].rearrange("p (h n) -> p h n", h=SH), ACT.Square)
                    act.activation(c_sz[:, t, :], pj[t][:, 0:256], ACT.Silu).then_inc(C["zx_out"], 1)
                act.preload_act_table_set("natural_log_exp_and_others")
                act.wait_ge(C["bct"], it + 1)
                act.activation(c_bt, sc[0][0:NS, 0:S], ACT.Copy)
                act.activation(c_ct, sc[0][0:NS, S:2 * S], ACT.Copy).then_inc(C["bct_out"], 1)
                act.wait_ge(C["dt_in"], it + 1)
                act.activation(dts[:, 1, :], dts[:, 0, :], ACT.Exp).then_inc(C["dt_exp"], 1)
                for t in range(T):
                    act.wait_ge(C["bcd_out"], it * T + T)
                    act.activation(c_sq[:, t, :, 64:128], c_bcd[:, t, 0:NS].unsqueeze(1).broadcast_to((P, SH, NS)), ACT.Square
                                   ).then_inc(C["sq_out"], 1)
                act.wait_ge(C["soft"], it + 1)
                act.activation(dec_all[:, :], dts[:, 8, :], ACT.Exp).then_inc(C["dec1"], 1)
                act.wait_ge(C["arg_done"], it * 8 + 8)
                act.activation(c_dec[:, :, 0:P], c_arg[:, 0:4, :], ACT.Exp).then_inc(C["dec_done"], 1)
                act.activation(c_dec[:, :, 2 * P:3 * P], c_arg[:, 4:8, :], ACT.Exp).then_inc(C["dec_done"], 1)
                for h in range(SH):
                    m = act.activation(c_dec[:, h, P:2 * P], ov[1][:, P * h:P * h + P], ACT.Exp, bias=dts[:, 9, h:h + 1])
                m.then_inc(C["dec_done"], 1)
                for t in range(T):
                    act.wait_ge(C["mean2"], it * T + t + 1)
                    rstd(act, link, t).then_inc(C["rstd2"], 1)
                for t in range(T):
                    act.wait_ge(C["yn_tr"], it * T + t + 1)
                    for c in range(2):
                        m = act.activation(c_yt[:, c, P * t:P * t + P], tp[t][:, P * c:P * c + P], ACT.Identity,
                                           scale=lnw[:, c, 0:1], bias=lnw[:, c, 1:2])
                    m.then_inc(C["yt_done"], 1)
                for t in range(T):
                    act.wait_ge(C["mean3"], it * T + t + 1)
                    rstd(act, link, t).then_inc(C["rstd3"], 1)
                assert link.n[0] == LA_C, link.n
            with act.Fori(0, DEPTH) as l:
                act.wait_ge(B["state_done"], l * NB)
                act.activation(bias_col[:, 0:2].unsqueeze(1), ln_gb[:, bass.ds(l, 1), :], ACT.Copy)
                for c in range(6):
                    fn = FC[c % 3][1]
                    m = act.activation(bias_col[0:fn, 2 + c:3 + c].unsqueeze(1), b_f1[0:fn, bass.ds(l, 1), c:c + 1], ACT.Copy)
                m.then_inc(B["gb_act"], 1)
                act.wait_ge(B["gb_act"], l + 1)
                with act.Fori(0, NB) as b:
                    act_layer(act, l * NB + b, LA_B)

def host_constants():
    i = np.arange(S)
    causal = np.where(i[None, :] <= i[:, None], 0.0, MASKED)
    near = np.where((i[None, :] <= i[:, None]) & (i[None, :] >= i[:, None] - WINDOW), 0.0, MASKED)

    def pack(m, span):
        return np.concatenate([m[P * t:P * t + P, k0:k0 + kn] for t, (k0, kn) in enumerate(span)], 1)

    half = np.arange(0, DH, 2, dtype=np.float32)
    freqs = i[:, None].astype(np.float32) * (1.0 / 10000.0 ** (half / DH)).astype(np.float32)[None, :]
    freqs = np.concatenate([freqs, freqs], -1)
    power = (i.astype(np.float32) - S // 2) / (WINDOW // 2)
    scale = (((half + 0.4 * DH) / (1.4 * DH))[None, :] ** power[:, None]).astype(np.float32)
    scale = np.concatenate([scale, scale], -1)
    cos, sin = np.cos(freqs), np.sin(freqs)
    sin = np.concatenate([-sin[:, :DH // 2], sin[:, DH // 2:]], -1)
    rot = np.stack([8 * cos * scale, 8 * sin * scale, cos / scale, sin / scale]).astype(np.float32)
    r = np.arange(P)
    return {
        "ident": np.eye(P, dtype=np.float32),
        "masks": np.concatenate([pack(causal, CAUSAL), pack(near, LOCAL)], 1).astype(np.float32),
        "triu": (r[:, None] <= r[None, :]).astype(np.float32),
        "later": np.where(r[None, :] >= r[:, None], 0.0, MASKED).astype(np.float32),
        "rot": rot,
    }


def layouts(i):
    t = np.ascontiguousarray
    g = {k: np.asarray(v) for k, v in i.items()}
    return {
        "x": g["L0_attn_x"],
        "w_qkv0": t(np.concatenate([g[k].reshape(INNER, D).T for k in ("L0_attn_wq", "L0_attn_wk", "L0_attn_wv")], 1)),
        "w_o0": t(g["L0_attn_wo"].T),
        "cent": g["L0_ffn_centroids"],
        "w_route": t(g["L0_ffn_w_route"].T),
        "w_moe1": t(g["L0_ffn_w1"].transpose(1, 0, 2).reshape(D, EH)),
        "w_moe2": g["L0_ffn_w2"].reshape(EH, D),
        "b_moe1": g["L0_ffn_b1"].reshape(1, EH),
        "b_moe2": g["L0_ffn_b2"],
        "w_in": t(g["L1_attn_in_proj_w"].T),
        "w_out": t(g["L1_attn_out_proj_w"].T),
        "ni_w": g["L1_attn_ni_w"], "ni_b": g["L1_attn_ni_b"],
        "ln_w": g["L1_attn_ln_w"], "ln_b": g["L1_attn_ln_b"],
        "no_w": g["L1_attn_no_w"], "no_b": g["L1_attn_no_b"],
        "A_log": g["L1_attn_A_log"], "dt_bias": g["L1_attn_dt_bias"], "Dparam": g["L1_attn_Dparam"],
        "w_qkv": g["L1_ffn_Wqkv"], "w_o": g["L1_ffn_Wo"],
        "q_scale": g["L1_ffn_q_scale"], "k_scale": g["L1_ffn_k_scale"],
        "f_g": t(g["L1_ffn_ln_g"].T), "f_b": t(g["L1_ffn_ln_b"].T),
        "w_f1": g["L1_ffn_W1"], "w_f2": g["L1_ffn_W2"],
        "b_f1": t(g["L1_ffn_b1"].T), "b_f2": g["L1_ffn_b2"],
    }


def kernel(**inputs):
    import concourse.bacc as bacc
    from concourse.bass_utils import run_bass_kernel_spmd

    arrays = {**layouts(inputs), **host_constants()}
    nc = bacc.Bacc("TRN2", target_bir_lowering=False, num_devices=1)
    a = {n: nc.dram_tensor("in_" + n, v.shape, mybir.dt.from_np(v.dtype), kind="ExternalInput").ap()
         for n, v in arrays.items()}
    out = nc.dram_tensor("out_x", (NB, S, D), F32, kind="ExternalOutput").ap()
    program(nc, a, out)
    r = run_bass_kernel_spmd(nc, [{"in_" + n: v for n, v in arrays.items()}], core_ids=[0])
    return r.results[0]["out_x"]
```

```python
from contextlib import ExitStack

import numpy as np

import concourse.bass as bass
from concourse import mybir

F32 = mybir.dt.float32
BF16 = mybir.dt.bfloat16
I32 = mybir.dt.int32
ALU = mybir.AluOpType
ACT = mybir.ActivationFunctionType
AX = mybir.AxisListType

P = 128
D = 128
NB = 16
S = 256
T = S // P
H = 16
DH = 64
INNER = H * DH
HALF = 8
NE = 8
DE = 64
EH = NE * DE
DEPTH = 6
WINDOW = 32
FI = int(D * 4 * 2 / 3)
FC = [(0, 128), (128, 128), (256, FI - 256)]
SH = 4
DI = SH * 64
NS = 64
EPS = 1e-5
LN_CAP = float(np.log(0.99))
GUARD = 95.0
STEPS = 16
MASKED = -1e30

CAUSAL = [(0, 128), (0, 256)]
LOCAL = [(0, 128), (96, 160)]


def program(nc, a, out):
    ctx = ExitStack()
    with ctx:
        def sb(name, shape, dt=F32):
            return ctx.enter_context(nc.sbuf_tensor(name, shape, dt))

        def sem(name):
            return ctx.enter_context(nc.semaphore(name))

        bank = {n: ctx.enter_context(nc.psum_tensor(n, [P, 512], F32))
                for n in ("pj0", "pj1", "tp0", "tp1", "sc0", "sc1", "ov0", "ov1")}
        pj = [bank["pj0"], bank["pj1"]]
        tp = [bank["tp0"], bank["tp1"]]
        sc = [bank["sc0"], bank["sc1"]]
        ov = [bank["ov0"], bank["ov1"]]

        x = sb("x", [P, NB * T, D])
        y = sb("y", [P, NB * T, D])
        ident = sb("ident", [P, P])
        ident_bf = sb("ident_bf", [P, P], BF16)
        causal_bf = sb("causal_bf", [P, 384], BF16)
        local_bf = sb("local_bf", [P, 288], BF16)
        triu = sb("triu", [P, P])
        later = sb("later", [P, P])
        ones = sb("ones", [P, P])
        rot = sb("rot", [P, 4, T, DH])
        w_big = sb("w_big", [P, 3 * INNER])
        w_o = sb("w_o", [P, 8, D])
        w_moe1 = sb("w_moe1", [P, EH])
        w_moe2 = sb("w_moe2", [P, 4, D])
        b_moe1 = sb("b_moe1", [1, EH])
        b_moe2 = sb("b_moe2", [NE, D])
        route = sb("route", [P, 2 * NE])
        cent = sb("cent", [NE, D])
        w_in = sb("w_in", [P, 2 * DI + 2 * NS + SH])
        w_out = sb("w_out", [P, 2, D])
        ni = sb("ni", [P, 2])
        lnw = sb("lnw", [P, 2, 2])
        now = sb("now", [P, 2, D])
        hp = sb("hp", [P, 3, SH])
        neg_a = sb("neg_a", [P, SH])
        qk_scale = sb("qk_scale", [P, DEPTH, 2, DH])
        ln_gb = sb("ln_gb", [P, DEPTH, 2])
        w_f1 = sb("w_f1", [P, 2 * FI])
        w_f2 = sb("w_f2", [P, 3, D])
        b_f1 = sb("b_f1", [P, DEPTH, 6])
        b_f2 = sb("b_f2", [1, DEPTH, D])
        tabs = sb("tabs", [P, 4, T, DH])
        cur = sb("cur", [P, T, D])
        mid = sb("mid", [P, T, D])
        xn = sb("xn", [P, T, D])
        xn2 = sb("xn2", [P, T, D])
        xt = sb("xt", [P, S])
        xt2 = sb("xt2", [P, S])
        qt = sb("qt", [P, H // 2, S])
        kt = sb("kt", [P, H // 2, S])
        v = sb("v", [P, T, INNER])
        sq = sb("sq", [P, 2, 512])
        rq = sb("rq", [P, 8, 512])
        rb = sb("rb", [P, 2, 512])
        ss = sb("ss", [P, 2 * T * 2, HALF])
        prob = sb("prob", [P, 2, 512])
        pt = sb("pt", [P, 2, 384])
        nm = sb("nm", [P, H, T])
        rs = sb("rs", [P, T, H])
        rinv = sb("rinv", [P, T, H])
        o = sb("o", [P, T, INNER])
        ot = sb("ot", [P, 8, S])
        hid = sb("hid", [P, 3, S])
        hsb = sb("hsb", [P, 3, 2 * S])
        gel = sb("gel", [P, 3, S])
        st = sb("st", [P, T, 6])
        mv = sb("mv", [P, T, 2])
        sm = sb("sm", [P, T, 8])
        lg = sb("lg", [P, T, 8 * 8])
        gate_t = sb("gate_t", [NE, S])
        o2 = o[:, :, :].rearrange("p t n -> p (t n)")
        v2 = v[:, :, :].rearrange("p t n -> p (t n)")
        qt2 = qt[:, :, :].rearrange("p t n -> p (t n)")
        kt2 = kt[:, :, :].rearrange("p t n -> p (t n)")
        rq2 = rq[:, :, :].rearrange("p t n -> p (t n)")
        c_sz = o2[:, 0:512].rearrange("p (t n) -> p t n", t=T)
        c_x = o2[:, 512:1024].rearrange("p (t n) -> p t n", t=T)
        c_y = o2[:, 1024:1536].rearrange("p (t n) -> p t n", t=T)
        c_yn = o2[:, 1536:2048].rearrange("p (t n) -> p t n", t=T)
        c_sq = v2[:, 0:1024].rearrange("p (t h n) -> p t h n", t=T, h=SH)
        c_bcd = v2[:, 1024:1024 + T * 132].rearrange("p (t n) -> p t n", t=T)
        c_bt = v2[0:NS, 1536:1792]
        c_ct = v2[0:NS, 1792:2048]
        c_dec = qt2[:, 0:1536].rearrange("p (h n) -> p h n", h=SH)
        c_gm = kt2[:, 0:1536].rearrange("p (h n) -> p h n", h=SH)
        c_lb = rq2[:, 0:1024].rearrange("p (g n) -> p g n", g=8)
        c_arg = rq2[:, 1024:2048].rearrange("p (g n) -> p g n", g=8)
        c_g = rq2[:, 2048:2432]
        c_yt = rq2[:, 2560:3072].rearrange("p (c n) -> p c n", c=2)
        dts = sb("dts", [P, 10, 8])
        dec_all = sb("dec_all", [P, 8])
        gmx = sb("gmx", [P, T, 12])
        flag = sb("flag", [P, 2])
        flag1 = sb("flag1", [1, 2])
        eps_c = sb("eps_c", [P, 4])
        xsh = sb("xsh", [P, S])
        xsf = sb("xsf", [P, S])
        carrier = sb("carrier", [P, 2])
        e_bc = sb("e_bc", [P, STEPS, 2 * NS])
        e_dec = sb("e_dec", [P, STEPS, 2])
        e_x = sb("e_x", [P, 2, STEPS])
        e_y = sb("e_y", [P, 2, STEPS])
        e_h = sb("e_h", [P, 2, NS])
        e_t = sb("e_t", [P, NS])
        d_bcd = nc.dram_tensor("scratch_bcd", (S, 132), F32).ap()
        d_dec = nc.dram_tensor("scratch_dec", (S, SH), F32).ap()
        d_x = nc.dram_tensor("scratch_x", (S, DI), F32).ap()
        d_y = nc.dram_tensor("scratch_y", (S, DI), F32).ap()

        first_in, consts_in, w2_in, xrest_in = sem("first_in"), sem("consts_in"), sem("w2_in"), sem("xrest_in")
        qk_in, v_in, o_in, f_in = sem("qk_in"), sem("v_in"), sem("o_in"), sem("f_in")
        out_done = sem("out_done")
        tabs_done = sem("tabs_done")
        prep, prep_t, prep_ok = sem("prep"), sem("prep_t"), sem("prep_ok")
        slow = sem("slow")
        x_final = sem("x_final")

        def signals(prefix, names):
            return {n: sem(prefix + n) for n in names.split()}

        core = "scores max_done exp_done pt_tr pt_done pv_done o_done o_tr ot_done wo_done state_done "
        A = signals("a_", core + "mean_done xnorm_done xn_done tr_x xt_done xt_now qkt_done qk_done qk_moved tr_v v_done "
                    "route_ps sumsq_in sumsq gate_in gate_exp lg_done gate_tr gatet_done moe_h moe_gelu moe_gated moe_tr "
                    "moet_done link_p link_a alink_p")
        C = signals("c_", "mean0 rstd0 mean1 rstd1 mean2 rstd2 mean3 rstd3 xn_done tr_x xt_done zx bcd bct zx_out bcd_out "
                    "bct_out sq_out dt_in dt_exp soft lb_done cums lrow arg_done dec1 dec_done g_ps gm_done guard_ps "
                    "gmx_done flag_tr flag_out scan_ok y_ps y_out yn_done yn_tr yt_done o_ps x_done dve_link act_link")
        B = signals("b_", core + "cur_in tr_x xt_done proj sq_done ssq_done ssum_done r_done rot_b rot_sum rot_done "
                    "qkt_ready qkt_done v_ps v_done mid_done mid_kept mid_tr midt_done back_tr mean rstd xn2_done xn2_tr xt2_done "
                    "hid_ps hid_out hid_gelu hid_done f_done link_a link_f alink_p alink_f")
        prep_a, slow_dma, prob_clear = sem("prep_a"), sem("slow_dma"), sem("prob_clear")

        block = ctx.enter_context(nc.Block())

        def W2_LOADS():
            yield triu[:, :], a["triu"]
            yield later[:, :], a["later"]
            yield rot[:, :, :, :], a["rot"].rearrange("k (t p) e -> p k t e", p=P)
            yield w_in[:, :], a["w_in"]
            yield w_out[:, :, :], a["w_out"].rearrange("(c p) n -> p c n", p=P)
            yield ni[:, 0:1], a["ni_w"].rearrange("(p a) -> p a", a=1)
            yield ni[:, 1:2], a["ni_b"].rearrange("(p a) -> p a", a=1)
            yield lnw[:, :, 0], a["ln_w"].rearrange("(c p) -> p c", p=P)
            yield lnw[:, :, 1], a["ln_b"].rearrange("(c p) -> p c", p=P)
            yield now[:, 0, :], a["no_w"].rearrange("(a n) -> a n", a=1).broadcast_to((P, D))
            yield now[:, 1, :], a["no_b"].rearrange("(a n) -> a n", a=1).broadcast_to((P, D))
            for n, k in enumerate(("A_log", "dt_bias", "Dparam")):
                yield hp[:, n, :], a[k].rearrange("(a n) -> a n", a=1).broadcast_to((P, SH))
            for n, k in enumerate(("q_scale", "k_scale")):
                yield qk_scale[:, :, n, :], a[k].rearrange("(a l) e -> a l e", a=1).broadcast_to((P, DEPTH, DH))
            yield ln_gb[:, :, 0], a["f_g"]
            yield ln_gb[:, :, 1], a["f_b"]
            for c in range(6):
                f0, fn = FC[c % 3]
                f0 += FI * (c // 3)
                yield b_f1[0:fn, :, c], a["b_f1"][f0:f0 + fn, :]
            yield b_f2[:, :, :], a["b_f2"].rearrange("(a l) n -> a l n", a=1)
        N_W2 = len(list(W2_LOADS()))
        N_CONST, N_FIRST = 6, 5

        N_TABS = T * 2 + T * 2 * 2

        def exact_scan(pool):
            with nc.allow_non_contiguous_dma("rare path"):
                def moved(ins):
                    ins.then_inc(slow_dma, 16)
                    pool.wait_ge(slow_dma, 16)
                    pool.dma_reset(range(slow_dma.num, slow_dma.num + 1))
                    pool.sem_clear(slow_dma)

                def did(ins):
                    ins.then_inc(slow, 1)
                    pool.wait_ge(slow, 1)
                    pool.sem_clear(slow)

                for t in range(T):
                    moved(pool.dma_start(d_bcd[P * t:P * t + P, :], c_bcd[:, t, :]))
                    moved(pool.dma_start(d_dec[P * t:P * t + P, :], dec_all[:, SH * t:SH * t + SH]))
                    moved(pool.dma_start(d_x[P * t:P * t + P, :], c_x[:, t, :]))
                did(pool.memset(e_h[:, :, :], 0.0))
                with pool.Fori(0, S // STEPS) as n:
                    at = n * STEPS
                    for i in range(STEPS):
                        moved(pool.dma_start(e_bc[:, i:i + 1, :],
                                             d_bcd[bass.ds(at + i, 1), 0:2 * NS].unsqueeze(0).broadcast_to((P, 1, 2 * NS))))
                    for hh in range(2):
                        for e in range(2):
                            h = 2 * hh + e
                            moved(pool.dma_start(e_dec[64 * e:64 * e + 64, :, hh],
                                                 d_dec[bass.ds(at, STEPS), h].unsqueeze(0).broadcast_to((64, STEPS))))
                        moved(pool.dma_start(e_x[:, hh, :], d_x[bass.ds(at, STEPS), P * hh:P * hh + P].rearrange("s p -> p s")))
                    for i in range(STEPS):
                        for hh in range(2):
                            hs = e_h[:, hh, :]
                            did(pool.tensor_scalar(e_t[:, :], e_bc[:, i, 0:NS], e_x[:, hh, i:i + 1], None, ALU.mult))
                            did(pool.tensor_scalar(hs, hs, e_dec[:, i, hh:hh + 1], None, ALU.mult))
                            did(pool.tensor_tensor(hs, hs, e_t[:, :], ALU.add))
                            did(pool.tensor_scalar(hs, hs, -10.0, 10.0, ALU.max, ALU.min))
                            did(pool.tensor_tensor(e_t[:, :], hs, e_bc[:, i, NS:2 * NS], ALU.mult))
                            w = NS // 2
                            while w >= 1:
                                dst = e_t[:, 0:w] if w > 1 else e_y[:, hh, i:i + 1]
                                did(pool.tensor_tensor(dst, e_t[:, 0:w], e_t[:, w:2 * w], ALU.add))
                                w //= 2
                    for hh in range(2):
                        moved(pool.dma_start(d_y[bass.ds(at, STEPS), P * hh:P * hh + P].rearrange("s p -> p s"), e_y[:, hh, :]))
                for t in range(T):
                    moved(pool.dma_start(c_y[:, t, :], d_y[P * t:P * t + P, :]))
        def wait(eng, s, n):
            if not isinstance(n, int) or n > 0:
                eng.wait_ge(s, n)

        def chain(eng, s, it, per):
            n = [0]

            def link(ins):
                n[0] += 1
                ins.then_inc(s, 1)
                eng.wait_ge(s, it * per + n[0])
                return ins
            link.n, link.sem, link.it = n, s, it
            link.per = per
            return link

        def tile_cols(span):
            return [(0, span[0][1]), (span[0][1], span[0][1] + span[1][1])]

        def pe_heads(pe, G, u, span, mask, extra):
            cols = tile_cols(span)
            local = span is LOCAL

            def scores(h):
                b = DH * (h % 2)
                wait(pe, G["exp_done"], u * H + max(h - 1, 0))
                pe.matmul(sc[h % 2][:, 0:cols[1][1]], ident_bf[:, :], mask[:, :], start=True, stop=False)
                for t in range(T):
                    k0, kn = span[t]
                    m = pe.matmul(sc[h % 2][:, cols[t][0]:cols[t][1]], qt[b:b + DH, h // 2, P * t:P * t + P],
                                  kt[b:b + DH, h // 2, k0:k0 + kn], start=False, stop=(t == T - 1))
                m.then_inc(G["scores"], 1)

            def turn(h):
                pe.wait_ge(G["exp_done"], u * H + h + 1)
                wait(pe, G["pt_done"], u * H + max(h - 1, 0))
                q = prob[:, h % 2, :]
                pe.transpose(tp[h % 2][:, 0:128], q[:, 0:128], ident[:, :])
                pe.transpose(tp[h % 2][:, 128:256], q[:, 384:512], ident[:, :])
                if local:
                    m = pe.transpose(tp[h % 2][:, 256:256 + WINDOW], q[0:WINDOW, 256:384], ident[0:WINDOW, 0:WINDOW])
                else:
                    m = pe.transpose(tp[h % 2][:, 256:384], q[:, 256:384], ident[:, :])
                m.then_inc(G["pt_tr"], 1)

            def weigh(h):
                pe.wait_ge(G["pt_done"], u * H + h + 1)
                if h % HALF == 0:
                    wait(pe, G["o_done"], u * 2 + h // HALF)
                q = pt[:, h % 2, :]
                c = DH * (h % HALF)
                vv = [v[:, t, h * DH:h * DH + DH] for t in range(T)]
                pe.matmul(ov[0][:, c:c + DH], q[:, 0:128], vv[0], start=True, stop=True)
                pe.matmul(ov[1][:, c:c + DH], q[:, 128:256], vv[1], start=True, stop=False)
                pe.matmul(ov[1][:, c:c + DH], q[:, 256:384], vv[0], start=False, stop=True).then_inc(G["pv_done"], 1)

            scores(0)
            scores(1)
            for h in range(H):
                turn(h)
                if h + 2 < H:
                    scores(h + 2)
                extra(h)
                weigh(h)

        def pe_turn_out(pe, G, u):
            for g in range(4):
                t, hf = g // 2, g % 2
                if g == 0:
                    pe.wait_ge(G["o_done"], u * 2 + 2)
                    pe.wait_ge(G["pt_done"], u * H + H)
                if g >= 2:
                    pe.wait_ge(G["ot_done"], u * 4 + g - 1)
                for j in range(4):
                    m = pe.transpose(tp[g % 2][:, 128 * j:128 * j + 128],
                                     o[:, t, 512 * hf + 128 * j:512 * hf + 128 * j + 128], ident[:, :])
                m.then_inc(G["o_tr"], 1)

        def on_dve(h):
            return h % 4 != 3

        def pt_copy(eng, G, u, h, n, copy):
            eng.wait_ge(G["pt_tr"], u * H + h + 1)
            wait(eng, G["pv_done"], u * H + max(h - 1, 0))
            wait(eng, G["pt_done"], u * H + h)
            copy(pt[:, h % 2, 0:n], tp[h % 2][:, 0:n]).then_inc(G["pt_done"], 1)

        def dve_heads(dve, G, u, span, link, extra):
            cols = tile_cols(span)
            n = 256 + (WINDOW if span is LOCAL else P)

            def top(h):
                dve.wait_ge(G["scores"], u * H + h + 1)
                for t in range(T):
                    m = dve.tensor_reduce(nm[:, h, t:t + 1], sc[h % 2][:, cols[t][0]:cols[t][1]], AX.X, ALU.max,
                                          negate=True)
                m.then_inc(G["max_done"], 1)

            top(0)
            top(1)
            for h in range(H):
                if on_dve(h):
                    pt_copy(dve, G, u, h, n, dve.tensor_copy)
                if h + 2 < H:
                    top(h + 2)
                if h == HALF:
                    dve_norm(dve, G, u, 0, link)
                extra(h)

        def dve_norm(dve, G, u, hf, link):
            dve.wait_ge(G["pv_done"], u * H + HALF * (hf + 1))
            link(dve.reciprocal(rinv[:, :, HALF * hf:HALF * hf + HALF], rs[:, :, HALF * hf:HALF * hf + HALF]))
            for t in range(T):
                m = dve.tensor_tensor(
                    o[:, t, 512 * hf:512 * hf + 512].rearrange("p (h e) -> p h e", h=HALF),
                    ov[t][:, :].rearrange("p (h e) -> p h e", h=HALF),
                    rinv[:, t, HALF * hf:HALF * hf + HALF].unsqueeze(2).broadcast_to((P, HALF, DH)), ALU.mult)
            m.then_inc(G["o_done"], 1)

        def out_copy(eng, G, u, g, copy):
            eng.wait_ge(G["o_tr"], u * 4 + g + 1)
            wait(eng, G["ot_done"], u * 4 + g)
            t, hf = g // 2, g % 2
            copy(ot[:, 4 * hf:4 * hf + 4, P * t:P * t + P],
                 tp[g % 2][:, :].rearrange("p (c n) -> p c n", c=4)).then_inc(G["ot_done"], 1)

        def act_heads(act, G, u, span, extra):
            cols = tile_cols(span)
            width = 256 + (WINDOW if span is LOCAL else P)

            def expo(h):
                act.wait_ge(G["max_done"], u * H + h + 1)
                wait(act, G["pt_tr"], u * H + max(h - 1, 0))
                for t in range(T):
                    n = span[t][1]
                    at = [0, 512 - n][t]
                    m = act.activation(prob[:, h % 2, at:at + n], sc[h % 2][:, cols[t][0]:cols[t][1]], ACT.Exp,
                                       bias=nm[:, h, t:t + 1], accum_out=rs[:, t, h:h + 1])
                m.then_inc(G["exp_done"], 1)

            expo(0)
            expo(1)
            for h in range(H):
                if not on_dve(h):
                    pt_copy(act, G, u, h, width, lambda o_, i_: act.activation(o_, i_, ACT.Copy))
                if h + 2 < H:
                    expo(h + 2)
                extra(h)

        def stats(dve, link, src, s, m_v):
            dve.bn_stats(s, src).then_inc(link.sem, 1)
            link.n[0] += 1
            dve.wait_ge(link.sem, link.it * link.per + link.n[0])
            dve.tensor_copy(carrier[:, 0:1], eps_c[:, 0:1])
            return dve.bn_aggr(m_v, s)

        def rstd(act, link, m_v, r):
            link(act.activation(r[:, 1:2], m_v[:, 1:2], ACT.Ln, bias=eps_c[:, 0:1]))
            return act.activation(r[:, 0:1], r[:, 1:2], ACT.Exp, scale=-0.5)

        def a_stages(i):
            known = isinstance(i, int)
            return (not known or i < NB), (not known or i > 0)

        A_PAIR = [5, 6, 7, 8, 9, 10, 11, 12]

        def a_pe(pe, i):
            new, old = a_stages(i)
            u = i - 1
            if old:
                pe.wait_ge(A["xt_now"], u + 1)
                wait(pe, A["state_done"], u)
                for g in range(4):
                    t, c = g // 2, g % 2
                    if g == 1:
                        pe.wait_ge(A["qk_done"], u * 8 + 8)
                    if g >= 2:
                        pe.wait_ge(A["v_done"], u * 4 + g - 1)
                    pe.matmul(pj[g % 2][:, :], xt[:, P * t:P * t + P],
                              w_big[:, 2 * INNER + 512 * c:2 * INNER + 512 * c + 512], start=True, stop=True
                              ).then_inc(A["tr_v"], 1)
                for t in range(T):
                    m = pe.matmul(ov[1][:, 16 * t:16 * t + 16], xt[:, P * t:P * t + P], route[:, :], start=True, stop=True)
                m.then_inc(A["route_ps"], 1)
                for t in range(T):
                    pe.wait_ge(A["v_done"], u * 4 + 3 + t)
                    pe.matmul(pj[t][:, :], xt[:, P * t:P * t + P], w_moe1[:, :], start=True, stop=False)
                    pe.matmul(pj[t][:, :], ones[0:1, :], b_moe1[:, :], start=False, stop=True).then_inc(A["moe_h"], 1)
                pe.wait_ge(A["gate_in"], u * T + T)
                pe.wait_ge(A["qk_moved"], u * 2 + 2)

            def extra(h):
                if new and h == 3:
                    pe.wait_ge(A["xn_done"], i * T + T)
                    wait(pe, A["moe_gelu"], i * T)
                    for t in range(T):
                        m = pe.transpose(pj[1][:, P * t:P * t + P], xn[:, t, :], ident[:, :])
                    m.then_inc(A["tr_x"], 1)
                if new and h in A_PAIR:
                    p = h - A_PAIR[0]
                    if p == 0:
                        pe.wait_ge(A["xt_done"], i + 1)
                    wait(pe, A["qk_done"], i * 8 + p)
                    for n in range(2):
                        m = pe.matmul(pj[1][:, S * n:S * n + S], w_big[:, INNER * n + P * p:INNER * n + P * p + P],
                                      xt2[:, :], start=True, stop=True)
                    m.then_inc(A["qkt_done"], 1)
                if old and h in (4, 5):
                    t = h - 4
                    pe.wait_ge(A["moe_gated"], u * T + t + 1)
                    wait(pe, A["moet_done"], u * T + t)
                    for c in range(4):
                        m = pe.transpose(pj[0][:, P * c:P * c + P], rb[:, t, P * c:P * c + P], ident[:, :])
                    m.then_inc(A["moe_tr"], 1)
                if old and h == 6:
                    pe.wait_ge(A["moet_done"], u * T + T)
                    for t in range(T):
                        m = pe.transpose(pj[0][0:NE, P * t:P * t + P], lg[:, t, 56:64], ident[:, :])
                    m.then_inc(A["gate_tr"], 1)
            if not old:
                for h in range(H):
                    extra(h)
                return
            pe_heads(pe, A, u, CAUSAL, causal_bf, extra)
            pe_turn_out(pe, A, u)
            pe.wait_ge(A["ot_done"], u * 4 + 4)
            pe.wait_ge(A["gatet_done"], u + 1)
            for t in range(T):
                acc = ov[0][:, D * t:D * t + D]
                for c in range(8):
                    pe.matmul(acc, ot[:, c, P * t:P * t + P], w_o[:, c, :], start=(c == 0), stop=False)
                for c in range(4):
                    pe.matmul(acc, moe_t[:, c, P * t:P * t + P], w_moe2[:, c, :], start=False, stop=False)
                pe.matmul(acc, gate_t[:, P * t:P * t + P], b_moe2[:, :], start=False, stop=True).then_inc(A["wo_done"], 1)

        moe_t = sq[:, :, :].rearrange("p a n -> p (a n)").rearrange("p (c n) -> p c n", c=4)

        def a_dve(dve, i):
            new, old = a_stages(i)
            u = i - 1
            if new:
                link_p = chain(dve, A["link_p"], i, 3)
                x_new = [x[:, bass.ds(i * T + t, 1), :].rearrange("p a n -> p (a n)") for t in range(T)]
            if old:
                link = chain(dve, A["link_a"], u, 18)
                dve.wait_ge(A["xt_done"], u + 1)
                wait(dve, A["wo_done"], u * T)
                dve.tensor_copy(xt[:, :], xt2[:, :]).then_inc(A["xt_now"], 1)
                dve.wait_ge(A["qk_done"], u * 8 + 8)
                dve.tensor_copy(qt[:, :, :], rq[:, :, 0:S]).then_inc(A["qk_moved"], 1)
                for g in (1, 3):
                    dve.wait_ge(A["tr_v"], u * 4 + g + 1)
                    wait(dve, A["v_done"], u * 4 + g)
                    dve.tensor_copy(v[:, g // 2, 512:1024], pj[1][:, :]).then_inc(A["v_done"], 1)
                dve.wait_ge(A["route_ps"], u + 1)
                dve.wait_ge(A["sumsq"], u * T + T)
                for t in range(T):
                    q = lg[:, t, :]
                    link(dve.tensor_scalar(q[:, 32:40], ov[1][:, 16 * t:16 * t + 8], sm[:, t, 4:5], None, ALU.mult))
                    link(dve.tensor_tensor(q[:, 0:8], q[:, 32:40], ov[1][:, 16 * t + 8:16 * t + 16], ALU.add))
                    dve.tensor_copy(carrier[:, 0:1], eps_c[:, 0:1])
                    link(dve.max(q[:, 8:16], q[:, 0:8]))
                    link(dve.tensor_scalar(q[:, 40:41], q[:, 8:9], -1.0, None, ALU.mult))
                    dve.tensor_scalar(q[:, 24:32], q[:, 0:8], q[:, 9:10], None, ALU.is_ge).then_inc(A["gate_in"], 1)

            def extra(h):
                if new and h == 0:
                    for t in range(T):
                        stats(dve, link_p, x_new[t], st[:, t, :], mv[:, t, :]).then_inc(A["mean_done"], 1)
                if new and h == 2:
                    for t in range(T):
                        dve.wait_ge(A["xnorm_done"], i * T + t + 1)
                        dve.tensor_scalar(xn[:, t, :], x_new[t], mv[:, t, 0:1], sm[:, t, 0:1], ALU.subtract, ALU.mult
                                          ).then_inc(A["xn_done"], 1)
                if new and h == 3:
                    dve.wait_ge(A["tr_x"], i + 1)
                    dve.tensor_copy(xt2[:, :], pj[1][:, 0:S]).then_inc(A["xt_done"], 1)
                if new and h == 4:
                    dve.wait_ge(A["xn_done"], i * T + T)
                    for t in range(T):
                        m = dve.tensor_tensor_reduce(hid[:, t, 0:D], xn[:, t, :], xn[:, t, :], 1.0, 0.0, ALU.mult, ALU.add,
                                                     sm[:, t, 5:6])
                    link_p(m)
                    dve.tensor_scalar(sm[:, :, 2:3], sm[:, :, 5:6], 1e-24, None, ALU.max).then_inc(A["sumsq_in"], 1)
                if new and h in A_PAIR and (h - A_PAIR[0]) % 2 == 1:
                    p = h - A_PAIR[0]
                    dve.wait_ge(A["qkt_done"], i * 8 + p + 1)
                    dve.wait_ge(A["qk_done"], i * 8 + p)
                    if p == 1:
                        wait(dve, A["qk_moved"], i * 2)
                    dve.tensor_scalar(rq[:, p, 0:S], pj[1][:, 0:S], 0.125, None, ALU.mult)
                    dve.tensor_copy(rq[:, p, S:2 * S], pj[1][:, S:2 * S]).then_inc(A["qk_done"], 1)
                if old and h == 1:
                    for t in range(T):
                        q = lg[:, t, :]
                        dve.wait_ge(A["gate_exp"], u * T + t + 1)
                        link(dve.tensor_tensor(q[:, 24:32], q[:, 24:32], q[:, 16:24], ALU.mult))
                        link(dve.tensor_reduce(q[:, 41:42], q[:, 24:32], AX.X, ALU.add))
                        link(dve.reciprocal(q[:, 42:43], q[:, 41:42]))
                        link(dve.tensor_scalar(q[:, 56:64], q[:, 24:32], q[:, 42:43], None, ALU.mult))
                    dve.tensor_copy(carrier[:, 0:1], eps_c[:, 0:1]).then_inc(A["lg_done"], 1)
                if old and h in (4, 5):
                    t = h - 4
                    dve.wait_ge(A["moe_tr"], u * T + t + 1)
                    dve.tensor_copy(moe_t[:, :, P * t:P * t + P], pj[0][:, :].rearrange("p (c n) -> p c n", c=4)
                                    ).then_inc(A["moet_done"], 1)
                if old and h == 6:
                    dve.wait_ge(A["gate_tr"], u + 1)
                    dve.tensor_copy(gate_t[:, :], pj[0][0:NE, 0:S]).then_inc(A["gatet_done"], 1)
            if not old:
                for h in range(H):
                    extra(h)
                return
            dve_heads(dve, A, u, CAUSAL, link, extra)
            dve_norm(dve, A, u, 1, link)
            for g in (1, 3):
                out_copy(dve, A, u, g, dve.tensor_copy)
            dve.wait_ge(A["wo_done"], u * T + T)
            xs = x[:, bass.ds(u * T, T), :]
            dve.tensor_tensor(xs, xs, ov[0][:, 0:T * D].rearrange("p (t n) -> p t n", t=T), ALU.add
                              ).then_inc(A["state_done"], 1)
            assert link.n[0] == link.per, link.n

        def a_act(act, i):
            new, old = a_stages(i)
            u = i - 1
            if new:
                link_p = chain(act, A["alink_p"], i, 4)
            if old:
                act.preload_act_table_set("gelu_and_others")
                act.wait_ge(A["qk_done"], u * 8 + 8)
                wait(act, A["wo_done"], u * T)
                act.activation(kt[:, :, :], rq[:, :, S:2 * S], ACT.Copy).then_inc(A["qk_moved"], 1)
                for g in (0, 2):
                    act.wait_ge(A["tr_v"], u * 4 + g + 1)
                    wait(act, A["v_done"], u * 4 + g)
                    act.activation(v[:, g // 2, 0:512], pj[0][:, :], ACT.Copy).then_inc(A["v_done"], 1)
                for t in range(T):
                    act.wait_ge(A["moe_h"], u * T + t + 1)
                    act.activation(rb[:, t, :], pj[t][:, :], ACT.Gelu).then_inc(A["moe_gelu"], 1)
            act.preload_act_table_set("natural_log_exp_and_others")

            def extra(h):
                if old and h == 0:
                    for t in range(T):
                        q = lg[:, t, :]
                        act.wait_ge(A["gate_in"], u * T + t + 1)
                        act.activation(q[:, 16:24], q[:, 0:8], ACT.Exp, bias=q[:, 40:41]).then_inc(A["gate_exp"], 1)
                if new and h == 1:
                    for t in range(T):
                        act.wait_ge(A["mean_done"], i * T + t + 1)
                        rstd(act, link_p, mv[:, t, :], sm[:, t, 0:2]).then_inc(A["xnorm_done"], 1)
                if new and h == 5:
                    for t in range(T):
                        act.wait_ge(A["sumsq_in"], i + 1)
                        link_p(act.activation(sm[:, t, 3:4], sm[:, t, 2:3], ACT.Ln, scale=2.0 ** 20))
                        act.activation(sm[:, t, 4:5], sm[:, t, 3:4], ACT.Exp, scale=-0.5, bias=eps_c[:, 1:2]
                                       ).then_inc(A["sumsq"], 1)
                if new and h in A_PAIR and (h - A_PAIR[0]) % 2 == 0:
                    p = h - A_PAIR[0]
                    act.wait_ge(A["qkt_done"], i * 8 + p + 1)
                    wait(act, A["qk_done"], i * 8 + p)
                    if p == 0:
                        wait(act, A["qk_moved"], i * 2)
                    act.activation(rq[:, p, 0:S], pj[1][:, 0:S], ACT.Copy, scale=0.125)
                    act.activation(rq[:, p, S:2 * S], pj[1][:, S:2 * S], ACT.Copy).then_inc(A["qk_done"], 1)
            if not old:
                for h in range(H):
                    extra(h)
                return
            act_heads(act, A, u, CAUSAL, extra)
            for g in (0, 2):
                out_copy(act, A, u, g, lambda o_, i_: act.activation(o_, i_, ACT.Copy))

        NU = DEPTH * NB

        def b_stages(i):
            known = isinstance(i, int)
            return [not known or 0 <= i - n < NU for n in range(4)]

        def layer_of(n):
            return n // NB

        FIRST_HALF = {10: 0, 11: 1}
        HID_SLOT = {7: 0, 8: 1, 9: 2}

        def b_turn_out(pe, n, g, bank):
            hf, t = g // 2, g % 2
            pe.wait_ge(B["o_done"], n * 2 + hf + 1)
            if g == 1:
                pe.wait_ge(B["ot_done"], n * 4 + 1)
            if hf:
                pe.wait_ge(B["pt_done"], n * H + H)
            for j in range(4):
                m = pe.transpose(bank[:, P * j:P * j + P], o[:, t, 512 * hf + P * j:512 * hf + P * j + P], ident[:, :])
            m.then_inc(B["o_tr"], 1)

        def b_out_copy(eng, n, g, bank, copy):
            hf, t = g // 2, g % 2
            eng.wait_ge(B["o_tr"], n * 4 + g + 1)
            wait(eng, B["ot_done"], n * 4 + g)
            copy(ot[:, 4 * hf:4 * hf + 4, P * t:P * t + P], bank[:, :].rearrange("p (c n) -> p c n", c=4)
                 ).then_inc(B["ot_done"], 1)

        def b_pe(pe, i):
            new, att, ffn, last = b_stages(i)
            u, w, z = i - 1, i - 2, i - 3

            def values(g):
                t, c = g // 2, g % 2
                if g == 0:
                    pe.wait_ge(v_in, 16 * (layer_of(u) + 1))
                    if ffn:
                        pe.wait_ge(B["ot_done"], w * 4 + 2)
                if g == 1:
                    pe.wait_ge(B["rot_b"], u * 8 + 8)
                if g >= 2:
                    pe.wait_ge(B["v_done"], u * 4 + g - 1)
                pe.matmul(pj[g % 2][:, :], xsh[:, P * t:P * t + P],
                          w_big[:, 2 * INNER + 512 * c:2 * INNER + 512 * c + 512], start=True, stop=True
                          ).then_inc(B["v_ps"], 1)

            def turn_qk(g):
                pe.wait_ge(B["rot_done"], u * 8 + g + 1)
                if g >= 2:
                    pe.wait_ge(B["qkt_done"], u * 8 + g - 1)
                elif ffn:
                    pe.wait_ge(B["ot_done"], w * 4 + 3 + g)
                for j in range(4):
                    m = pe.transpose(tp[g % 2][:, P * j:P * j + P], rq[:, g, P * j:P * j + P], ident[:, :])
                m.then_inc(B["qkt_ready"], 1)

            if new:
                pe.wait_ge(B["cur_in"], i + 1)
                if ffn:
                    pe.wait_ge(B["exp_done"], w * H + H)
                for t in range(T):
                    m = pe.transpose(sc[0][:, P * t:P * t + P], cur[:, t, :], ident[:, :])
                m.then_inc(B["tr_x"], 1)
            if att:
                values(0)
                values(1)
            if ffn:
                b_turn_out(pe, w, 2, tp[0])
                b_turn_out(pe, w, 3, tp[1])
            if att:
                values(2)
                values(3)
                turn_qk(0)
                turn_qk(1)
            if ffn:
                pe.wait_ge(B["ot_done"], w * 4 + 4)
                pe.wait_ge(o_in, 16 * (layer_of(w) + 1))
                for t in range(T):
                    for c in range(8):
                        m = pe.matmul(ov[0][:, D * t:D * t + D], ot[:, c, P * t:P * t + P], w_o[:, c, :],
                                      start=(c == 0), stop=(c == 7))
                m.then_inc(B["wo_done"], 1)
            if att:
                turn_qk(2)
                turn_qk(3)
            if last:
                pe.wait_ge(B["hid_done"], z * 3 + 3)
                if ffn:
                    pe.wait_ge(B["o_done"], w * 2 + 2)
                for t in range(T):
                    for c, (f0, fn) in enumerate(FC):
                        pe.matmul(ov[1][:, D * t:D * t + D], hid[0:fn, c, P * t:P * t + P], w_f2[0:fn, c, :],
                                  start=(c == 0), stop=False)
                    m = pe.matmul(ov[1][:, D * t:D * t + D], ones[0:1, :],
                                  b_f2[:, bass.ds(layer_of(z), 1), :].rearrange("p a n -> p (a n)"), start=False, stop=True)
                m.then_inc(B["f_done"], 1)
            if att:
                for g in range(4, 8):
                    turn_qk(g)
                pe.wait_ge(B["qkt_done"], u * 8 + 8)
                pe.wait_ge(B["v_done"], u * 4 + 4)
            if new:
                pe.wait_ge(B["xt_done"], i + 1)

            def extra(h):
                if h == 0:
                    if ffn:
                        pe.wait_ge(B["mid_done"], w + 1)
                    if last:
                        pe.wait_ge(B["state_done"], z + 1)
                if new and h % 2 == 0:
                    g = h // 2
                    if g == 0:
                        pe.wait_ge(qk_in, 16 * (layer_of(i) + 1))
                        if att:
                            pe.wait_ge(B["v_done"], u * 4 + 4)
                    else:
                        pe.wait_ge(B["rot_b"], i * 8 + g)
                    t, c = g // 4, g % 4
                    pe.matmul(pj[1][:, :], xsh[:, P * t:P * t + P], w_big[:, 512 * c:512 * c + 512], start=True, stop=True
                              ).then_inc(B["proj"], 1)
                if ffn and h == 1:
                    for t in range(T):
                        m = pe.transpose(pj[0][:, P * t:P * t + P], mid[:, t, :], ident[:, :])
                    m.then_inc(B["mid_tr"], 1)
                if ffn and h == 2:
                    pe.wait_ge(B["midt_done"], w + 1)
                    for t in range(T):
                        m = pe.transpose(pj[0][:, S + P * t:S + P * t + P], xsf[:, P * t:P * t + P], ident[:, :])
                    m.then_inc(B["back_tr"], 1)
                if ffn and h == 5:
                    pe.wait_ge(B["xn2_done"], w * T + T)
                    for t in range(T):
                        m = pe.transpose(pj[0][:, P * t:P * t + P], xn2[:, t, :], ident[:, :])
                    m.then_inc(B["xn2_tr"], 1)
                if ffn and h in HID_SLOT:
                    c = HID_SLOT[h]
                    f0, fn = FC[c]
                    if c == 0:
                        pe.wait_ge(B["xt2_done"], w + 1)
                        pe.wait_ge(f_in, 16 * 4 * (layer_of(w) + 1))
                    wait(pe, B["hid_out"], w * 3 + c)
                    for n in range(2):
                        m = pe.matmul(pj[0][0:fn, S * n:S * n + S], w_f1[:, FI * n + f0:FI * n + f0 + fn], xt2[:, :],
                                      start=True, stop=True)
                    m.then_inc(B["hid_ps"], 1)
                if att and h in FIRST_HALF:
                    if ffn and FIRST_HALF[h] == 0:
                        pe.wait_ge(B["hid_out"], w * 3 + 3)
                    b_turn_out(pe, u, FIRST_HALF[h], pj[0])
            if att:
                pe_heads(pe, B, u, LOCAL, local_bf, extra)
            else:
                for h in range(H):
                    extra(h)

        def shifted(dve, dst, src, done):
            dve.tensor_copy(dst[0:64, :], src[0:64, 0:S])
            dve.tensor_copy(dst[64:128, 1:S], src[64:128, 0:S - 1]).then_inc(done, 1)

        def turned(g, copy):
            t, c = g // 4, g % 4
            dst = (qt if c < 2 else kt)[:, 4 * (c % 2):4 * (c % 2) + 4, P * t:P * t + P]
            return copy(dst, tp[g % 2][:, :].rearrange("p (c n) -> p c n", c=4))

        def b_dve(dve, i):
            new, att, ffn, last = b_stages(i)
            u, w, z = i - 1, i - 2, i - 3
            link = chain(dve, B["link_a"], u, 2)
            link_f = chain(dve, B["link_f"], w, 2)

            def turn_odd(g):
                dve.wait_ge(B["qkt_ready"], u * 8 + g + 1)
                dve.wait_ge(B["qkt_done"], u * 8 + g)
                turned(g, dve.tensor_copy).then_inc(B["qkt_done"], 1)

            if ffn:
                b_out_copy(dve, w, 3, tp[1], dve.tensor_copy)
            if last:
                fb = b_f1[:, bass.ds(layer_of(z), 1), :].rearrange("p a n -> p (a n)")
                for c, (f0, fn) in enumerate(FC):
                    dve.wait_ge(B["hid_gelu"], z * 3 + c + 1)
                    dve.scalar_tensor_tensor(hid[0:fn, c, :], hsb[0:fn, c, 0:S], fb[0:fn, c:c + 1],
                                             gel[0:fn, c, :], ALU.add, ALU.mult).then_inc(B["hid_done"], 1)
            if att:
                turn_odd(1)
            if ffn:
                dve.wait_ge(B["wo_done"], w + 1)
                if last:
                    dve.wait_ge(B["mid_kept"], z + 1)
                dve.tensor_tensor(mid[:, :, :], y[:, bass.ds((w % NB) * T, T), :],
                                  ov[0][:, 0:2 * D].rearrange("p (t n) -> p t n", t=T), ALU.add).then_inc(B["mid_done"], 1)
            if new:
                dve.wait_ge(B["tr_x"], i + 1)
                if att:
                    dve.wait_ge(B["v_ps"], u * 4 + 4)
                shifted(dve, xsh, sc[0], B["xt_done"])
            if att:
                turn_odd(3)
                turn_odd(5)
            if last:
                dve.wait_ge(B["f_done"], z + 1)
                if not ffn:
                    dve.wait_ge(B["mid_kept"], z + 1)
                ys = y[:, bass.ds((z % NB) * T, T), :]
                dve.tensor_tensor(ys, ys, ov[1][:, 0:2 * D].rearrange("p (t n) -> p t n", t=T), ALU.add
                                  ).then_inc(B["state_done"], 1)
            if att:
                turn_odd(7)

            def rotate(g):
                t, c = g // 4, g % 4
                k = 2 * (c // 2)
                src = pj[1][:, :].rearrange("p (h e) -> p h e", h=HALF)
                heads = (P, HALF, 32)
                dve.wait_ge(B["sq_done"], i * 8 + g + 1)
                dve.tensor_reduce(ss[:, g, :], sq[:, g % 2, :].rearrange("p (h e) -> p h e", h=HALF), AX.X, ALU.add
                                  ).then_inc(B["ssq_done"], 1)
                if g == 0:
                    dve.wait_ge(tabs_done, (layer_of(i) + 1) * N_TABS)
                    if att:
                        dve.wait_ge(B["qkt_ready"], u * 8 + 8)
                dve.tensor_tensor(rq[:, g, :].rearrange("p (h e) -> p h e", h=HALF), src,
                                  tabs[:, k, t, :].unsqueeze(1).broadcast_to((P, HALF, DH)), ALU.mult)
                dve.wait_ge(B["ssq_done"], i * 8 + g + 1)
                dve.tensor_scalar(ss[:, g, :], ss[:, g, :], 1e-24, None, ALU.max).then_inc(B["ssum_done"], 1)
                wait(dve, B["rot_sum"], i * 8 + max(g - 1, 0))
                dst = rb[:, g % 2, :].rearrange("p (h e) -> p h e", h=HALF)
                dve.tensor_tensor(dst[:, :, 0:32], src[:, :, 32:64],
                                  tabs[:, k + 1, t, 0:32].unsqueeze(1).broadcast_to(heads), ALU.mult)
                dve.tensor_tensor(dst[:, :, 32:64], src[:, :, 0:32],
                                  tabs[:, k + 1, t, 32:64].unsqueeze(1).broadcast_to(heads), ALU.mult
                                  ).then_inc(B["rot_b"], 1)

            def extra(h):
                if new and h % 2 == 1:
                    rotate(h // 2)
                if ffn and h == 1:
                    dve.wait_ge(B["mid_tr"], w + 1)
                    shifted(dve, xsf, pj[0], B["midt_done"])
                if ffn and h == 2:
                    dve.wait_ge(B["back_tr"], w + 1)
                    for t in range(T):
                        stats(dve, link_f, pj[0][:, S + P * t:S + P * t + P], st[:, t, :], mv[:, t, :]
                              ).then_inc(B["mean"], 1)
                if ffn and h == 4:
                    for t in range(T):
                        dve.wait_ge(B["rstd"], w * T + t + 1)
                        dve.tensor_scalar(xn2[:, t, :], pj[0][:, S + P * t:S + P * t + P], mv[:, t, 0:1], sm[:, t, 0:1],
                                          ALU.subtract, ALU.mult).then_inc(B["xn2_done"], 1)
                if ffn and h == 6:
                    dve.wait_ge(B["xn2_tr"], w + 1)
                    gb = ln_gb[:, bass.ds(layer_of(w), 1), :].rearrange("p a n -> p (a n)")
                    dve.tensor_scalar(xt2[:, :], pj[0][:, 0:S], gb[:, 0:1], gb[:, 1:2],
                                      ALU.mult, ALU.add).then_inc(B["xt2_done"], 1)
                if att and h == 12:
                    b_out_copy(dve, u, 1, pj[0], dve.tensor_copy)
            if att:
                dve_heads(dve, B, u, LOCAL, link, extra)
                dve_norm(dve, B, u, 1, link)
            else:
                for h in range(H):
                    extra(h)

        def b_act(act, i):
            new, att, ffn, last = b_stages(i)
            u, w, z = i - 1, i - 2, i - 3
            link = chain(act, B["alink_p"], i, 8)
            link_f = chain(act, B["alink_f"], w, 2)
            copy = lambda o_, i_: act.activation(o_, i_, ACT.Copy)

            def value(g):
                act.wait_ge(B["v_ps"], u * 4 + g + 1)
                copy(v[:, g // 2, 512 * (g % 2):512 * (g % 2) + 512], pj[g % 2][:, :]).then_inc(B["v_done"], 1)

            def turn_even(g):
                act.wait_ge(B["qkt_ready"], u * 8 + g + 1)
                wait(act, B["qkt_done"], u * 8 + g)
                turned(g, copy).then_inc(B["qkt_done"], 1)

            if att:
                value(0)
                value(1)
            if ffn:
                b_out_copy(act, w, 2, tp[0], copy)
            if att:
                value(2)
                value(3)
                for g in (0, 2, 4, 6):
                    turn_even(g)
            act.preload_act_table_set("natural_log_exp_and_others")

            def factor(g):
                act.wait_ge(B["ssum_done"], i * 8 + g + 1)
                link(act.activation(ss[:, g, :], ss[:, g, :], ACT.Ln, scale=2.0 ** 20))
                act.activation(ss[:, g, :], ss[:, g, :], ACT.Exp, scale=-0.5, bias=eps_c[:, 1:2]).then_inc(B["r_done"], 1)

            def extra(h):
                if ffn and h == 3:
                    for t in range(T):
                        act.wait_ge(B["mean"], w * T + t + 1)
                        rstd(act, link_f, mv[:, t, :], sm[:, t, 0:2]).then_inc(B["rstd"], 1)
                if new and h % 2 == 0:
                    g = h // 2
                    act.wait_ge(B["proj"], i * 8 + g + 1)
                    wait(act, B["ssum_done"], i * 8 + max(g - 1, 0))
                    act.activation(sq[:, g % 2, :], pj[1][:, :], ACT.Square).then_inc(B["sq_done"], 1)
                    if g >= 1:
                        factor(g - 1)
                if ffn and h in HID_SLOT:
                    c = HID_SLOT[h]
                    act.wait_ge(B["hid_ps"], w * 3 + c + 1)
                    if last and c == 0:
                        act.wait_ge(B["hid_done"], z * 3 + 3)
                    fn = FC[c][1]
                    copy(hsb[0:fn, c, :], pj[0][0:fn, :]).then_inc(B["hid_out"], 1)
                if att and h == 10:
                    b_out_copy(act, u, 0, pj[0], copy)
            if att:
                act_heads(act, B, u, LOCAL, extra)
            else:
                for h in range(H):
                    extra(h)
            if new:
                factor(7)
            if ffn:
                act.preload_act_table_set("gelu_and_others")
                fb = b_f1[:, bass.ds(layer_of(w), 1), :].rearrange("p a n -> p (a n)")
                act.wait_ge(B["hid_out"], w * 3 + 3)
                for c, (f0, fn) in enumerate(FC):
                    act.activation(gel[0:fn, c, :], hsb[0:fn, c, S:2 * S], ACT.Gelu, bias=fb[0:fn, 3 + c:4 + c]
                                   ).then_inc(B["hid_gelu"], 1)

        def b_cur(pool, n, first_layer=False):
            if not first_layer:
                pool.wait_ge(B["state_done"], n - NB + 1)
            wait(pool, B["tr_x"], n)
            pool.tensor_copy(cur[:, :, :], y[:, bass.ds((n % NB) * T, T), :]).then_inc(B["cur_in"], 1)

        def b_keep(pool, n):
            pool.wait_ge(B["mid_done"], n + 1)
            pool.tensor_copy(y[:, bass.ds((n % NB) * T, T), :], mid[:, :, :]).then_inc(B["mid_kept"], 1)

        def b_rotate(pool, i):
            for g in range(8):
                pool.wait_ge(B["rot_b"], i * 8 + g + 1)
                pool.tensor_tensor(rq[:, g, :], rq[:, g, :], rb[:, g % 2, :], ALU.add).then_inc(B["rot_sum"], 1)
                pool.wait_ge(B["rot_sum"], i * 8 + g + 1)
                pool.wait_ge(B["r_done"], i * 8 + g + 1)
                q = rq[:, g, :].rearrange("p (h e) -> p h e", h=HALF)
                pool.tensor_tensor(q, q, ss[:, g, :].unsqueeze(2).broadcast_to((P, HALF, DH)), ALU.mult
                                   ).then_inc(B["rot_done"], 1)

        @block.sync
        def _(sp):
            xin = a["x"].rearrange("b (t p) d -> p (b t) d", p=P)
            for dst, src in ((x[:, 0:T, :], xin[:, 0:T, :]), (w_big[:, :], a["w_qkv0"]), (ident[:, :], a["ident"]),
                             (cent[:, :], a["cent"]), (route[:, NE:2 * NE], a["w_route"])):
                sp.dma_start(dst, src).then_inc(first_in, 16)
            for dst, src in ((o[:, 0, 0:672], a["masks"]),
                             (w_o[:, :, :], a["w_o0"].rearrange("(c p) n -> p c n", p=P)),
                             (w_moe1[:, :], a["w_moe1"]), (w_moe2[:, :, :], a["w_moe2"].rearrange("(c p) n -> p c n", p=P)),
                             (b_moe1[:, :], a["b_moe1"]), (b_moe2[:, :], a["b_moe2"])):
                sp.dma_start(dst, src).then_inc(consts_in, 16)
            sp.dma_start(x[:, T:NB * T, :], xin[:, T:NB * T, :]).then_inc(xrest_in, 16)
            with nc.allow_non_contiguous_dma("small per-partition columns"):
                for dst, src in W2_LOADS():
                    sp.dma_start(dst, src).then_inc(w2_in, 16)
            def layer_weights(l):
                wq = a["w_qkv"][bass.ds(l, 1), :, :]
                wait(sp, B["proj"], l * NB * 8)
                sp.dma_start(w_big[:, 0:2 * INNER], wq[:, :, 0:2 * INNER].rearrange("a p n -> p (a n)")).then_inc(qk_in, 16)
                wait(sp, B["v_ps"], l * NB * 4)
                sp.dma_start(w_big[:, 2 * INNER:3 * INNER], wq[:, :, 2 * INNER:3 * INNER].rearrange("a p n -> p (a n)")
                             ).then_inc(v_in, 16)
                wait(sp, B["wo_done"], l * NB)
                sp.dma_start(w_o[:, :, :], a["w_o"][bass.ds(l, 1), :, :].rearrange("a (c p) n -> p (a c) n", p=P)
                             ).then_inc(o_in, 16)
                wait(sp, B["f_done"], l * NB)
                sp.dma_start(w_f1[:, :], a["w_f1"][bass.ds(l, 1), :, :].rearrange("a p n -> p (a n)")).then_inc(f_in, 16)
                for c, (f0, fn) in enumerate(FC):
                    sp.dma_start(w_f2[0:fn, c, :], a["w_f2"][bass.ds(l, 1), f0:f0 + fn, :].rearrange("a p n -> p (a n)")
                                 ).then_inc(f_in, 16)

            sp.wait_ge(A["wo_done"], NB * T)
            layer_weights(0)
            with sp.Fori(1, DEPTH) as l:
                layer_weights(l)
            sp.wait_ge(x_final, NB)
            sp.dma_start(out.rearrange("b (t p) d -> p (b t) d", p=P), x[:, :, :]).then_inc(out_done, 16)
            sp.wait_ge(out_done, 16)

        @block.gpsimd
        def _(pool):
            pool.memset(ones[:, :], 1.0).then_inc(prep, 1)
            pool.memset(xsh[:, :], 0.0).then_inc(prep, 1)
            pool.memset(xsf[:, :], 0.0).then_inc(prep, 1)
            pool.memset(eps_c[:, 0:1], EPS).then_inc(prep, 1)
            pool.memset(eps_c[:, 1:2], float(10 * np.log(2.0))).then_inc(prep, 1)
            with pool.Fori(0, NB) as u:
                for t in range(T):
                    pool.wait_ge(A["lg_done"], u + 1)
                    pool.wait_ge(A["moe_gelu"], u * T + t + 1)
                    pool.tensor_tensor(rb[:, t, :].rearrange("p (e n) -> p e n", e=NE),
                                       rb[:, t, :].rearrange("p (e n) -> p e n", e=NE),
                                       lg[:, t, 56:64].unsqueeze(2).broadcast_to((P, NE, DE)), ALU.mult
                                       ).then_inc(A["moe_gated"], 1)
            with pool.Fori(0, NB) as it:
                pool.wait_ge(C["flag_out"], it + 1)
                pool.wait_ge(C["y_out"], it * T + T)
                pool.wait_ge(C["dec1"], it + 1)
                pool.tensor_tensor(carrier[:, 1:2], eps_c[:, 0:1], eps_c[:, 0:1], ALU.add)
                bound = pool.value_load(flag1[0:1, 0:1].bitcast(I32))
                with pool.If(bound > int(np.float32(GUARD).view(np.int32))):
                    exact_scan(pool)
                pool.memset(flag1[0:1, 1:2], 0.0).then_inc(C["scan_ok"], 1)
            pool.wait_ge(A["state_done"], NB)
            pool.memset(prob[:, :, 256:352], 0.0).then_inc(prob_clear, 1)
            pool.memset(pt[:, :, 256 + WINDOW:384], 0.0).then_inc(prob_clear, 1)
            def rotary_tables(l):
                for k in range(4):
                    sc_ = qk_scale[:, bass.ds(l, 1), k // 2, :]
                    for t in range(T):
                        for lo, n, at in (((0, DH, 0),) if k % 2 == 0 else ((0, 32, 32), (32, 32, 0))):
                            pool.tensor_tensor(tabs[:, k, t, lo:lo + n].unsqueeze(1), rot[:, k, t, lo:lo + n].unsqueeze(1),
                                               sc_[:, :, at:at + n], ALU.mult).then_inc(tabs_done, 1)

            pool.wait_ge(w2_in, 16 * N_W2)
            rotary_tables(0)
            b_cur(pool, 0, first_layer=True)
            b_rotate(pool, 0)
            b_cur(pool, 1, first_layer=True)
            with pool.Fori(1, NB - 1) as i:
                b_rotate(pool, i)
                b_cur(pool, i + 1, first_layer=True)
                b_keep(pool, i - 1)
            b_rotate(pool, NB - 1)
            b_cur(pool, NB)
            b_keep(pool, NB - 2)
            with pool.Fori(1, DEPTH) as l:
                rotary_tables(l)
                with pool.Fori(0, NB) as b:
                    b_rotate(pool, l * NB + b)
                    b_cur(pool, l * NB + b + 1)
                    b_keep(pool, l * NB + b - 1)
            b_keep(pool, NU - 1)
            pool.wait_ge(B["state_done"], DEPTH * NB)
            for b in range(NB):
                pool.tensor_tensor(x[:, b * T:b * T + T, :], x[:, b * T:b * T + T, :], y[:, b * T:b * T + T, :],
                                   ALU.add).then_inc(x_final, 1)

        @block.tensor
        def _(pe):
            pe.wait_ge(prep_ok, 2)
            pe.wait_ge(first_in, 16 * N_FIRST)
            pe.transpose(tp[0][:, 0:NE], cent[:, :], ident[0:NE, 0:NE]).then_inc(prep_t, 1)
            pe.wait_ge(prep_ok, 3)
            pe.wait_ge(prep, 5)
            pe.wait_ge(consts_in, 16 * N_CONST)
            a_pe(pe, 0)
            a_pe(pe, 1)
            with pe.Fori(2, NB) as i:
                a_pe(pe, i)
            a_pe(pe, NB)
            pe.wait_ge(w2_in, 16 * N_W2)
            pe.wait_ge(A["state_done"], NB)
            def scan_unit(it):
                pe.wait_ge(C["xn_done"], it * T + T)
                wait(pe, C["yt_done"], it * T)
                for t in range(T):
                    m = pe.transpose(tp[0][:, P * t:P * t + P], xn[:, t, :], ident[:, :])
                m.then_inc(C["tr_x"], 1)
                pe.wait_ge(C["xt_done"], it + 1)
                wait(pe, C["x_done"], it)
                for t in range(T):
                    pe.matmul(pj[t][:, :], xt[:, P * t:P * t + P], w_in[:, 0:512], start=True, stop=True).then_inc(C["zx"], 1)
                    pe.matmul(tp[t][:, 256:256 + 132], xt[:, P * t:P * t + P], w_in[:, 512:644],
                              start=True, stop=True).then_inc(C["bcd"], 1)
                for n in range(2):
                    m = pe.matmul(sc[0][0:NS, S * n:S * n + S], w_in[:, 512 + NS * n:512 + NS * n + NS], xt[:, :],
                                  start=True, stop=True)
                m.then_inc(C["bct"], 1)
                pe.wait_ge(C["soft"], it + 1)
                pe.wait_ge(C["bcd_out"], it * T + T)
                pe.matmul(tp[0][:, 0:8], triu[:, :], dts[:, 8, :], start=True, stop=True)
                pe.matmul(tp[0][:, 8:16], ones[:, :], dts[:, 8, :], start=True, stop=True).then_inc(C["cums"], 1)
                pe.wait_ge(C["lb_done"], it + 1)
                for g in range(8):
                    m = pe.matmul(ov[g // 4][:, P * (g % 4):P * (g % 4) + P], c_lb[:, g, :], triu[:, :], start=True, stop=True)
                    if g % 4 == 3:
                        m.then_inc(C["lrow"], 1)
                pe.wait_ge(C["bct_out"], it + 1)
                for n, (s_, t_) in enumerate(((0, 0), (0, 1), (1, 1))):
                    m = pe.matmul(sc[1][:, P * n:P * n + P], c_bt[:, P * s_:P * s_ + P], c_ct[:, P * t_:P * t_ + P],
                                  start=True, stop=True)
                m.then_inc(C["g_ps"], 1)
                pe.wait_ge(C["dec_done"], it * 3 + 3)
                pe.wait_ge(C["sq_out"], it * T + T)
                pe.wait_ge(C["zx_out"], it * T + T)
                for h in range(SH):
                    pe.matmul(pj[0][:, P * h:P * h + P], c_dec[:, h, 0:P], c_sq[:, 0, h, :], start=True, stop=True)
                    pe.matmul(pj[1][:, P * h:P * h + P], c_dec[:, h, P:2 * P], c_sq[:, 0, h, :], start=True, stop=False)
                    m = pe.matmul(pj[1][:, P * h:P * h + P], c_dec[:, h, 2 * P:3 * P], c_sq[:, 1, h, :], start=False, stop=True)
                m.then_inc(C["guard_ps"], 1)
                pe.wait_ge(C["gm_done"], it + 1)
                for h in range(SH):
                    c = slice(64 * h, 64 * h + 64)
                    pe.matmul(ov[0][:, c], c_gm[:, h, 0:P], c_x[:, 0, c], start=True, stop=True)
                    pe.matmul(ov[1][:, c], c_gm[:, h, P:2 * P], c_x[:, 0, c], start=True, stop=False)
                    m = pe.matmul(ov[1][:, c], c_gm[:, h, 2 * P:3 * P], c_x[:, 1, c], start=False, stop=True)
                m.then_inc(C["y_ps"], 1)
                pe.wait_ge(C["gmx_done"], it + 1)
                pe.wait_ge(C["soft"], it + 1)
                pe.wait_ge(C["arg_done"], it * 8 + 8)
                pe.transpose(tp[0][0:1, 0:P], flag[:, 0:1], ident[:, :]).then_inc(C["flag_tr"], 1)
                pe.wait_ge(C["yn_done"], it * T + T)
                pe.wait_ge(C["flag_out"], it + 1)
                for t in range(T):
                    for c in range(2):
                        m = pe.transpose(tp[t][:, P * c:P * c + P], c_yn[:, t, P * c:P * c + P], ident[:, :])
                    m.then_inc(C["yn_tr"], 1)
                pe.wait_ge(C["yt_done"], it * T + T)
                for t in range(T):
                    for c in range(2):
                        m = pe.matmul(pj[0][:, D * t:D * t + D], c_yt[:, c, P * t:P * t + P], w_out[:, c, :],
                                      start=(c == 0), stop=(c == 1))
                m.then_inc(C["o_ps"], 1)

            scan_unit(0)
            with pe.Fori(1, NB) as it:
                scan_unit(it)
            pe.wait_ge(C["x_done"], NB)
            pe.wait_ge(prob_clear, 2)
            for i in range(4):
                b_pe(pe, i)
            with pe.Fori(4, NU) as i:
                b_pe(pe, i)
            for i in range(NU, NU + 3):
                b_pe(pe, i)

        @block.vector
        def _(dve):
            dve.wait_ge(first_in, 16 * N_FIRST)
            dve.wait_ge(consts_in, 16 * N_CONST)
            dve.tensor_copy(ident_bf[:, :], ident[:, :])
            dve.tensor_copy(causal_bf[:, :], o[:, 0, 0:384])
            dve.tensor_copy(local_bf[:, :], o[:, 0, 384:672]).then_inc(prep_ok, 1)
            dve.wait_ge(prep_t, 1)
            dve.tensor_copy(route[:, 0:NE], tp[0][:, 0:NE]).then_inc(prep_ok, 1)
            dve.wait_ge(first_in, 16 * N_FIRST)
            dve.wait_ge(xrest_in, 16)
            a_dve(dve, 0)
            a_dve(dve, 1)
            with dve.Fori(2, NB) as i:
                a_dve(dve, i)
            a_dve(dve, NB)
            dve.wait_ge(w2_in, 16 * N_W2)
            def scan_unit(it):
                link = chain(dve, C["dve_link"], it, 37)
                for t in range(T):
                    xs = x[:, bass.ds(it * T + t, 1), :].rearrange("p a n -> p (a n)")
                    stats(dve, link, xs, st[:, t, :], mv[:, t, :]).then_inc(C["mean0"], 1)
                for t in range(T):
                    xs = x[:, bass.ds(it * T + t, 1), :].rearrange("p a n -> p (a n)")
                    ys = y[:, bass.ds(it * T + t, 1), :].rearrange("p a n -> p (a n)")
                    dve.wait_ge(C["rstd0"], it * T + t + 1)
                    link(dve.tensor_scalar(ys, xs, mv[:, t, 0:1], sm[:, t, 0:1], ALU.subtract, ALU.mult))
                    dve.tensor_copy(carrier[:, 0:1], eps_c[:, 0:1])
                    stats(dve, link, ys, st[:, t, :], mv[:, t, :]).then_inc(C["mean1"], 1)
                for t in range(T):
                    ys = y[:, bass.ds(it * T + t, 1), :].rearrange("p a n -> p (a n)")
                    dve.wait_ge(C["rstd1"], it * T + t + 1)
                    dve.tensor_scalar(xn[:, t, :], ys, mv[:, t, 0:1], sm[:, t, 0:1], ALU.subtract, ALU.mult
                                      ).then_inc(C["xn_done"], 1)
                for t in range(T):
                    dve.wait_ge(C["bcd"], it * T + t + 1)
                    dve.tensor_copy(c_bcd[:, t, :], tp[t][:, 256:388]).then_inc(C["bcd_out"], 1)
                dve.wait_ge(C["bcd_out"], it * T + T)
                dve.tensor_tensor(dts[:, 0, :].rearrange("p (t h) -> p t h", t=T), c_bcd[:, :, 128:132],
                                  hp[:, 1, :].unsqueeze(1).broadcast_to((P, T, SH)), ALU.add).then_inc(C["dt_in"], 1)
                dve.wait_ge(C["dt_exp"], it + 1)
                d = [dts[:, i, :] for i in range(10)]
                link(dve.tensor_scalar(d[1], d[1], 1.0, None, ALU.min))
                link(dve.tensor_scalar(d[2], d[1], 2.0, None, ALU.add))
                link(dve.reciprocal(d[3], d[2]))
                link(dve.tensor_tensor(d[2], d[1], d[3], ALU.mult))
                link(dve.tensor_tensor(d[3], d[2], d[2], ALU.mult))
                link(dve.tensor_scalar(d[4], d[3], 2.0 / 7, 2.0 / 5, ALU.mult, ALU.add))
                link(dve.tensor_tensor(d[4], d[4], d[3], ALU.mult))
                link(dve.tensor_scalar(d[4], d[4], 2.0 / 3, None, ALU.add))
                link(dve.tensor_tensor(d[4], d[4], d[3], ALU.mult))
                link(dve.tensor_scalar(d[4], d[4], 2.0, None, ALU.add))
                link(dve.tensor_tensor(d[4], d[4], d[2], ALU.mult))
                link(dve.tensor_scalar(d[4], d[4], 0.001, 0.1, ALU.max, ALU.min))
                link(dve.tensor_tensor(d[5].rearrange("p (t h) -> p t h", t=T), d[4].rearrange("p (t h) -> p t h", t=T),
                                       neg_a[:, :].unsqueeze(1).broadcast_to((P, T, SH)), ALU.mult))
                dve.tensor_scalar(d[8], d[5], LN_CAP, None, ALU.min).then_inc(C["soft"], 1)
                dve.wait_ge(C["soft"], it + 1)
                dve.tensor_copy(c_lb[:, :, :], d[8].unsqueeze(2).broadcast_to((P, 8, P))).then_inc(C["lb_done"], 1)
                dve.wait_ge(C["cums"], it + 1)
                dve.tensor_copy(d[6], tp[0][:, 0:8])
                link(dve.tensor_copy(d[7], tp[0][:, 8:16]))
                link(dve.tensor_tensor(d[9], d[7], d[6], ALU.subtract))
                for g in range(8):
                    dve.wait_ge(C["lrow"], it * 2 + g // 4 + 1)
                    dve.scalar_tensor_tensor(c_arg[:, g, :], ov[g // 4][:, P * (g % 4):P * (g % 4) + P], dts[:, 6, g:g + 1],
                                             later[:, :], ALU.subtract, ALU.add).then_inc(C["arg_done"], 1)
                dve.wait_ge(C["g_ps"], it + 1)
                link(dve.tensor_copy(c_g, sc[1][:, 0:384]))
                dve.wait_ge(C["dec_done"], it * 3 + 3)
                dve.tensor_tensor(c_gm[:, :, :], c_dec[:, :, :], c_g.unsqueeze(1).broadcast_to((P, SH, 384)), ALU.mult
                                  ).then_inc(C["gm_done"], 1)
                dve.wait_ge(C["guard_ps"], it + 1)
                for t in range(T):
                    link(dve.tensor_reduce(gmx[:, t, 0:8], pj[t][:, :].rearrange("p (h n) -> p h n", n=64), AX.X, ALU.max))
                link(dve.tensor_tensor(gmx[:, :, 8:12], gmx[:, :, 0:8:2], gmx[:, :, 1:8:2], ALU.mult))
                dve.tensor_reduce(flag[:, 0:1], gmx[:, :, 8:12], AX.XY, ALU.max).then_inc(C["gmx_done"], 1)
                dve.wait_ge(C["flag_tr"], it + 1)
                wait(dve, C["scan_ok"], it)
                dve.tensor_reduce(flag1[0:1, 0:1], tp[0][0:1, 0:P], AX.X, ALU.max).then_inc(C["flag_out"], 1)
                dve.wait_ge(C["y_ps"], it + 1)
                for t in range(T):
                    dve.tensor_copy(c_y[:, t, :], ov[t][:, 0:DI]).then_inc(C["y_out"], 1)
                dve.wait_ge(C["zx_out"], it * T + T)
                for t in range(T):
                    dve.tensor_tensor(c_yn[:, t, :].rearrange("p (h n) -> p h n", h=SH),
                                      c_x[:, t, :].rearrange("p (h n) -> p h n", h=SH),
                                      hp[:, 2, :].unsqueeze(2).broadcast_to((P, SH, 64)), ALU.mult)
                dve.wait_ge(C["scan_ok"], it + 1)
                link(dve.tensor_copy(flag[:, 1:2], eps_c[:, 0:1]))
                link(dve.tensor_tensor(c_yn[:, :, :], c_yn[:, :, :], c_y[:, :, :], ALU.add))
                link(dve.tensor_tensor(c_yn[:, :, :], c_yn[:, :, :], c_sz[:, :, :], ALU.mult))
                for t in range(T):
                    stats(dve, link, c_yn[:, t, :], st[:, t, :], mv[:, t, :]).then_inc(C["mean2"], 1)
                for t in range(T):
                    dve.wait_ge(C["rstd2"], it * T + t + 1)
                    dve.tensor_scalar(c_yn[:, t, :], c_yn[:, t, :], mv[:, t, 0:1], sm[:, t, 0:1], ALU.subtract, ALU.mult
                                      ).then_inc(C["yn_done"], 1)
                dve.wait_ge(C["o_ps"], it + 1)
                link(dve.tensor_scalar(xn[:, :, :].rearrange("p t n -> p (t n)"), pj[0][:, 0:2 * D], 10.0, -10.0, ALU.min, ALU.max))
                for t in range(T):
                    stats(dve, link, xn[:, t, :], st[:, t, :], mv[:, t, :]).then_inc(C["mean3"], 1)
                for t in range(T):
                    dve.wait_ge(C["rstd3"], it * T + t + 1)
                    link(dve.tensor_scalar(xn[:, t, :], xn[:, t, :], mv[:, t, 0:1], sm[:, t, 0:1], ALU.subtract, ALU.mult))
                link(dve.tensor_tensor(xn[:, :, :], xn[:, :, :], now[:, 0, :].unsqueeze(1).broadcast_to((P, T, D)), ALU.mult))
                link(dve.tensor_tensor(xn[:, :, :], xn[:, :, :], now[:, 1, :].unsqueeze(1).broadcast_to((P, T, D)), ALU.add))
                xs = x[:, bass.ds(it * T, T), :]
                dve.tensor_tensor(xs, xs, xn[:, :, :], ALU.add).then_inc(C["x_done"], 1)
                assert link.n[0] == 37, link.n

            scan_unit(0)
            with dve.Fori(1, NB) as it:
                scan_unit(it)
            for i in range(4):
                b_dve(dve, i)
            with dve.Fori(4, NU) as i:
                b_dve(dve, i)
            for i in range(NU, NU + 3):
                b_dve(dve, i)

        @block.scalar
        def _(act):
            act.wait_ge(first_in, 16 * N_FIRST)
            act.wait_ge(prep, 5)
            act.activation(lg[0:NE, 0, 0:1], cent[:, 0:1], ACT.Copy).then_inc(prep_a, 1)
            act.wait_ge(prep_a, 1)
            act.activation(rb[0:NE, 0, 0:D], cent[:, :], ACT.Square, accum_out=eps_c[0:NE, 2:3]).then_inc(prep_a, 1)
            act.wait_ge(prep_a, 2)
            act.activation(eps_c[0:NE, 3:4], eps_c[0:NE, 2:3], ACT.Ln, scale=2.0 ** 20).then_inc(prep_a, 1)
            act.wait_ge(prep_a, 3)
            act.activation(eps_c[0:NE, 2:3], eps_c[0:NE, 3:4], ACT.Exp, scale=-0.5, bias=eps_c[0:NE, 1:2]).then_inc(prep_a, 1)
            act.wait_ge(prep_a, 4)
            act.activation(cent[:, :], cent[:, :], ACT.Copy, scale=eps_c[0:NE, 2:3]).then_inc(prep_ok, 1)
            a_act(act, 0)
            a_act(act, 1)
            with act.Fori(2, NB) as i:
                a_act(act, i)
            a_act(act, NB)
            act.wait_ge(w2_in, 16 * N_W2)
            act.activation(neg_a[:, :], hp[:, 0, :], ACT.Exp).then_inc(prep_a, 1)
            act.wait_ge(prep_a, 5)
            act.activation(neg_a[:, :], neg_a[:, :], ACT.Copy, scale=-1.0).then_inc(prep_ok, 1)
            def scan_unit(it):
                link = chain(act, C["act_link"], it, 8)
                act.preload_act_table_set("natural_log_exp_and_others")
                for mean, done in ((C["mean0"], C["rstd0"]), (C["mean1"], C["rstd1"])):
                    for t in range(T):
                        act.wait_ge(mean, it * T + t + 1)
                        rstd(act, link, mv[:, t, :], sm[:, t, 0:2]).then_inc(done, 1)
                act.wait_ge(C["tr_x"], it + 1)
                act.activation(xt[:, :], tp[0][:, 0:S], ACT.Identity, scale=ni[:, 0:1], bias=ni[:, 1:2]).then_inc(C["xt_done"], 1)
                for t in range(T):
                    act.wait_ge(C["zx"], it * T + t + 1)
                    act.activation(c_x[:, t, :], pj[t][:, 256:512], ACT.Copy)
                    act.activation(c_sq[:, t, :, 0:64], pj[t][:, 256:512].rearrange("p (h n) -> p h n", h=SH), ACT.Square)
                    act.activation(c_sz[:, t, :], pj[t][:, 0:256], ACT.Silu).then_inc(C["zx_out"], 1)
                act.preload_act_table_set("natural_log_exp_and_others")
                act.wait_ge(C["bct"], it + 1)
                act.activation(c_bt, sc[0][0:NS, 0:S], ACT.Copy)
                act.activation(c_ct, sc[0][0:NS, S:2 * S], ACT.Copy).then_inc(C["bct_out"], 1)
                act.wait_ge(C["dt_in"], it + 1)
                act.activation(dts[:, 1, :], dts[:, 0, :], ACT.Exp).then_inc(C["dt_exp"], 1)
                for t in range(T):
                    act.wait_ge(C["bcd_out"], it * T + T)
                    act.activation(c_sq[:, t, :, 64:128], c_bcd[:, t, 0:NS].unsqueeze(1).broadcast_to((P, SH, NS)), ACT.Square
                                   ).then_inc(C["sq_out"], 1)
                act.wait_ge(C["soft"], it + 1)
                act.activation(dec_all[:, :], dts[:, 8, :], ACT.Exp).then_inc(C["dec1"], 1)
                act.wait_ge(C["arg_done"], it * 8 + 8)
                act.activation(c_dec[:, :, 0:P], c_arg[:, 0:4, :], ACT.Exp).then_inc(C["dec_done"], 1)
                act.activation(c_dec[:, :, 2 * P:3 * P], c_arg[:, 4:8, :], ACT.Exp).then_inc(C["dec_done"], 1)
                for h in range(SH):
                    m = act.activation(c_dec[:, h, P:2 * P], ov[1][:, P * h:P * h + P], ACT.Exp, bias=dts[:, 9, h:h + 1])
                m.then_inc(C["dec_done"], 1)
                for t in range(T):
                    act.wait_ge(C["mean2"], it * T + t + 1)
                    rstd(act, link, mv[:, t, :], sm[:, t, 0:2]).then_inc(C["rstd2"], 1)
                for t in range(T):
                    act.wait_ge(C["yn_tr"], it * T + t + 1)
                    for c in range(2):
                        m = act.activation(c_yt[:, c, P * t:P * t + P], tp[t][:, P * c:P * c + P], ACT.Identity,
                                           scale=lnw[:, c, 0:1], bias=lnw[:, c, 1:2])
                    m.then_inc(C["yt_done"], 1)
                for t in range(T):
                    act.wait_ge(C["mean3"], it * T + t + 1)
                    rstd(act, link, mv[:, t, :], sm[:, t, 0:2]).then_inc(C["rstd3"], 1)
                assert link.n[0] == 8, link.n

            scan_unit(0)
            with act.Fori(1, NB) as it:
                scan_unit(it)
            for i in range(4):
                b_act(act, i)
            with act.Fori(4, NU) as i:
                b_act(act, i)
            for i in range(NU, NU + 3):
                b_act(act, i)


def host_constants():
    i = np.arange(S)
    causal = np.where(i[None, :] <= i[:, None], 0.0, MASKED)
    near = np.where((i[None, :] <= i[:, None]) & (i[None, :] >= i[:, None] - WINDOW), 0.0, MASKED)

    def pack(m, span):
        return np.concatenate([m[P * t:P * t + P, k0:k0 + kn] for t, (k0, kn) in enumerate(span)], 1)

    half = np.arange(0, DH, 2, dtype=np.float32)
    freqs = i[:, None].astype(np.float32) * (1.0 / 10000.0 ** (half / DH)).astype(np.float32)[None, :]
    freqs = np.concatenate([freqs, freqs], -1)
    power = (i.astype(np.float32) - S // 2) / (WINDOW // 2)
    scale = (((half + 0.4 * DH) / (1.4 * DH))[None, :] ** power[:, None]).astype(np.float32)
    scale = np.concatenate([scale, scale], -1)
    cos, sin = np.cos(freqs), np.sin(freqs)
    sin = np.concatenate([-sin[:, :DH // 2], sin[:, DH // 2:]], -1)
    rot = np.stack([8 * cos * scale, 8 * sin * scale, cos / scale, sin / scale]).astype(np.float32)
    r = np.arange(P)
    return {
        "ident": np.eye(P, dtype=np.float32),
        "masks": np.concatenate([pack(causal, CAUSAL), pack(near, LOCAL)], 1).astype(np.float32),
        "triu": (r[:, None] <= r[None, :]).astype(np.float32),
        "later": np.where(r[None, :] >= r[:, None], 0.0, MASKED).astype(np.float32),
        "rot": rot,
    }


def layouts(i):
    t = np.ascontiguousarray
    g = {k: np.asarray(v) for k, v in i.items()}
    return {
        "x": g["L0_attn_x"],
        "w_qkv0": t(np.concatenate([g[k].reshape(INNER, D).T for k in ("L0_attn_wq", "L0_attn_wk", "L0_attn_wv")], 1)),
        "w_o0": t(g["L0_attn_wo"].T),
        "cent": g["L0_ffn_centroids"],
        "w_route": t(g["L0_ffn_w_route"].T),
        "w_moe1": t(g["L0_ffn_w1"].transpose(1, 0, 2).reshape(D, EH)),
        "w_moe2": g["L0_ffn_w2"].reshape(EH, D),
        "b_moe1": g["L0_ffn_b1"].reshape(1, EH),
        "b_moe2": g["L0_ffn_b2"],
        "w_in": t(g["L1_attn_in_proj_w"].T),
        "w_out": t(g["L1_attn_out_proj_w"].T),
        "ni_w": g["L1_attn_ni_w"], "ni_b": g["L1_attn_ni_b"],
        "ln_w": g["L1_attn_ln_w"], "ln_b": g["L1_attn_ln_b"],
        "no_w": g["L1_attn_no_w"], "no_b": g["L1_attn_no_b"],
        "A_log": g["L1_attn_A_log"], "dt_bias": g["L1_attn_dt_bias"], "Dparam": g["L1_attn_Dparam"],
        "w_qkv": g["L1_ffn_Wqkv"], "w_o": g["L1_ffn_Wo"],
        "q_scale": g["L1_ffn_q_scale"], "k_scale": g["L1_ffn_k_scale"],
        "f_g": t(g["L1_ffn_ln_g"].T), "f_b": t(g["L1_ffn_ln_b"].T),
        "w_f1": g["L1_ffn_W1"], "w_f2": g["L1_ffn_W2"],
        "b_f1": t(g["L1_ffn_b1"].T), "b_f2": g["L1_ffn_b2"],
    }


def kernel(**inputs):
    import concourse.bacc as bacc
    from concourse.bass_utils import run_bass_kernel_spmd

    arrays = {**layouts(inputs), **host_constants()}
    nc = bacc.Bacc("TRN2", target_bir_lowering=False, num_devices=1)
    a = {n: nc.dram_tensor("in_" + n, v.shape, mybir.dt.from_np(v.dtype), kind="ExternalInput").ap()
         for n, v in arrays.items()}
    out = nc.dram_tensor("out_x", (NB, S, D), F32, kind="ExternalOutput").ap()
    program(nc, a, out)
    r = run_bass_kernel_spmd(nc, [{"in_" + n: v for n, v in arrays.items()}], core_ids=[0])
    return r.results[0]["out_x"]
```

```python
from contextlib import ExitStack

import numpy as np

import concourse.bass as bass
from concourse import mybir

F32 = mybir.dt.float32
BF16 = mybir.dt.bfloat16
I32 = mybir.dt.int32
ALU = mybir.AluOpType
ACT = mybir.ActivationFunctionType
AX = mybir.AxisListType

P = 128
D = 128
NB = 16
S = 256
T = S // P
H = 16
DH = 64
INNER = H * DH
HALF = 8
NE = 8
DE = 64
EH = NE * DE
DEPTH = 6
WINDOW = 32
FI = int(D * 4 * 2 / 3)
FC = [(0, 128), (128, 128), (256, FI - 256)]
SH = 4
DI = SH * 64
NS = 64
EPS = 1e-5
LN_CAP = float(np.log(0.99))
GUARD = 95.0
STEPS = 16
MASKED = -1e30

CAUSAL = [(0, 128), (0, 256)]
LOCAL = [(0, 128), (96, 160)]


def program(nc, a, out):
    ctx = ExitStack()
    with ctx:
        def sb(name, shape, dt=F32):
            return ctx.enter_context(nc.sbuf_tensor(name, shape, dt))

        def sem(name):
            return ctx.enter_context(nc.semaphore(name))

        bank = {n: ctx.enter_context(nc.psum_tensor(n, [P, 512], F32))
                for n in ("pj0", "pj1", "tp0", "tp1", "sc0", "sc1", "ov0", "ov1")}
        pj = [bank["pj0"], bank["pj1"]]
        tp = [bank["tp0"], bank["tp1"]]
        sc = [bank["sc0"], bank["sc1"]]
        ov = [bank["ov0"], bank["ov1"]]

        x = sb("x", [P, NB * T, D])
        y = sb("y", [P, NB * T, D])
        ident = sb("ident", [P, P])
        ident_bf = sb("ident_bf", [P, P], BF16)
        causal_bf = sb("causal_bf", [P, 384], BF16)
        local_bf = sb("local_bf", [P, 288], BF16)
        triu = sb("triu", [P, P])
        later = sb("later", [P, P])
        ones = sb("ones", [P, P])
        rot = sb("rot", [P, 4, T, DH])
        w_big = sb("w_big", [P, 3 * INNER])
        w_o = sb("w_o", [P, 8, D])
        w_moe1 = sb("w_moe1", [P, EH])
        w_moe2 = sb("w_moe2", [P, 4, D])
        b_moe1 = sb("b_moe1", [1, EH])
        b_moe2 = sb("b_moe2", [NE, D])
        route = sb("route", [P, 2 * NE])
        cent = sb("cent", [NE, D])
        w_in = sb("w_in", [P, 2 * DI + 2 * NS + SH])
        w_out = sb("w_out", [P, 2, D])
        ni = sb("ni", [P, 2])
        lnw = sb("lnw", [P, 2, 2])
        now = sb("now", [P, 2, D])
        hp = sb("hp", [P, 3, SH])
        neg_a = sb("neg_a", [P, SH])
        qk_scale = sb("qk_scale", [P, DEPTH, 2, DH])
        ln_gb = sb("ln_gb", [P, DEPTH, 2])
        w_f1 = sb("w_f1", [P, 2 * FI])
        w_f2 = sb("w_f2", [P, 3, D])
        b_f1 = sb("b_f1", [P, DEPTH, 6])
        b_f2 = sb("b_f2", [P, DEPTH, D])
        tabs = sb("tabs", [P, 4, T, DH])
        cur = sb("cur", [P, T, D])
        mid = sb("mid", [P, T, D])
        xn = sb("xn", [P, T, D])
        xn2 = sb("xn2", [P, T, D])
        xt = sb("xt", [P, S])
        xt2 = sb("xt2", [P, S])
        qt = sb("qt", [P, H // 2, S])
        kt = sb("kt", [P, H // 2, S])
        v = sb("v", [P, T, INNER])
        sq = sb("sq", [P, 2, 512])
        rq = sb("rq", [P, 8, 512])
        rb = sb("rb", [P, 2, 512])
        ss = sb("ss", [P, 2 * T * 2, HALF])
        prob = sb("prob", [P, 2, 512])
        pt = sb("pt", [P, 2, 384])
        nm = sb("nm", [P, H, T])
        rs = sb("rs", [P, T, H])
        rinv = sb("rinv", [P, T, H])
        o = sb("o", [P, T, INNER])
        ot = sb("ot", [P, 8, S])
        hid = sb("hid", [P, 3, S])
        raw = sb("raw", [P, 2, 512])
        xm = sb("xm", [P, T, D])
        hsb = sb("hsb", [P, 3, 2 * S])
        gel = sb("gel", [P, 3, S])
        st = sb("st", [P, T, 6])
        mv = sb("mv", [P, T, 2])
        sm = sb("sm", [P, T, 8])
        lg = sb("lg", [P, T, 8 * 8])
        gate_t = sb("gate_t", [NE, S])
        qts, kts = [qt, sb("qt_odd", [P, H // 2, S])], [kt, sb("kt_odd", [P, H // 2, S])]
        xsh = sb("xsh", [P, S])
        vs, xshs = [v, sb("v_odd", [P, T, INNER])], [xsh, sb("xsh_odd", [P, S])]

        def flat(b):
            return b[:, :, :].rearrange("p t n -> p (t n)")

        o2 = o[:, :, :].rearrange("p t n -> p (t n)")
        v2 = v[:, :, :].rearrange("p t n -> p (t n)")
        qt2 = qt[:, :, :].rearrange("p t n -> p (t n)")
        kt2 = kt[:, :, :].rearrange("p t n -> p (t n)")
        rq2 = rq[:, :, :].rearrange("p t n -> p (t n)")
        ot2 = ot[:, :, :].rearrange("p t n -> p (t n)")
        c_y = ot2[:, 0:512].rearrange("p (t n) -> p t n", t=T)
        c_yn = ot2[:, 512:1024].rearrange("p (t n) -> p t n", t=T)
        c_sz, c_x, c_sq, c_bcd, c_dec, c_gm = [], [], [], [], [], []
        for par, (flat_dec, flat_gm) in enumerate(((qt2, kt2), (flat(qts[1]), flat(kts[1])))):
            c_sz.append(o2[:, 1024 * par:1024 * par + 512].rearrange("p (t n) -> p t n", t=T))
            c_x.append(o2[:, 1024 * par + 512:1024 * par + 1024].rearrange("p (t n) -> p t n", t=T))
            flat_sq = (v2, flat(hsb))[par]
            c_sq.append(flat_sq[:, 0:1024].rearrange("p (t h n) -> p t h n", t=T, h=SH))
            c_bcd.append(flat_sq[:, 1024:1024 + T * 132].rearrange("p (t n) -> p t n", t=T))
            c_dec.append(flat_dec[:, 0:1536].rearrange("p (h n) -> p h n", h=SH))
            c_gm.append(flat_gm[:, 0:1536].rearrange("p (h n) -> p h n", h=SH))
        c_bt = v2[0:NS, 1536:1792]
        c_ct = v2[0:NS, 1792:2048]
        c_lb = rq2[:, 0:1024].rearrange("p (g n) -> p g n", g=8)
        c_arg = rq2[:, 1024:2048].rearrange("p (g n) -> p g n", g=8)
        c_g = rq2[:, 2048:2432]
        c_yt = rq2[:, 2560:3072].rearrange("p (c n) -> p c n", c=2)
        st_b, mv_b, sm_b = sb("st_b", [P, T, 6]), sb("mv_b", [P, T, 2]), sb("sm_b", [P, T, 2])
        dts = sb("dts", [P, 10, 8])
        dec_all = [sb("dec_even", [P, 2 * SH]), sb("dec_odd", [P, 2 * SH])]
        gmx = sb("gmx", [P, T, 12])
        flag = sb("flag", [P, 2])
        flag1 = sb("flag1", [1, 2])
        eps_c = sb("eps_c", [P, 4])
        xsf = sb("xsf", [P, S])
        carrier = sb("carrier", [P, 2])
        e_bc = vs[1][:, :, :].rearrange("p t n -> p (t n)").rearrange("p (s n) -> p s n", s=STEPS)
        e_dec = sb("e_dec", [P, STEPS, 2])
        e_x = sb("e_x", [P, 2, STEPS])
        e_y = sb("e_y", [P, 2, STEPS])
        e_h = sb("e_h", [P, 2, NS])
        e_t = sb("e_t", [P, NS])
        d_bcd = nc.dram_tensor("scratch_bcd", (S, 132), F32).ap()
        d_dec = nc.dram_tensor("scratch_dec", (S, SH), F32).ap()
        d_x = nc.dram_tensor("scratch_x", (S, DI), F32).ap()
        d_y = nc.dram_tensor("scratch_y", (S, DI), F32).ap()

        first_in, consts_in, w2_in, xrest_in = sem("first_in"), sem("consts_in"), sem("w2_in"), sem("xrest_in")
        qk_in, qk2_in, v_in, o_in, f_in = sem("qk_in"), sem("qk2_in"), sem("v_in"), sem("o_in"), sem("f_in")
        out_done = sem("out_done")
        tabs_done = sem("tabs_done")
        prep, prep_t, prep_ok = sem("prep"), sem("prep_t"), sem("prep_ok")
        slow = sem("slow")
        x_final = sem("x_final")

        def signals(prefix, names):
            return {n: sem(prefix + n) for n in names.split()}

        core = "scores max_done exp_done pt_tr pt_done pv_done o_done o_tr ot_done wo_done state_done "
        A = signals("a_", core + "mean_done xnorm_done xn_done tr_x xt_done xt_now qkt_done qk_done qk_moved tr_v v_done "
                    "route_ps sumsq_in sumsq gate_in gate_exp lg_done gate_tr gatet_done moe_h moe_gelu moe_gated moe_tr "
                    "moet_done link_p link_a alink_p")
        C = signals("c_", "mean0 rstd0 mean1 rstd1 mean2 rstd2 mean3 rstd3 xn_done tr_x xt_done zx bcd bct zx_out bcd_out "
                    "bct_out sq_out dt_in dt_exp soft lb_done cums lrow arg_done dec1 dec_done g_ps gm_done guard_ps "
                    "gmx_done flag_tr flag_out scan_ok y_ps y_out yn_done yn_tr yt_done o_ps x_done link_f link_b alink_f alink_b")
        B = signals("b_", core + "cur_in tr_x xt_done proj sq_done ssq_done ssum_done raw_done r_done rot_cos rot_sin rot_sum rot_done "
                    "qkt_ready qkt_done v_ps v_done mid_done mid_kept mid_tr midt_done back_tr back_out mean rstd xn2_done xn2_tr xt2_done "
                    "hid_ps hid_out hid_gelu hid_done f_done link_a link_n link_f alink_p alink_7 alink_f")
        prep_a, slow_dma, prob_clear = sem("prep_a"), sem("slow_dma"), sem("prob_clear")

        block = ctx.enter_context(nc.Block())

        def W2_LOADS():
            yield triu[:, :], a["triu"]
            yield later[:, :], a["later"]
            yield rot[:, :, :, :], a["rot"].rearrange("k (t p) e -> p k t e", p=P)
            yield w_in[:, :], a["w_in"]
            yield w_out[:, :, :], a["w_out"].rearrange("(c p) n -> p c n", p=P)
            yield ni[:, 0:1], a["ni_w"].rearrange("(p a) -> p a", a=1)
            yield ni[:, 1:2], a["ni_b"].rearrange("(p a) -> p a", a=1)
            yield lnw[:, :, 0], a["ln_w"].rearrange("(c p) -> p c", p=P)
            yield lnw[:, :, 1], a["ln_b"].rearrange("(c p) -> p c", p=P)
            yield now[:, 0, :], a["no_w"].rearrange("(a n) -> a n", a=1).broadcast_to((P, D))
            yield now[:, 1, :], a["no_b"].rearrange("(a n) -> a n", a=1).broadcast_to((P, D))
            for n, k in enumerate(("A_log", "dt_bias", "Dparam")):
                yield hp[:, n, :], a[k].rearrange("(a n) -> a n", a=1).broadcast_to((P, SH))
            for n, k in enumerate(("q_scale", "k_scale")):
                yield qk_scale[:, :, n, :], a[k].rearrange("(a l) e -> a l e", a=1).broadcast_to((P, DEPTH, DH))
            yield ln_gb[:, :, 0], a["f_g"]
            yield ln_gb[:, :, 1], a["f_b"]
            for c in range(6):
                f0, fn = FC[c % 3]
                f0 += FI * (c // 3)
                yield b_f1[0:fn, :, c], a["b_f1"][f0:f0 + fn, :]
            yield b_f2[:, :, :], a["b_f2"].rearrange("(a l) n -> a l n", a=1).broadcast_to((P, DEPTH, D))
        N_W2 = len(list(W2_LOADS()))
        N_CONST, N_FIRST = 6, 5

        N_TABS = 2 + 2 * 2

        def exact_scan(pool, par):
            with nc.allow_non_contiguous_dma("rare path"):
                def moved(ins):
                    ins.then_inc(slow_dma, 16)
                    pool.wait_ge(slow_dma, 16)
                    pool.dma_reset(range(slow_dma.num, slow_dma.num + 1))
                    pool.sem_clear(slow_dma)

                def did(ins):
                    ins.then_inc(slow, 1)
                    pool.wait_ge(slow, 1)
                    pool.sem_clear(slow)

                for t in range(T):
                    moved(pool.dma_start(d_bcd[P * t:P * t + P, :], c_bcd[par][:, t, :]))
                    moved(pool.dma_start(d_dec[P * t:P * t + P, :], dec_all[par][:, SH * t:SH * t + SH]))
                    moved(pool.dma_start(d_x[P * t:P * t + P, :], c_x[par][:, t, :]))
                did(pool.memset(e_h[:, :, :], 0.0))
                with pool.Fori(0, S // STEPS) as n:
                    at = n * STEPS
                    for i in range(STEPS):
                        moved(pool.dma_start(e_bc[:, i:i + 1, :],
                                             d_bcd[bass.ds(at + i, 1), 0:2 * NS].unsqueeze(0).broadcast_to((P, 1, 2 * NS))))
                    for hh in range(2):
                        for e in range(2):
                            h = 2 * hh + e
                            moved(pool.dma_start(e_dec[64 * e:64 * e + 64, :, hh],
                                                 d_dec[bass.ds(at, STEPS), h].unsqueeze(0).broadcast_to((64, STEPS))))
                        moved(pool.dma_start(e_x[:, hh, :], d_x[bass.ds(at, STEPS), P * hh:P * hh + P].rearrange("s p -> p s")))
                    for i in range(STEPS):
                        for hh in range(2):
                            hs = e_h[:, hh, :]
                            did(pool.tensor_scalar(e_t[:, :], e_bc[:, i, 0:NS], e_x[:, hh, i:i + 1], None, ALU.mult))
                            did(pool.tensor_scalar(hs, hs, e_dec[:, i, hh:hh + 1], None, ALU.mult))
                            did(pool.tensor_tensor(hs, hs, e_t[:, :], ALU.add))
                            did(pool.tensor_scalar(hs, hs, -10.0, 10.0, ALU.max, ALU.min))
                            did(pool.tensor_tensor(e_t[:, :], hs, e_bc[:, i, NS:2 * NS], ALU.mult))
                            w = NS // 2
                            while w >= 1:
                                dst = e_t[:, 0:w] if w > 1 else e_y[:, hh, i:i + 1]
                                did(pool.tensor_tensor(dst, e_t[:, 0:w], e_t[:, w:2 * w], ALU.add))
                                w //= 2
                    for hh in range(2):
                        moved(pool.dma_start(d_y[bass.ds(at, STEPS), P * hh:P * hh + P].rearrange("s p -> p s"), e_y[:, hh, :]))
                for t in range(T):
                    moved(pool.dma_start(c_y[:, t, :], d_y[P * t:P * t + P, :]))
        def wait(eng, s, n):
            if not isinstance(n, int) or n > 0:
                eng.wait_ge(s, n)

        def chain(eng, s, it, per):
            n = [0]

            def link(ins):
                n[0] += 1
                ins.then_inc(s, 1)
                eng.wait_ge(s, it * per + n[0])
                return ins
            link.n, link.sem, link.it = n, s, it
            link.per = per
            return link

        def tile_cols(span):
            return [(0, span[0][1]), (span[0][1], span[0][1] + span[1][1])]

        def pe_scores(pe, G, u, h, span, mask, q_t, k_t):
            cols = tile_cols(span)
            b = DH * (h % 2)
            wait(pe, G["exp_done"], after(u * H, h - 1))
            pe.matmul(sc[h % 2][:, 0:cols[1][1]], ident_bf[:, :], mask[:, :], start=True, stop=False)
            for t in range(T):
                k0, kn = span[t]
                m = pe.matmul(sc[h % 2][:, cols[t][0]:cols[t][1]], q_t[b:b + DH, h // 2, P * t:P * t + P],
                              k_t[b:b + DH, h // 2, k0:k0 + kn], start=False, stop=(t == T - 1))
            m.then_inc(G["scores"], 1)

        def pe_turn(pe, G, u, h, span):
            pe.wait_ge(G["exp_done"], u * H + h + 1)
            wait(pe, G["pt_done"], after(u * H, h - 1))
            q = prob[:, h % 2, :]
            pe.transpose(tp[h % 2][:, 0:128], q[:, 0:128], ident[:, :])
            pe.transpose(tp[h % 2][:, 128:256], q[:, 384:512], ident[:, :])
            if span is LOCAL:
                m = pe.transpose(tp[h % 2][:, 256:256 + WINDOW], q[0:WINDOW, 256:384], ident[0:WINDOW, 0:WINDOW])
            else:
                m = pe.transpose(tp[h % 2][:, 256:384], q[:, 256:384], ident[:, :])
            m.then_inc(G["pt_tr"], 1)

        def pe_weigh(pe, G, u, h, vals):
            pe.wait_ge(G["pt_done"], u * H + h + 1)
            if h % HALF == 0:
                wait(pe, G["o_done"], u * 2 + h // HALF)
            q = pt[:, h % 2, :]
            c = DH * (h % HALF)
            vv = [vals[:, t, h * DH:h * DH + DH] for t in range(T)]
            pe.matmul(ov[0][:, c:c + DH], q[:, 0:128], vv[0], start=True, stop=True)
            pe.matmul(ov[1][:, c:c + DH], q[:, 128:256], vv[1], start=True, stop=False)
            pe.matmul(ov[1][:, c:c + DH], q[:, 256:384], vv[0], start=False, stop=True).then_inc(G["pv_done"], 1)

        def dve_top(dve, G, u, h, span):
            cols = tile_cols(span)
            dve.wait_ge(G["scores"], u * H + h + 1)
            for t in range(T):
                m = dve.tensor_reduce(nm[:, h, t:t + 1], sc[h % 2][:, cols[t][0]:cols[t][1]], AX.X, ALU.max, negate=True)
            m.then_inc(G["max_done"], 1)

        def act_exp(act, G, u, h, span):
            cols = tile_cols(span)
            act.wait_ge(G["max_done"], u * H + h + 1)
            wait(act, G["pt_tr"], after(u * H, h - 1))
            for t in range(T):
                n = span[t][1]
                at = [0, 512 - n][t]
                m = act.activation(prob[:, h % 2, at:at + n], sc[h % 2][:, cols[t][0]:cols[t][1]], ACT.Exp,
                                   bias=nm[:, h, t:t + 1], accum_out=rs[:, t, h:h + 1])
            m.then_inc(G["exp_done"], 1)

        def after(heads, n):
            return heads + n if not isinstance(heads, int) else max(heads + n, 0)

        def pe_heads(pe, G, u, span, mask, extra):
            for h in range(H):
                pe_turn(pe, G, u, h, span)
                if h + 2 < H:
                    pe_scores(pe, G, u, h + 2, span, mask, qt, kt)
                if h > 0:
                    pe_weigh(pe, G, u, h - 1, v)
                extra(h)
            pe_weigh(pe, G, u, H - 1, v)

        def pe_turn_out(pe, G, u):
            for g in range(4):
                t, hf = g // 2, g % 2
                if g == 0:
                    pe.wait_ge(G["o_done"], u * 2 + 2)
                    pe.wait_ge(G["pt_done"], u * H + H)
                if g >= 2:
                    pe.wait_ge(G["ot_done"], u * 4 + g - 1)
                for j in range(4):
                    m = pe.transpose(tp[g % 2][:, 128 * j:128 * j + 128],
                                     o[:, t, 512 * hf + 128 * j:512 * hf + 128 * j + 128], ident[:, :])
                m.then_inc(G["o_tr"], 1)

        def on_dve(h):
            return h % 4 != 1

        def pt_copy(eng, G, u, h, span, copy):
            n = 256 + (WINDOW if span is LOCAL else P)
            eng.wait_ge(G["pt_tr"], u * H + h + 1)
            wait(eng, G["pv_done"], after(u * H, h - 1))
            wait(eng, G["pt_done"], u * H + h)
            copy(pt[:, h % 2, 0:n], tp[h % 2][:, 0:n]).then_inc(G["pt_done"], 1)

        def dve_heads(dve, G, u, span, link, extra):
            dve_top(dve, G, u, 0, span)
            dve_top(dve, G, u, 1, span)
            for h in range(H):
                if on_dve(h):
                    pt_copy(dve, G, u, h, span, dve.tensor_copy)
                if h + 2 < H:
                    dve_top(dve, G, u, h + 2, span)
                if h == HALF:
                    dve_norm(dve, G, u, 0, link)
                extra(h)

        def dve_norm(dve, G, u, hf, link):
            dve.wait_ge(G["pv_done"], u * H + HALF * (hf + 1))
            link(dve.reciprocal(rinv[:, :, HALF * hf:HALF * hf + HALF], rs[:, :, HALF * hf:HALF * hf + HALF]))
            for t in range(T):
                m = dve.tensor_tensor(
                    o[:, t, 512 * hf:512 * hf + 512].rearrange("p (h e) -> p h e", h=HALF),
                    ov[t][:, :].rearrange("p (h e) -> p h e", h=HALF),
                    rinv[:, t, HALF * hf:HALF * hf + HALF].unsqueeze(2).broadcast_to((P, HALF, DH)), ALU.mult)
            m.then_inc(G["o_done"], 1)

        def out_copy(eng, G, u, g, copy):
            eng.wait_ge(G["o_tr"], u * 4 + g + 1)
            wait(eng, G["ot_done"], u * 4 + g)
            t, hf = g // 2, g % 2
            copy(ot[:, 4 * hf:4 * hf + 4, P * t:P * t + P],
                 tp[g % 2][:, :].rearrange("p (c n) -> p c n", c=4)).then_inc(G["ot_done"], 1)

        def act_heads(act, G, u, span, extra):
            act_exp(act, G, u, 0, span)
            act_exp(act, G, u, 1, span)
            for h in range(H):
                if not on_dve(h):
                    pt_copy(act, G, u, h, span, lambda o_, i_: act.activation(o_, i_, ACT.Copy))
                if h + 2 < H:
                    act_exp(act, G, u, h + 2, span)
                extra(h)

        def stats(dve, link, src, s, m_v):
            dve.bn_stats(s, src).then_inc(link.sem, 1)
            link.n[0] += 1
            dve.wait_ge(link.sem, link.it * link.per + link.n[0])
            dve.tensor_copy(carrier[:, 0:1], eps_c[:, 0:1])
            return dve.bn_aggr(m_v, s)

        def rstd(act, link, m_v, r):
            link(act.activation(r[:, 1:2], m_v[:, 1:2], ACT.Ln, bias=eps_c[:, 0:1]))
            return act.activation(r[:, 0:1], r[:, 1:2], ACT.Exp, scale=-0.5)

        def a_stages(i):
            known = isinstance(i, int)
            return (not known or i < NB), (not known or 0 < i <= NB), (not known or i > 1)

        A_PAIR = [5, 6, 7, 8, 9, 10, 11, 12]

        def a_pe(pe, i):
            new, old, last = a_stages(i)
            u, w = i - 1, i - 2
            if old:
                pe.wait_ge(A["xt_now"], u + 1)
                for g in range(4):
                    t, c = g // 2, g % 2
                    if g == 1:
                        pe.wait_ge(A["qk_done"], u * 8 + 8)
                    if g >= 2:
                        pe.wait_ge(A["v_done"], u * 4 + g - 1)
                    pe.matmul(pj[g % 2][:, :], xt[:, P * t:P * t + P],
                              w_big[:, 2 * INNER + 512 * c:2 * INNER + 512 * c + 512], start=True, stop=True
                              ).then_inc(A["tr_v"], 1)
            if last:
                pe_turn_out(pe, A, w)
            if old:
                wait(pe, A["o_done"], u * 2)
                for t in range(T):
                    m = pe.matmul(ov[1][:, 16 * t:16 * t + 16], xt[:, P * t:P * t + P], route[:, :], start=True, stop=True)
                m.then_inc(A["route_ps"], 1)
                for t in range(T):
                    pe.wait_ge(A["v_done"], u * 4 + 3 + t)
                    pe.matmul(pj[t][:, :], xt[:, P * t:P * t + P], w_moe1[:, :], start=True, stop=False)
                    pe.matmul(pj[t][:, :], ones[0:1, :], b_moe1[:, :], start=False, stop=True).then_inc(A["moe_h"], 1)
                pe.wait_ge(A["qk_moved"], u * 2 + 2)
                pe_scores(pe, A, u, 0, CAUSAL, causal_bf, qt, kt)
                pe_scores(pe, A, u, 1, CAUSAL, causal_bf, qt, kt)
            if last:
                pe.wait_ge(A["ot_done"], w * 4 + 4)
                pe.wait_ge(A["gatet_done"], w + 1)
                for t in range(T):
                    acc = ov[0][:, D * t:D * t + D]
                    for c in range(8):
                        pe.matmul(acc, ot[:, c, P * t:P * t + P], w_o[:, c, :], start=(c == 0), stop=False)
                    for c in range(4):
                        pe.matmul(acc, moe_t[:, c, P * t:P * t + P], w_moe2[:, c, :], start=False, stop=False)
                    pe.matmul(acc, gate_t[:, P * t:P * t + P], b_moe2[:, :], start=False, stop=True).then_inc(A["wo_done"], 1)
            if old:
                pe.wait_ge(A["gate_in"], u * T + T)

            def extra(h):
                if old and last and h == 0:
                    pe.wait_ge(A["state_done"], w + 1)
                if new and h == 3:
                    pe.wait_ge(A["xn_done"], i * T + T)
                    wait(pe, A["moe_gelu"], i * T)
                    for t in range(T):
                        m = pe.transpose(pj[1][:, P * t:P * t + P], xn[:, t, :], ident[:, :])
                    m.then_inc(A["tr_x"], 1)
                if new and h in A_PAIR:
                    p = h - A_PAIR[0]
                    if p == 0:
                        pe.wait_ge(A["xt_done"], i + 1)
                    wait(pe, A["qk_done"], i * 8 + p)
                    for n in range(2):
                        m = pe.matmul(pj[1][:, S * n:S * n + S], w_big[:, INNER * n + P * p:INNER * n + P * p + P],
                                      xt2[:, :], start=True, stop=True)
                    m.then_inc(A["qkt_done"], 1)
                if old and h in (4, 5):
                    t = h - 4
                    pe.wait_ge(A["moe_gated"], u * T + t + 1)
                    wait(pe, A["moet_done"], u * T + t)
                    for c in range(4):
                        m = pe.transpose(pj[0][:, P * c:P * c + P], rb[:, t, P * c:P * c + P], ident[:, :])
                    m.then_inc(A["moe_tr"], 1)
                if old and h == 6:
                    pe.wait_ge(A["moet_done"], u * T + T)
                    for t in range(T):
                        m = pe.transpose(pj[0][0:NE, P * t:P * t + P], lg[:, t, 56:64], ident[:, :])
                    m.then_inc(A["gate_tr"], 1)
            if not old:
                for h in range(H):
                    extra(h)
                return
            pe_heads(pe, A, u, CAUSAL, causal_bf, extra)

        moe_t = sq[:, :, :].rearrange("p a n -> p (a n)").rearrange("p (c n) -> p c n", c=4)

        def a_dve(dve, i):
            new, old, last = a_stages(i)
            u, w = i - 1, i - 2
            if new:
                link_p = chain(dve, A["link_p"], i, 3)
                x_new = [x[:, bass.ds(i * T + t, 1), :].rearrange("p a n -> p (a n)") for t in range(T)]
            if old:
                link = chain(dve, A["link_a"], u, 18)
                dve.wait_ge(A["qk_done"], u * 8 + 8)
                dve.tensor_copy(qt[:, :, :], rq[:, :, 0:S]).then_inc(A["qk_moved"], 1)
                for g in (1, 3):
                    dve.wait_ge(A["tr_v"], u * 4 + g + 1)
                    wait(dve, A["v_done"], u * 4 + g)
                    dve.tensor_copy(v[:, g // 2, 512:1024], pj[1][:, :]).then_inc(A["v_done"], 1)
            if last:
                for g in (1, 3):
                    out_copy(dve, A, w, g, dve.tensor_copy)
            if old:
                dve.wait_ge(A["route_ps"], u + 1)
                dve.wait_ge(A["sumsq"], u * T + T)
                for t in range(T):
                    q = lg[:, t, :]
                    link(dve.tensor_scalar(q[:, 32:40], ov[1][:, 16 * t:16 * t + 8], sm[:, t, 4:5], None, ALU.mult))
                    link(dve.tensor_tensor(q[:, 0:8], q[:, 32:40], ov[1][:, 16 * t + 8:16 * t + 16], ALU.add))
                    dve.tensor_copy(carrier[:, 0:1], eps_c[:, 0:1])
                    link(dve.max(q[:, 8:16], q[:, 0:8]))
                    link(dve.tensor_scalar(q[:, 40:41], q[:, 8:9], -1.0, None, ALU.mult))
                    dve.tensor_scalar(q[:, 24:32], q[:, 0:8], q[:, 9:10], None, ALU.is_ge).then_inc(A["gate_in"], 1)


            def extra(h):
                if last and h == 0:
                    dve.wait_ge(A["wo_done"], w * T + T)
                    xs = x[:, bass.ds(w * T, T), :]
                    dve.tensor_tensor(xs, xs, ov[0][:, 0:T * D].rearrange("p (t n) -> p t n", t=T), ALU.add
                                      ).then_inc(A["state_done"], 1)
                if new and h == 0:
                    for t in range(T):
                        stats(dve, link_p, x_new[t], st[:, t, :], mv[:, t, :]).then_inc(A["mean_done"], 1)
                if new and h == 2:
                    for t in range(T):
                        dve.wait_ge(A["xnorm_done"], i * T + t + 1)
                        dve.tensor_scalar(xn[:, t, :], x_new[t], mv[:, t, 0:1], sm[:, t, 0:1], ALU.subtract, ALU.mult
                                          ).then_inc(A["xn_done"], 1)
                if new and h == 3:
                    dve.wait_ge(A["tr_x"], i + 1)
                    dve.tensor_copy(xt2[:, :], pj[1][:, 0:S]).then_inc(A["xt_done"], 1)
                if new and h == 4:
                    dve.wait_ge(A["xn_done"], i * T + T)
                    for t in range(T):
                        m = dve.tensor_tensor_reduce(hid[:, t, 0:D], xn[:, t, :], xn[:, t, :], 1.0, 0.0, ALU.mult, ALU.add,
                                                     sm[:, t, 5:6])
                    link_p(m)
                    dve.tensor_scalar(sm[:, :, 2:3], sm[:, :, 5:6], 1e-24, None, ALU.max).then_inc(A["sumsq_in"], 1)
                if new and h in A_PAIR and (h - A_PAIR[0]) % 2 == 1:
                    p = h - A_PAIR[0]
                    dve.wait_ge(A["qkt_done"], i * 8 + p + 1)
                    dve.wait_ge(A["qk_done"], i * 8 + p)
                    if p == 1:
                        wait(dve, A["qk_moved"], i * 2)
                    dve.tensor_scalar(rq[:, p, 0:S], pj[1][:, 0:S], 0.125, None, ALU.mult)
                    dve.tensor_copy(rq[:, p, S:2 * S], pj[1][:, S:2 * S]).then_inc(A["qk_done"], 1)
                if new and h == H - 1:
                    dve.wait_ge(A["xt_done"], i + 1)
                    dve.tensor_copy(xt[:, :], xt2[:, :]).then_inc(A["xt_now"], 1)
                if old and h == 1:
                    for t in range(T):
                        q = lg[:, t, :]
                        dve.wait_ge(A["gate_exp"], u * T + t + 1)
                        link(dve.tensor_tensor(q[:, 24:32], q[:, 24:32], q[:, 16:24], ALU.mult))
                        link(dve.tensor_reduce(q[:, 41:42], q[:, 24:32], AX.X, ALU.add))
                        link(dve.reciprocal(q[:, 42:43], q[:, 41:42]))
                        link(dve.tensor_scalar(q[:, 56:64], q[:, 24:32], q[:, 42:43], None, ALU.mult))
                    dve.tensor_copy(carrier[:, 0:1], eps_c[:, 0:1]).then_inc(A["lg_done"], 1)
                if old and h in (4, 5):
                    t = h - 4
                    dve.wait_ge(A["moe_tr"], u * T + t + 1)
                    dve.tensor_copy(moe_t[:, :, P * t:P * t + P], pj[0][:, :].rearrange("p (c n) -> p c n", c=4)
                                    ).then_inc(A["moet_done"], 1)
                if old and h == 6:
                    dve.wait_ge(A["gate_tr"], u + 1)
                    dve.tensor_copy(gate_t[:, :], pj[0][0:NE, 0:S]).then_inc(A["gatet_done"], 1)
            if not old:
                for h in range(H):
                    extra(h)
                return
            dve_heads(dve, A, u, CAUSAL, link, extra)
            dve_norm(dve, A, u, 1, link)
            assert link.n[0] == link.per, link.n

        def a_act(act, i):
            new, old, last = a_stages(i)
            u, w = i - 1, i - 2
            if new:
                link_p = chain(act, A["alink_p"], i, 4)
            if old:
                act.preload_act_table_set("gelu_and_others")
                act.wait_ge(A["qk_done"], u * 8 + 8)
                act.activation(kt[:, :, :], rq[:, :, S:2 * S], ACT.Copy).then_inc(A["qk_moved"], 1)
                for g in (0, 2):
                    act.wait_ge(A["tr_v"], u * 4 + g + 1)
                    wait(act, A["v_done"], u * 4 + g)
                    act.activation(v[:, g // 2, 0:512], pj[0][:, :], ACT.Copy).then_inc(A["v_done"], 1)
            if last:
                for g in (0, 2):
                    out_copy(act, A, w, g, lambda o_, i_: act.activation(o_, i_, ACT.Copy))
            if old:
                for t in range(T):
                    act.wait_ge(A["moe_h"], u * T + t + 1)
                    act.activation(rb[:, t, :], pj[t][:, :], ACT.Gelu).then_inc(A["moe_gelu"], 1)
            act.preload_act_table_set("natural_log_exp_and_others")

            def extra(h):
                if old and h == 0:
                    for t in range(T):
                        q = lg[:, t, :]
                        act.wait_ge(A["gate_in"], u * T + t + 1)
                        act.activation(q[:, 16:24], q[:, 0:8], ACT.Exp, bias=q[:, 40:41]).then_inc(A["gate_exp"], 1)
                if new and h == 1:
                    for t in range(T):
                        act.wait_ge(A["mean_done"], i * T + t + 1)
                        rstd(act, link_p, mv[:, t, :], sm[:, t, 0:2]).then_inc(A["xnorm_done"], 1)
                if new and h == 5:
                    for t in range(T):
                        act.wait_ge(A["sumsq_in"], i + 1)
                        link_p(act.activation(sm[:, t, 3:4], sm[:, t, 2:3], ACT.Ln, scale=2.0 ** 20))
                        act.activation(sm[:, t, 4:5], sm[:, t, 3:4], ACT.Exp, scale=-0.5, bias=eps_c[:, 1:2]
                                       ).then_inc(A["sumsq"], 1)
                if new and h in A_PAIR and (h - A_PAIR[0]) % 2 == 0:
                    p = h - A_PAIR[0]
                    act.wait_ge(A["qkt_done"], i * 8 + p + 1)
                    wait(act, A["qk_done"], i * 8 + p)
                    if p == 0:
                        wait(act, A["qk_moved"], i * 2)
                    act.activation(rq[:, p, 0:S], pj[1][:, 0:S], ACT.Copy, scale=0.125)
                    act.activation(rq[:, p, S:2 * S], pj[1][:, S:2 * S], ACT.Copy).then_inc(A["qk_done"], 1)
            if not old:
                for h in range(H):
                    extra(h)
                return
            act_heads(act, A, u, CAUSAL, extra)

        def c_stages(i):
            known = isinstance(i, int)
            return not known or i < NB, not known or i > 0

        def c_pe(pe, i, par):
            front, back = c_stages(i)
            k = i - 1
            if back:
                dec, sqs = c_dec[1 - par], c_sq[1 - par]
                wait(pe, C["flag_out"], k)
                wait(pe, C["yt_done"], k * T)
                pe.wait_ge(C["dec_done"], k * 3 + 3)
                pe.wait_ge(C["sq_out"], k * T + T)
                pe.wait_ge(C["zx_out"], k * T + T)
                for h in range(SH):
                    pe.matmul(ov[0][:, P * h:P * h + P], dec[:, h, 0:P], sqs[:, 0, h, :], start=True, stop=True)
                    pe.matmul(ov[1][:, P * h:P * h + P], dec[:, h, P:2 * P], sqs[:, 0, h, :], start=True, stop=False)
                    m = pe.matmul(ov[1][:, P * h:P * h + P], dec[:, h, 2 * P:3 * P], sqs[:, 1, h, :], start=False, stop=True)
                m.then_inc(C["guard_ps"], 1)
            if back:
                gm, xs = c_gm[1 - par], c_x[1 - par]
                pe.wait_ge(C["gm_done"], k + 1)
                wait(pe, C["x_done"], k)
                for h in range(SH):
                    c = slice(64 * h, 64 * h + 64)
                    c1 = slice(DI + 64 * h, DI + 64 * h + 64)
                    pe.matmul(tp[1][:, c], gm[:, h, 0:P], xs[:, 0, c], start=True, stop=True)
                    pe.matmul(tp[1][:, c1], gm[:, h, P:2 * P], xs[:, 0, c], start=True, stop=False)
                    m = pe.matmul(tp[1][:, c1], gm[:, h, 2 * P:3 * P], xs[:, 1, c], start=False, stop=True)
                m.then_inc(C["y_ps"], 1)
            if front:
                pe.wait_ge(C["xn_done"], i * T + T)
                wait(pe, C["arg_done"], i * 8)
                for t in range(T):
                    m = pe.transpose(tp[0][:, P * t:P * t + P], xn[:, t, :], ident[:, :])
                m.then_inc(C["tr_x"], 1)
            if front:
                pe.wait_ge(C["xt_done"], i + 1)
                wait(pe, C["dec_done"], i * 3)
                wait(pe, C["gm_done"], i)
                for t in range(T):
                    pe.matmul(pj[t][:, :], xt[:, P * t:P * t + P], w_in[:, 0:512], start=True, stop=True).then_inc(C["zx"], 1)
                    pe.matmul(bcd_bank[t], xt[:, P * t:P * t + P], w_in[:, 512:644], start=True, stop=True
                              ).then_inc(C["bcd"], 1)
                for n in range(2):
                    m = pe.matmul(sc[0][0:NS, S * n:S * n + S], w_in[:, 512 + NS * n:512 + NS * n + NS], xt[:, :],
                                  start=True, stop=True)
                m.then_inc(C["bct"], 1)
            if back:
                pe.wait_ge(C["gmx_done"], k + 1)
                pe.transpose(ov[0][0:1, 0:P], flag[:, 0:1], ident[:, :]).then_inc(C["flag_tr"], 1)
            if front:
                pe.wait_ge(C["soft"], i + 1)
                pe.wait_ge(C["bcd_out"], i * T + T)
                pe.matmul(tp[0][:, 0:8], triu[:, :], dts[:, 8, :], start=True, stop=True)
                pe.matmul(tp[0][:, 8:16], ones[:, :], dts[:, 8, :], start=True, stop=True).then_inc(C["cums"], 1)
                pe.wait_ge(C["lb_done"], i + 1)
                pe.wait_ge(C["zx_out"], i * T + T)
                for g in range(8):
                    m = pe.matmul(pj[g // 4][:, P * (g % 4):P * (g % 4) + P], c_lb[:, g, :], triu[:, :], start=True, stop=True)
                    if g % 4 == 3:
                        m.then_inc(C["lrow"], 1)
            if front:
                pe.wait_ge(C["bct_out"], i + 1)
                for n, (s_, t_) in enumerate(((0, 0), (0, 1), (1, 1))):
                    m = pe.matmul(sc[1][:, P * n:P * n + P], c_bt[:, P * s_:P * s_ + P], c_ct[:, P * t_:P * t_ + P],
                                  start=True, stop=True)
                m.then_inc(C["g_ps"], 1)
            if back:
                for t in range(T):
                    pe.wait_ge(C["yn_done"], k * T + t + 1)
                    for c in range(2):
                        m = pe.transpose(ov[1][:, DI * t + P * c:DI * t + P * c + P], c_yn[:, t, P * c:P * c + P], ident[:, :])
                    m.then_inc(C["yn_tr"], 1)
                pe.wait_ge(C["yt_done"], k * T + T)
                pe.wait_ge(C["y_out"], k * T + T)
                for t in range(T):
                    for c in range(2):
                        m = pe.matmul(tp[1][:, D * t:D * t + D], c_yt[:, c, P * t:P * t + P], w_out[:, c, :],
                                      start=(c == 0), stop=(c == 1))
                m.then_inc(C["o_ps"], 1)

        bcd_bank = [tp[0][:, 256:256 + 132], sc[1][:, 0:132]]

        def c_dve(dve, i, par):
            front, back = c_stages(i)
            k = i - 1
            link = chain(dve, C["link_f"], i, N_LINK_F)
            link_b = chain(dve, C["link_b"], k, N_LINK_B)
            d = [dts[:, n, :] for n in range(10)]
            if front:
                x_t = [x[:, bass.ds(i * T + t, 1), :].rearrange("p a n -> p (a n)") for t in range(T)]
                y_t = [y[:, bass.ds(i * T + t, 1), :].rearrange("p a n -> p (a n)") for t in range(T)]
                for t in range(T):
                    stats(dve, link, x_t[t], st[:, t, :], mv[:, t, :]).then_inc(C["mean0"], 1)
            if front:
                for t in range(T):
                    dve.wait_ge(C["rstd0"], i * T + t + 1)
                    link(dve.tensor_scalar(y_t[t], x_t[t], mv[:, t, 0:1], sm[:, t, 0:1], ALU.subtract, ALU.mult))
                    dve.tensor_copy(carrier[:, 0:1], eps_c[:, 0:1])
                    stats(dve, link, y_t[t], st[:, t, :], mv[:, t, :]).then_inc(C["mean1"], 1)
            if front:
                for t in range(T):
                    dve.wait_ge(C["rstd1"], i * T + t + 1)
                    dve.tensor_scalar(xn[:, t, :], y_t[t], mv[:, t, 0:1], sm[:, t, 0:1], ALU.subtract, ALU.mult
                                      ).then_inc(C["xn_done"], 1)
            if back:
                dve.wait_ge(C["guard_ps"], k + 1)
                for t in range(T):
                    link_b(dve.tensor_reduce(gmx[:, t, 0:8], ov[t][:, :].rearrange("p (h n) -> p h n", n=64), AX.X, ALU.max))
                link_b(dve.tensor_tensor(gmx[:, :, 8:12], gmx[:, :, 0:8:2], gmx[:, :, 1:8:2], ALU.mult))
                dve.tensor_reduce(flag[:, 0:1], gmx[:, :, 8:12], AX.XY, ALU.max).then_inc(C["gmx_done"], 1)
            if back:
                for t in range(T):
                    m = dve.tensor_tensor(c_yn[:, t, :].rearrange("p (h n) -> p h n", h=SH),
                                          c_x[1 - par][:, t, :].rearrange("p (h n) -> p h n", h=SH),
                                          hp[:, 2, :].unsqueeze(2).broadcast_to((P, SH, 64)), ALU.mult)
                link_b(m)
            if back:
                dve.wait_ge(C["y_ps"], k + 1)
                for t in range(T):
                    dve.tensor_copy(c_y[:, t, :], tp[1][:, DI * t:DI * t + DI]).then_inc(C["y_out"], 1)
            if front:
                for t in range(T):
                    dve.wait_ge(C["bcd"], i * T + t + 1)
                    dve.tensor_copy(c_bcd[par][:, t, :], bcd_bank[t]).then_inc(C["bcd_out"], 1)
                dve.wait_ge(C["bcd_out"], i * T + T)
                dve.tensor_tensor(dts[:, 0, :].rearrange("p (t h) -> p t h", t=T), c_bcd[par][:, :, 128:132],
                                  hp[:, 1, :].unsqueeze(1).broadcast_to((P, T, SH)), ALU.add).then_inc(C["dt_in"], 1)
            if front:
                dve.wait_ge(C["dt_exp"], i + 1)
                link(dve.tensor_scalar(d[1], d[1], 1.0, None, ALU.min))
                link(dve.tensor_scalar(d[2], d[1], 2.0, None, ALU.add))
                link(dve.reciprocal(d[3], d[2]))
                link(dve.tensor_tensor(d[2], d[1], d[3], ALU.mult))
                link(dve.tensor_tensor(d[3], d[2], d[2], ALU.mult))
                link(dve.tensor_scalar(d[4], d[3], 2.0 / 7, 2.0 / 5, ALU.mult, ALU.add))
                link(dve.tensor_tensor(d[4], d[4], d[3], ALU.mult))
                link(dve.tensor_scalar(d[4], d[4], 2.0 / 3, None, ALU.add))
                link(dve.tensor_tensor(d[4], d[4], d[3], ALU.mult))
                link(dve.tensor_scalar(d[4], d[4], 2.0, None, ALU.add))
                link(dve.tensor_tensor(d[4], d[4], d[2], ALU.mult))
                link(dve.tensor_scalar(d[4], d[4], 0.001, 0.1, ALU.max, ALU.min))
                link(dve.tensor_tensor(d[5].rearrange("p (t h) -> p t h", t=T), d[4].rearrange("p (t h) -> p t h", t=T),
                                       neg_a[:, :].unsqueeze(1).broadcast_to((P, T, SH)), ALU.mult))
                dve.tensor_scalar(d[8], d[5], LN_CAP, None, ALU.min).then_inc(C["soft"], 1)
                dve.wait_ge(C["soft"], i + 1)
                dve.tensor_copy(c_lb[:, :, :], d[8].unsqueeze(2).broadcast_to((P, 8, P))).then_inc(C["lb_done"], 1)
            if back:
                dve.wait_ge(C["flag_tr"], k + 1)
                wait(dve, C["scan_ok"], k)
                dve.tensor_reduce(flag1[0:1, 0:1], ov[0][0:1, 0:P], AX.X, ALU.max).then_inc(C["flag_out"], 1)
            if back:
                dve.wait_ge(C["scan_ok"], k + 1)
                link_b(dve.tensor_copy(flag[:, 1:2], eps_c[:, 0:1]))
                link_b(dve.tensor_tensor(c_yn[:, :, :], c_yn[:, :, :], c_y[:, :, :], ALU.add))
                link_b(dve.tensor_tensor(c_yn[:, :, :], c_yn[:, :, :], c_sz[1 - par][:, :, :], ALU.mult))
                dve.tensor_copy(carrier[:, 0:1], eps_c[:, 0:1])
                for t in range(T):
                    stats(dve, link_b, c_yn[:, t, :], st_b[:, t, :], mv_b[:, t, :]).then_inc(C["mean2"], 1)
            if back:
                for t in range(T):
                    dve.wait_ge(C["rstd2"], k * T + t + 1)
                    dve.tensor_scalar(c_yn[:, t, :], c_yn[:, t, :], mv_b[:, t, 0:1], sm_b[:, t, 0:1], ALU.subtract, ALU.mult
                                      ).then_inc(C["yn_done"], 1)
            if front:
                dve.wait_ge(C["cums"], i + 1)
                dve.tensor_copy(d[6], tp[0][:, 0:8])
                link(dve.tensor_copy(d[7], tp[0][:, 8:16]))
                link(dve.tensor_tensor(d[9], d[7], d[6], ALU.subtract))
                for g in range(8):
                    dve.wait_ge(C["lrow"], i * 2 + g // 4 + 1)
                    dve.scalar_tensor_tensor(c_arg[:, g, :], pj[g // 4][:, P * (g % 4):P * (g % 4) + P], dts[:, 6, g:g + 1],
                                             later[:, :], ALU.subtract, ALU.add).then_inc(C["arg_done"], 1)
                dve.wait_ge(C["g_ps"], i + 1)
                link(dve.tensor_copy(c_g, sc[1][:, 0:384]))
            if back:
                dve.wait_ge(C["o_ps"], k + 1)
                link_b(dve.tensor_scalar(xn2[:, :, :].rearrange("p t n -> p (t n)"), tp[1][:, 0:2 * D], 10.0, -10.0,
                                         ALU.min, ALU.max))
                dve.tensor_copy(carrier[:, 0:1], eps_c[:, 0:1])
                for t in range(T):
                    stats(dve, link_b, xn2[:, t, :], st_b[:, t, :], mv_b[:, t, :]).then_inc(C["mean3"], 1)
            if front:
                dve.wait_ge(C["dec_done"], i * 3 + 3)
                dve.tensor_tensor(c_gm[par][:, :, :], c_dec[par][:, :, :], c_g.unsqueeze(1).broadcast_to((P, SH, 384)),
                                  ALU.mult).then_inc(C["gm_done"], 1)
            if back:
                for t in range(T):
                    dve.wait_ge(C["rstd3"], k * T + t + 1)
                    link_b(dve.tensor_scalar(xn2[:, t, :], xn2[:, t, :], mv_b[:, t, 0:1], sm_b[:, t, 0:1], ALU.subtract, ALU.mult))
                link_b(dve.tensor_tensor(xn2[:, :, :], xn2[:, :, :], now[:, 0, :].unsqueeze(1).broadcast_to((P, T, D)), ALU.mult))
                link_b(dve.tensor_tensor(xn2[:, :, :], xn2[:, :, :], now[:, 1, :].unsqueeze(1).broadcast_to((P, T, D)), ALU.add))
                xs = x[:, bass.ds(k * T, T), :]
                dve.tensor_tensor(xs, xs, xn2[:, :, :], ALU.add).then_inc(C["x_done"], 1)
                assert link_b.n[0] == N_LINK_B, link_b.n
            if front:
                assert link.n[0] == N_LINK_F, link.n

        N_LINK_F, N_LINK_B = 22, 16

        def c_act(act, i, par):
            front, back = c_stages(i)
            k = i - 1
            link = chain(act, C["alink_f"], i, 4)
            link_b = chain(act, C["alink_b"], k, 4)
            if front:
                for mean, done in ((C["mean0"], C["rstd0"]), (C["mean1"], C["rstd1"])):
                    for t in range(T):
                        act.wait_ge(mean, i * T + t + 1)
                        rstd(act, link, mv[:, t, :], sm[:, t, 0:2]).then_inc(done, 1)
                act.wait_ge(C["tr_x"], i + 1)
                act.activation(xt[:, :], tp[0][:, 0:S], ACT.Identity, scale=ni[:, 0:1], bias=ni[:, 1:2]).then_inc(C["xt_done"], 1)
                act.preload_act_table_set("silu_and_others")
                for t in range(T):
                    act.wait_ge(C["zx"], i * T + t + 1)
                    act.activation(c_x[par][:, t, :], pj[t][:, 256:512], ACT.Copy)
                    act.activation(c_sq[par][:, t, :, 0:64], pj[t][:, 256:512].rearrange("p (h n) -> p h n", h=SH), ACT.Square)
                    act.activation(c_sz[par][:, t, :], pj[t][:, 0:256], ACT.Silu).then_inc(C["zx_out"], 1)
                act.preload_act_table_set("natural_log_exp_and_others")
                act.wait_ge(C["dt_in"], i + 1)
                act.activation(dts[:, 1, :], dts[:, 0, :], ACT.Exp).then_inc(C["dt_exp"], 1)
                act.wait_ge(C["bct"], i + 1)
                act.activation(c_bt, sc[0][0:NS, 0:S], ACT.Copy)
                act.activation(c_ct, sc[0][0:NS, S:2 * S], ACT.Copy).then_inc(C["bct_out"], 1)
                for t in range(T):
                    act.wait_ge(C["bcd_out"], i * T + T)
                    act.activation(c_sq[par][:, t, :, 64:128], c_bcd[par][:, t, 0:NS].unsqueeze(1).broadcast_to((P, SH, NS)),
                                   ACT.Square).then_inc(C["sq_out"], 1)
            if back:
                for t in range(T):
                    act.wait_ge(C["mean2"], k * T + t + 1)
                    rstd(act, link_b, mv_b[:, t, :], sm_b[:, t, 0:2]).then_inc(C["rstd2"], 1)
            if back:
                for t in range(T):
                    act.wait_ge(C["yn_tr"], k * T + T)
                    for c in range(2):
                        m = act.activation(c_yt[:, c, P * t:P * t + P], ov[1][:, DI * t + P * c:DI * t + P * c + P],
                                           ACT.Identity, scale=lnw[:, c, 0:1], bias=lnw[:, c, 1:2])
                    m.then_inc(C["yt_done"], 1)
            if front:
                act.wait_ge(C["soft"], i + 1)
                act.activation(dec_all[par][:, :], dts[:, 8, :], ACT.Exp).then_inc(C["dec1"], 1)
            if front:
                act.wait_ge(C["arg_done"], i * 8 + 8)
                act.activation(c_dec[par][:, :, 0:P], c_arg[:, 0:4, :], ACT.Exp).then_inc(C["dec_done"], 1)
                act.activation(c_dec[par][:, :, 2 * P:3 * P], c_arg[:, 4:8, :], ACT.Exp).then_inc(C["dec_done"], 1)
                for h in range(SH):
                    m = act.activation(c_dec[par][:, h, P:2 * P], pj[1][:, P * h:P * h + P], ACT.Exp, bias=dts[:, 9, h:h + 1])
                m.then_inc(C["dec_done"], 1)
            if back:
                for t in range(T):
                    act.wait_ge(C["mean3"], k * T + t + 1)
                    rstd(act, link_b, mv_b[:, t, :], sm_b[:, t, 0:2]).then_inc(C["rstd3"], 1)

        def c_pool(pool, k, par):
            pool.wait_ge(C["flag_out"], k + 1)
            pool.wait_ge(C["y_out"], k * T + T)
            pool.wait_ge(C["dec1"], k + 1)
            pool.tensor_tensor(carrier[:, 1:2], eps_c[:, 0:1], eps_c[:, 0:1], ALU.add)
            bound = pool.value_load(flag1[0:1, 0:1].bitcast(I32))
            with pool.If(bound > int(np.float32(GUARD).view(np.int32))):
                exact_scan(pool, par)
            pool.memset(flag1[0:1, 1:2], 0.0).then_inc(C["scan_ok"], 1)

        NU = DEPTH * NB
        GROUPS = [(t, k, hf) for hf in range(2) for t in range(T) for k in range(2)]
        QK_SLOT = {2 * g: g for g in range(8)}
        V_SLOT = {1: 0, 5: 1, 7: 2, 9: 3}
        TURN_SLOT = {5: 0, 7: 1, 9: 2, 11: 3, 13: 4, 15: 5}

        def b_stages(i):
            known = isinstance(i, int)
            return [not known or 0 <= i - n < NU for n in (-1, 0, 1, 2, 3)]

        def layer_of(n):
            return n // NB

        def read_out(pe, *uses):
            for there, s, n in uses:
                if there:
                    return wait(pe, s, n)

        def b_pe(pe, i, par):
            nxt, new, att, ffn, last = b_stages(i)
            u, w, z = i - 1, i - 2, i - 3
            qk_out, v_out, raw_out = B["qkt_done"], B["v_done"], B["raw_done"]
            ot_out, hid_out = B["ot_done"], B["hid_out"]

            def turn_qk(n, g):
                pe.wait_ge(B["rot_done"], n * 8 + g + 1)
                for j in range(4):
                    m = pe.transpose(pj[0][:, P * j:P * j + P], rq[:, g, P * j:P * j + P], ident[:, :])
                m.then_inc(B["qkt_ready"], 1)

            def turn_out(n, g, bank):
                hf, t = g // 2, g % 2
                pe.wait_ge(B["o_done"], n * 2 + hf + 1)
                for j in range(4):
                    m = pe.transpose(bank[:, P * j:P * j + P], o[:, t, 512 * hf + P * j:512 * hf + P * j + P], ident[:, :])
                m.then_inc(B["o_tr"], 1)

            def hidden(n, c, bank):
                f0, fn = FC[c]
                for a_ in range(2):
                    m = pe.matmul(bank[0:fn, S * a_:S * a_ + S], w_f1[:, FI * a_ + f0:FI * a_ + f0 + fn], xt2[:, :],
                                  start=True, stop=True)
                m.then_inc(B["hid_ps"], 1)

            def bank0(h):
                if h == 0 and last:
                    read_out(pe, (att, qk_out, u * 8 + 6), (True, hid_out, z * 3 + 2))
                    hidden(z, 2, pj[0])
                if h == 1 and att:
                    read_out(pe, (last, hid_out, z * 3 + 3), (True, qk_out, u * 8 + 6))
                    turn_qk(u, 6)
                if h == 2 and ffn:
                    read_out(pe, (att, qk_out, u * 8 + 7), (last, hid_out, z * 3 + 3))
                    turn_out(w, 2, pj[0])
                if h == 3 and att:
                    read_out(pe, (ffn, ot_out, w * 4 + 3), (True, qk_out, u * 8 + 7))
                    turn_qk(u, 7)
                if h == 4:
                    read_out(pe, (att, qk_out, u * 8 + 8), (ffn, ot_out, w * 4 + 3), (last, hid_out, z * 3 + 3))
                    if last:
                        pe.wait_ge(B["hid_done"], z * 3 + 3)
                        for t in range(T):
                            acc = pj[0][:, S + D * t:S + D * t + D]
                            for c, (f0, fn) in enumerate(FC):
                                m = pe.matmul(acc, hid[0:fn, c, P * t:P * t + P], w_f2[0:fn, c, :], start=(c == 0),
                                              stop=(c == 2))
                        m.then_inc(B["f_done"], 1)
                    if ffn:
                        pe.wait_ge(ot_out, w * 4 + 4)
                        pe.wait_ge(o_in, 16 * (layer_of(w) + 1))
                        for t in range(T):
                            for c in range(8):
                                m = pe.matmul(pj[0][:, D * t:D * t + D], ot[:, c, P * t:P * t + P], w_o[:, c, :],
                                              start=(c == 0), stop=(c == 7))
                        m.then_inc(B["wo_done"], 1)
                if h in TURN_SLOT and new:
                    g = TURN_SLOT[h]
                    if g == 0:
                        read_out(pe, (att and not ffn, qk_out, u * 8 + 8), (ffn, B["mid_done"], w + 1))
                        if last:
                            pe.wait_ge(B["state_done"], z + 1)
                    else:
                        between = {1: (ffn, B["midt_done"], w + 1), 2: (ffn, B["back_out"], w + 1),
                                   3: (att, ot_out, u * 4 + 1), 4: (ffn, B["xt2_done"], w + 1),
                                   5: (nxt, B["xt_done"], i + 2)}[g]
                        read_out(pe, between, (True, qk_out, i * 8 + g))
                    turn_qk(i, g)
                if h == 6 and ffn:
                    read_out(pe, (new, qk_out, i * 8 + 1), (last, B["state_done"], z + 1))
                    pe.wait_ge(B["mid_done"], w + 1)
                    for t in range(T):
                        m = pe.transpose(pj[0][:, P * t:P * t + P], mid[:, t, :], ident[:, :])
                    m.then_inc(B["mid_tr"], 1)
                if h == 8 and ffn:
                    read_out(pe, (new, qk_out, i * 8 + 2))
                    pe.wait_ge(B["midt_done"], w + 1)
                    for t in range(T):
                        m = pe.transpose(pj[0][:, P * t:P * t + P], xsf[:, P * t:P * t + P], ident[:, :])
                    m.then_inc(B["back_tr"], 1)
                if h == 10 and att:
                    read_out(pe, (new, qk_out, i * 8 + 3), (ffn, B["back_out"], w + 1))
                    turn_out(u, 0, pj[0])
                if h == 12 and ffn:
                    read_out(pe, (new, qk_out, i * 8 + 4), (att, ot_out, u * 4 + 1))
                    pe.wait_ge(B["xn2_done"], w * T + T)
                    for t in range(T):
                        m = pe.transpose(pj[0][:, P * t:P * t + P], xn2[:, t, :], ident[:, :])
                    m.then_inc(B["xn2_tr"], 1)
                if h == 14 and nxt:
                    read_out(pe, (new, qk_out, i * 8 + 5))
                    pe.wait_ge(B["cur_in"], i + 2)
                    for t in range(T):
                        m = pe.transpose(pj[0][:, P * t:P * t + P], cur[:, t, :], ident[:, :])
                    m.then_inc(B["tr_x"], 1)

            def bank1(h):
                if h in QK_SLOT and new:
                    g = QK_SLOT[h]
                    if g == 0:
                        pe.wait_ge(B["xt_done"], i + 1)
                        pe.wait_ge(qk_in, 16 * (layer_of(i) + 1))
                    if g == 4:
                        pe.wait_ge(qk2_in, 16 * (layer_of(i) + 1))
                    before = {0: ((last, hid_out, z * 3 + 2), (att, raw_out, u * 8 + 8)),
                              1: ((True, v_out, i * 4 + 1),),
                              2: ((ffn, ot_out, w * 4 + 4), (True, raw_out, i * 8 + 2)),
                              3: ((True, v_out, i * 4 + 2),),
                              4: ((True, v_out, i * 4 + 3),),
                              5: ((True, v_out, i * 4 + 4),),
                              6: ((att, ot_out, u * 4 + 2), (True, raw_out, i * 8 + 6)),
                              7: ((ffn, hid_out, w * 3 + 1), (True, raw_out, i * 8 + 7))}[g]
                    read_out(pe, *before)
                    t, k, hf = GROUPS[g]
                    c = INNER * k + 512 * hf
                    pe.matmul(pj[1][:, :], xshs[par][:, P * t:P * t + P], w_big[:, c:c + 512], start=True, stop=True
                              ).then_inc(B["proj"], 1)
                if h in V_SLOT and new:
                    g = V_SLOT[h]
                    if g == 0:
                        pe.wait_ge(v_in, 16 * (layer_of(i) + 1))
                    pe.wait_ge(raw_out, i * 8 + h // 2 + 1)
                    t, c = g // 2, g % 2
                    pe.matmul(pj[1][:, :], xshs[par][:, P * t:P * t + P],
                              w_big[:, 2 * INNER + 512 * c:2 * INNER + 512 * c + 512], start=True, stop=True
                              ).then_inc(B["v_ps"], 1)
                if h == 3 and ffn:
                    read_out(pe, (new, raw_out, i * 8 + 2), (last, hid_out, z * 3 + 2))
                    turn_out(w, 3, pj[1])
                if h == 11 and att:
                    read_out(pe, (new, raw_out, i * 8 + 6), (ffn, ot_out, w * 4 + 4))
                    turn_out(u, 1, pj[1])
                if h == 13 and ffn:
                    read_out(pe, (new, raw_out, i * 8 + 7), (att, ot_out, u * 4 + 2))
                    pe.wait_ge(B["xt2_done"], w + 1)
                    pe.wait_ge(f_in, 16 * 4 * (layer_of(w) + 1))
                    hidden(w, 0, pj[1])
                if h == 15 and ffn:
                    read_out(pe, (new, raw_out, i * 8 + 8), (True, hid_out, w * 3 + 1))
                    hidden(w, 1, pj[1])

            def weigh(h):
                if h == 0 and ffn:
                    pe_weigh(pe, B, w, H - 1, vs[par])
                if h > 0 and att:
                    if h == 1:
                        pe.wait_ge(v_out, u * 4 + 4)
                    pe_weigh(pe, B, u, h - 1, vs[1 - par])

            for h in range(H):
                if att:
                    pe_turn(pe, B, u, h, LOCAL)
                if h + 2 < H and att:
                    if h + 2 == HALF:
                        pe.wait_ge(qk_out, u * 8 + 8)
                    pe_scores(pe, B, u, h + 2, LOCAL, local_bf, qts[1 - par], kts[1 - par])
                if h + 2 >= H and new:
                    if h + 2 == H:
                        pe.wait_ge(qk_out, i * 8 + 4)
                    pe_scores(pe, B, i, h + 2 - H, LOCAL, local_bf, qts[par], kts[par])
                late = h in (1, 9)
                if not late:
                    weigh(h)
                bank1(h)
                bank0(h)
                if late:
                    weigh(h)

        def shifted(dve, dst, src, done):
            dve.tensor_copy(dst[0:64, :], src[0:64, 0:S])
            dve.tensor_copy(dst[64:128, 1:S], src[64:128, 0:S - 1]).then_inc(done, 1)

        def turned(eng, n, par, g, copy):
            t, k, hf = GROUPS[g]
            eng.wait_ge(B["qkt_ready"], n * 8 + g + 1)
            wait(eng, B["qkt_done"], n * 8 + g)
            copy((kts if k else qts)[par][:, 4 * hf:4 * hf + 4, P * t:P * t + P],
                 pj[0][:, :].rearrange("p (c n) -> p c n", c=4)).then_inc(B["qkt_done"], 1)

        def raw_copy(eng, n, g, copy):
            eng.wait_ge(B["proj"], n * 8 + g + 1)
            wait(eng, B["rot_cos"], after(n * 8, g - 1))
            wait(eng, B["rot_sin"], after(n * 8, g - 1))
            copy(raw[:, g % 2, :], pj[1][:, :]).then_inc(B["raw_done"], 1)

        def turned_out(eng, n, g, bank, copy):
            hf, t = g // 2, g % 2
            eng.wait_ge(B["o_tr"], n * 4 + g + 1)
            wait(eng, B["ot_done"], n * 4 + g)
            copy(ot[:, 4 * hf:4 * hf + 4, P * t:P * t + P], bank[:, :].rearrange("p (c n) -> p c n", c=4)
                 ).then_inc(B["ot_done"], 1)

        def b_dve(dve, i, par):
            nxt, new, att, ffn, last = b_stages(i)
            u, w, z = i - 1, i - 2, i - 3
            link = chain(dve, B["link_a"], u, 1)
            link_n = chain(dve, B["link_n"], w, 1)
            link_f = chain(dve, B["link_f"], w, 2)

            def squares(n, g):
                if not isinstance(n, int) or n > 0:
                    dve.wait_ge(B["rot_done"], n * 8 + g - 7)
                dve.wait_ge(B["sq_done"], n * 8 + g + 1)
                dve.tensor_reduce(ss[:, g, :], sq[:, g % 2, :].rearrange("p (h e) -> p h e", h=HALF), AX.X, ALU.add
                                  ).then_inc(B["ssq_done"], 1)
                dve.wait_ge(B["ssq_done"], n * 8 + g + 1)
                dve.tensor_scalar(ss[:, g, :], ss[:, g, :], 1e-24, None, ALU.max).then_inc(B["ssum_done"], 1)

            def cos_part(n, g):
                t, k, hf = GROUPS[g]
                dve.wait_ge(B["raw_done"], n * 8 + g + 1)
                if g == 0:
                    dve.wait_ge(tabs_done, (layer_of(n) + 1) * N_TABS)
                if not isinstance(n, int) or n > 0:
                    dve.wait_ge(B["qkt_ready"], n * 8 + g - 7)
                dve.tensor_tensor(rq[:, g, :].rearrange("p (h e) -> p h e", h=HALF),
                                  raw[:, g % 2, :].rearrange("p (h e) -> p h e", h=HALF),
                                  tabs[:, 2 * k, t, :].unsqueeze(1).broadcast_to((P, HALF, DH)), ALU.mult
                                  ).then_inc(B["rot_cos"], 1)

            def copy_out(h):
                if h == 0 and att:
                    turned(dve, u, 1 - par, 5, dve.tensor_copy)
                if h == 2 and att:
                    turned(dve, u, 1 - par, 6, dve.tensor_copy)
                if h == 3 and new:
                    raw_copy(dve, i, 1, dve.tensor_copy)
                if h == 4 and ffn:
                    turned_out(dve, w, 3, pj[1], dve.tensor_copy)
                if h == 5 and ffn:
                    dve.wait_ge(B["wo_done"], w + 1)
                    if last:
                        dve.wait_ge(B["mid_kept"], z + 1)
                    dve.tensor_tensor(mid[:, :, :], y[:, bass.ds((w % NB) * T, T), :],
                                      pj[0][:, 0:2 * D].rearrange("p (t n) -> p t n", t=T), ALU.add
                                      ).then_inc(B["mid_done"], 1)
                if h == 5 and last:
                    dve.wait_ge(B["f_done"], z + 1)
                    if not ffn:
                        dve.wait_ge(B["mid_kept"], z + 1)
                    ys = y[:, bass.ds((z % NB) * T, T), :]
                    dve.tensor_tensor(ys, ys, pj[0][:, S:S + 2 * D].rearrange("p (t n) -> p t n", t=T), ALU.add
                                      ).then_inc(B["state_done"], 1)
                if h == 7 and ffn:
                    dve.wait_ge(B["mid_tr"], w + 1)
                    shifted(dve, xsf, pj[0], B["midt_done"])
                if h == 8 and new:
                    turned(dve, i, par, 1, dve.tensor_copy)
                if h == 12:
                    if new:
                        turned(dve, i, par, 3, dve.tensor_copy)
                    if att:
                        turned_out(dve, u, 1, pj[1], dve.tensor_copy)
                if h == 13 and ffn:
                    dve.wait_ge(B["xn2_tr"], w + 1)
                    gb = ln_gb[:, bass.ds(layer_of(w), 1), :].rearrange("p a n -> p (a n)")
                    dve.tensor_scalar(xt2[:, :], pj[0][:, 0:S], gb[:, 0:1], gb[:, 1:2],
                                      ALU.mult, ALU.add).then_inc(B["xt2_done"], 1)
                if h == 15 and nxt:
                    dve.wait_ge(B["tr_x"], i + 2)
                    shifted(dve, xshs[1 - par], pj[0], B["xt_done"])

            def extra(h):
                if ffn and h == 0:
                    dve_norm(dve, B, w, 1, link_n)
                if att and h == 8:
                    dve_norm(dve, B, u, 0, link)
                if new and h % 2 == 1:
                    cos_part(i, h // 2)
                if att and h == 0:
                    squares(u, 7)
                if new and h % 2 == 0 and h > 0:
                    squares(i, h // 2 - 1)
                if last and h == 2:
                    fb = b_f1[:, bass.ds(layer_of(z), 1), :].rearrange("p a n -> p (a n)")
                    for c, (f0, fn) in enumerate(FC):
                        dve.wait_ge(B["hid_gelu"], z * 3 + c + 1)
                        dve.scalar_tensor_tensor(hid[0:fn, c, :], hsb[0:fn, c, 0:S], fb[0:fn, c:c + 1],
                                                 gel[0:fn, c, :], ALU.add, ALU.mult).then_inc(B["hid_done"], 1)
                if ffn and h == 9:
                    dve.wait_ge(B["back_out"], w + 1)
                    for t in range(T):
                        stats(dve, link_f, xm[:, t, :], st[:, t, :], mv[:, t, :]).then_inc(B["mean"], 1)
                if ffn and h == 11:
                    for t in range(T):
                        dve.wait_ge(B["rstd"], w * T + t + 1)
                        dve.tensor_scalar(xn2[:, t, :], xm[:, t, :], mv[:, t, 0:1], sm[:, t, 0:1],
                                          ALU.subtract, ALU.mult).then_inc(B["xn2_done"], 1)

            for h in range(H):
                copy_out(h)
                if att and on_dve(h):
                    pt_copy(dve, B, u, h, LOCAL, dve.tensor_copy)
                if h + 2 < H and att:
                    dve_top(dve, B, u, h + 2, LOCAL)
                if h + 2 >= H and new:
                    dve_top(dve, B, i, h + 2 - H, LOCAL)
                extra(h)

        def b_act(act, i, par):
            nxt, new, att, ffn, last = b_stages(i)
            u, w, z = i - 1, i - 2, i - 3
            link = chain(act, B["alink_p"], i, 7)
            link_7 = chain(act, B["alink_7"], u, 1)
            link_f = chain(act, B["alink_f"], w, 2)
            copy = lambda o_, i_: act.activation(o_, i_, ACT.Copy)

            def factor(n, g, link):
                act.wait_ge(B["ssum_done"], n * 8 + g + 1)
                link(act.activation(ss[:, g, :], ss[:, g, :], ACT.Ln, scale=2.0 ** 20))
                act.activation(ss[:, g, :], ss[:, g, :], ACT.Exp, scale=-0.5, bias=eps_c[:, 1:2]).then_inc(B["r_done"], 1)

            def hidden_out(n, c, bank):
                fn = FC[c][1]
                act.wait_ge(B["hid_ps"], n * 3 + c + 1)
                copy(hsb[0:fn, c, :], bank[0:fn, :]).then_inc(B["hid_out"], 1)

            def copy_out(h):
                if new and h % 2 == 1 and h != 3:
                    raw_copy(act, i, h // 2, copy)
                if h == 0 and last:
                    hidden_out(z, 1, pj[1])
                if h == 1 and last:
                    hidden_out(z, 2, pj[0])
                if h == 4 and att:
                    turned(act, u, 1 - par, 7, copy)
                if h == 3 and ffn:
                    turned_out(act, w, 2, pj[0], copy)
                if h in (6, 10, 14) and new:
                    turned(act, i, par, (h - 6) // 2, copy)
                if h == 9 and ffn:
                    act.wait_ge(B["back_tr"], w + 1)
                    copy(xm[:, :, :].rearrange("p t n -> p (t n)"), pj[0][:, 0:S]).then_inc(B["back_out"], 1)
                if h == 11 and att:
                    turned_out(act, u, 0, pj[0], copy)
                if h == 14 and ffn:
                    if last:
                        act.wait_ge(B["hid_done"], z * 3 + 3)
                    hidden_out(w, 0, pj[1])

            def extra(h):
                if h in V_SLOT and new:
                    g = V_SLOT[h]
                    act.wait_ge(B["v_ps"], i * 4 + g + 1)
                    copy(vs[par][:, g // 2, 512 * (g % 2):512 * (g % 2) + 512], pj[1][:, :]).then_inc(B["v_done"], 1)
                if new and h % 2 == 1:
                    g = h // 2
                    act.wait_ge(B["raw_done"], i * 8 + g + 1)
                    wait(act, B["ssum_done"], after(i * 8, g - 1))
                    act.activation(sq[:, g % 2, :], raw[:, g % 2, :], ACT.Square).then_inc(B["sq_done"], 1)
                if h == 1 and att:
                    factor(u, 7, link_7)
                if new and h % 2 == 1 and h > 1:
                    factor(i, h // 2 - 1, link)
                if h == 1 and last:
                    act.preload_act_table_set("gelu_and_others")
                    fb = b_f1[:, bass.ds(layer_of(z), 1), :].rearrange("p a n -> p (a n)")
                    act.wait_ge(B["hid_out"], z * 3 + 3)
                    for c, (f0, fn) in enumerate(FC):
                        act.activation(gel[0:fn, c, :], hsb[0:fn, c, S:2 * S], ACT.Gelu, bias=fb[0:fn, 3 + c:4 + c]
                                       ).then_inc(B["hid_gelu"], 1)
                    act.preload_act_table_set("natural_log_exp_and_others")
                if ffn and h == 10:
                    for t in range(T):
                        act.wait_ge(B["mean"], w * T + t + 1)
                        rstd(act, link_f, mv[:, t, :], sm[:, t, 0:2]).then_inc(B["rstd"], 1)

            for h in range(H):
                copy_out(h)
                if att and not on_dve(h):
                    pt_copy(act, B, u, h, LOCAL, copy)
                if h + 2 < H and att:
                    act_exp(act, B, u, h + 2, LOCAL)
                if h + 2 >= H and new:
                    act_exp(act, B, i, h + 2 - H, LOCAL)
                extra(h)

        def b_cur(pool, n, first_layer=False):
            if not first_layer:
                pool.wait_ge(B["state_done"], n - NB + 1)
            wait(pool, B["tr_x"], n)
            pool.tensor_copy(cur[:, :, :], y[:, bass.ds((n % NB) * T, T), :]).then_inc(B["cur_in"], 1)

        def b_keep(pool, n):
            pool.wait_ge(B["mid_done"], n + 1)
            pool.tensor_tensor(y[:, bass.ds((n % NB) * T, T), :], mid[:, :, :],
                               b_f2[:, bass.ds(layer_of(n), 1), :].broadcast_to((P, T, D)), ALU.add).then_inc(B["mid_kept"], 1)

        def b_sin(pool, i, g):
            t, k, hf = GROUPS[g]
            src = raw[:, g % 2, :].rearrange("p (h e) -> p h e", h=HALF)
            dst = rb[:, g % 2, :].rearrange("p (h e) -> p h e", h=HALF)
            if g == 0:
                pool.wait_ge(tabs_done, (layer_of(i) + 1) * N_TABS)
            pool.wait_ge(B["raw_done"], i * 8 + g + 1)
            for lo in (0, 32):
                m = pool.tensor_tensor(dst[:, :, lo:lo + 32], src[:, :, 32 - lo:64 - lo],
                                       tabs[:, 2 * k + 1, t, lo:lo + 32].unsqueeze(1).broadcast_to((P, HALF, 32)), ALU.mult)
            m.then_inc(B["rot_sin"], 1)

        def b_sum(pool, i, g):
            pool.wait_ge(B["rot_sin"], i * 8 + g + 1)
            pool.wait_ge(B["rot_cos"], i * 8 + g + 1)
            pool.tensor_tensor(rq[:, g, :], rq[:, g, :], rb[:, g % 2, :], ALU.add).then_inc(B["rot_sum"], 1)
            pool.wait_ge(B["rot_sum"], i * 8 + g + 1)
            pool.wait_ge(B["r_done"], i * 8 + g + 1)
            q = rq[:, g, :].rearrange("p (h e) -> p h e", h=HALF)
            pool.tensor_tensor(q, q, ss[:, g, :].unsqueeze(2).broadcast_to((P, HALF, DH)), ALU.mult
                               ).then_inc(B["rot_done"], 1)

        def b_pool(pool, i, first_layer=False, keep=True, before=True):
            if before:
                b_sum(pool, i - 1, 7)
            for g in range(3):
                b_sin(pool, i, g)
                b_sum(pool, i, g)
            if keep:
                b_keep(pool, i - 2)
            b_cur(pool, i + 1, first_layer)
            for g in range(3, 7):
                b_sin(pool, i, g)
                b_sum(pool, i, g)
            b_sin(pool, i, 7)

        @block.sync
        def _(sp):
            xin = a["x"].rearrange("b (t p) d -> p (b t) d", p=P)
            for dst, src in ((x[:, 0:T, :], xin[:, 0:T, :]), (w_big[:, :], a["w_qkv0"]), (ident[:, :], a["ident"]),
                             (cent[:, :], a["cent"]), (route[:, NE:2 * NE], a["w_route"])):
                sp.dma_start(dst, src).then_inc(first_in, 16)
            for dst, src in ((o[:, 0, 0:672], a["masks"]),
                             (w_o[:, :, :], a["w_o0"].rearrange("(c p) n -> p c n", p=P)),
                             (w_moe1[:, :], a["w_moe1"]), (w_moe2[:, :, :], a["w_moe2"].rearrange("(c p) n -> p c n", p=P)),
                             (b_moe1[:, :], a["b_moe1"]), (b_moe2[:, :], a["b_moe2"])):
                sp.dma_start(dst, src).then_inc(consts_in, 16)
            sp.dma_start(x[:, T:NB * T, :], xin[:, T:NB * T, :]).then_inc(xrest_in, 16)
            with nc.allow_non_contiguous_dma("small per-partition columns"):
                for dst, src in W2_LOADS():
                    sp.dma_start(dst, src).then_inc(w2_in, 16)
            def layer_weights(l):
                wq = a["w_qkv"][bass.ds(l, 1), :, :]
                for hf in range(2):
                    if not isinstance(l, int):
                        sp.wait_ge(B["proj"], l * NB * 8 - 4 * (1 - hf))
                    sp.dma_start(w_big[:, 0:2 * INNER].rearrange("p (k n) -> p k n", k=2)[:, :, 512 * hf:512 * hf + 512],
                                 wq[:, :, 0:2 * INNER].rearrange("a p (k n) -> p (a k) n", k=2)[:, :, 512 * hf:512 * hf + 512]
                                 ).then_inc((qk_in, qk2_in)[hf], 16)
                wait(sp, B["v_ps"], l * NB * 4)
                sp.dma_start(w_big[:, 2 * INNER:3 * INNER], wq[:, :, 2 * INNER:3 * INNER].rearrange("a p n -> p (a n)")
                             ).then_inc(v_in, 16)
                wait(sp, B["wo_done"], l * NB)
                sp.dma_start(w_o[:, :, :], a["w_o"][bass.ds(l, 1), :, :].rearrange("a (c p) n -> p (a c) n", p=P)
                             ).then_inc(o_in, 16)
                wait(sp, B["f_done"], l * NB)
                sp.dma_start(w_f1[:, :], a["w_f1"][bass.ds(l, 1), :, :].rearrange("a p n -> p (a n)")).then_inc(f_in, 16)
                for c, (f0, fn) in enumerate(FC):
                    sp.dma_start(w_f2[0:fn, c, :], a["w_f2"][bass.ds(l, 1), f0:f0 + fn, :].rearrange("a p n -> p (a n)")
                                 ).then_inc(f_in, 16)

            sp.wait_ge(A["wo_done"], NB * T)
            layer_weights(0)
            with sp.Fori(1, DEPTH) as l:
                layer_weights(l)
            xout = out.rearrange("b (t p) d -> p (b t) d", p=P)
            parts = [(0, NB // 2), (NB // 2, NB - 1), (NB - 1, NB)]
            for lo, hi in parts:
                sp.wait_ge(x_final, hi)
                sp.dma_start(xout[:, lo * T:hi * T, :], x[:, lo * T:hi * T, :]).then_inc(out_done, 16)
            sp.wait_ge(out_done, 16 * len(parts))

        @block.gpsimd
        def _(pool):
            pool.memset(ones[:, :], 1.0).then_inc(prep, 1)
            pool.memset(xsh[:, :], 0.0).then_inc(prep, 1)
            pool.memset(xsf[:, :], 0.0).then_inc(prep, 1)
            pool.memset(xshs[1][:, :], 0.0).then_inc(prep, 1)
            pool.memset(eps_c[:, 0:1], EPS).then_inc(prep, 1)
            pool.memset(eps_c[:, 1:2], float(10 * np.log(2.0))).then_inc(prep, 1)
            with pool.Fori(0, NB) as u:
                for t in range(T):
                    pool.wait_ge(A["lg_done"], u + 1)
                    pool.wait_ge(A["moe_gelu"], u * T + t + 1)
                    pool.tensor_tensor(rb[:, t, :].rearrange("p (e n) -> p e n", e=NE),
                                       rb[:, t, :].rearrange("p (e n) -> p e n", e=NE),
                                       lg[:, t, 56:64].unsqueeze(2).broadcast_to((P, NE, DE)), ALU.mult
                                       ).then_inc(A["moe_gated"], 1)
            with pool.Fori(0, NB // 2) as j:
                c_pool(pool, j * 2, 0)
                c_pool(pool, j * 2 + 1, 1)
            pool.wait_ge(A["state_done"], NB)
            pool.memset(prob[:, :, 256:352], 0.0).then_inc(prob_clear, 1)
            pool.memset(pt[:, :, 256 + WINDOW:384], 0.0).then_inc(prob_clear, 1)
            def rotary_tables(l):
                for k in range(4):
                    for lo, n, at in (((0, DH, 0),) if k % 2 == 0 else ((0, 32, 32), (32, 32, 0))):
                        pool.tensor_tensor(tabs[:, k, :, lo:lo + n], rot[:, k, :, lo:lo + n],
                                           qk_scale[:, bass.ds(l, 1), k // 2, at:at + n].broadcast_to((P, T, n)), ALU.mult
                                           ).then_inc(tabs_done, 1)

            pool.wait_ge(w2_in, 16 * N_W2)
            rotary_tables(0)
            b_cur(pool, 0, first_layer=True)
            b_pool(pool, 0, first_layer=True, keep=False, before=False)
            b_pool(pool, 1, first_layer=True, keep=False)
            with pool.Fori(2, NB - 1) as i:
                b_pool(pool, i, first_layer=True)
            b_pool(pool, NB - 1)
            with pool.Fori(1, DEPTH) as l:
                pool.wait_ge(B["rot_cos"], l * NB * 8)
                pool.wait_ge(B["rot_sin"], l * NB * 8)
                rotary_tables(l)
                with pool.Fori(0, NB) as b:
                    b_pool(pool, l * NB + b)
            b_sum(pool, NU - 1, 7)
            b_keep(pool, NU - 2)
            b_keep(pool, NU - 1)
            for b in range(NB):
                pool.wait_ge(B["state_done"], (DEPTH - 1) * NB + b + 1)
                pool.tensor_tensor(x[:, b * T:b * T + T, :], x[:, b * T:b * T + T, :], y[:, b * T:b * T + T, :],
                                   ALU.add).then_inc(x_final, 1)

        @block.tensor
        def _(pe):
            pe.wait_ge(prep_ok, 2)
            pe.wait_ge(first_in, 16 * N_FIRST)
            pe.transpose(tp[0][:, 0:NE], cent[:, :], ident[0:NE, 0:NE]).then_inc(prep_t, 1)
            pe.wait_ge(prep_ok, 3)
            pe.wait_ge(prep, 6)
            pe.wait_ge(consts_in, 16 * N_CONST)
            for i in range(3):
                a_pe(pe, i)
            with pe.Fori(3, NB) as i:
                a_pe(pe, i)
            a_pe(pe, NB)
            a_pe(pe, NB + 1)
            pe.wait_ge(w2_in, 16 * N_W2)
            pe.wait_ge(A["state_done"], NB)
            c_pe(pe, 0, 0)
            c_pe(pe, 1, 1)
            with pe.Fori(0, (NB - 2) // 2) as j:
                c_pe(pe, j * 2 + 2, 0)
                c_pe(pe, j * 2 + 3, 1)
            c_pe(pe, NB, 0)
            pe.wait_ge(C["x_done"], NB)
            pe.wait_ge(prob_clear, 2)
            for i in range(-1, 4):
                b_pe(pe, i, i % 2)
            with pe.Fori(0, (NU - 4) // 2) as j:
                b_pe(pe, j * 2 + 4, 0)
                b_pe(pe, j * 2 + 5, 1)
            for i in range(NU, NU + 3):
                b_pe(pe, i, i % 2)

        @block.vector
        def _(dve):
            dve.wait_ge(first_in, 16 * N_FIRST)
            dve.wait_ge(consts_in, 16 * N_CONST)
            dve.tensor_copy(ident_bf[:, :], ident[:, :])
            dve.tensor_copy(causal_bf[:, :], o[:, 0, 0:384])
            dve.tensor_copy(local_bf[:, :], o[:, 0, 384:672]).then_inc(prep_ok, 1)
            dve.wait_ge(prep_t, 1)
            dve.tensor_copy(route[:, 0:NE], tp[0][:, 0:NE]).then_inc(prep_ok, 1)
            dve.wait_ge(first_in, 16 * N_FIRST)
            dve.wait_ge(xrest_in, 16)
            for i in range(3):
                a_dve(dve, i)
            with dve.Fori(3, NB) as i:
                a_dve(dve, i)
            a_dve(dve, NB)
            a_dve(dve, NB + 1)
            dve.wait_ge(w2_in, 16 * N_W2)
            c_dve(dve, 0, 0)
            c_dve(dve, 1, 1)
            with dve.Fori(0, (NB - 2) // 2) as j:
                c_dve(dve, j * 2 + 2, 0)
                c_dve(dve, j * 2 + 3, 1)
            c_dve(dve, NB, 0)
            for i in range(-1, 4):
                b_dve(dve, i, i % 2)
            with dve.Fori(0, (NU - 4) // 2) as j:
                b_dve(dve, j * 2 + 4, 0)
                b_dve(dve, j * 2 + 5, 1)
            for i in range(NU, NU + 3):
                b_dve(dve, i, i % 2)

        @block.scalar
        def _(act):
            act.wait_ge(first_in, 16 * N_FIRST)
            act.wait_ge(prep, 6)
            act.activation(lg[0:NE, 0, 0:1], cent[:, 0:1], ACT.Copy).then_inc(prep_a, 1)
            act.wait_ge(prep_a, 1)
            act.activation(rb[0:NE, 0, 0:D], cent[:, :], ACT.Square, accum_out=eps_c[0:NE, 2:3]).then_inc(prep_a, 1)
            act.wait_ge(prep_a, 2)
            act.activation(eps_c[0:NE, 3:4], eps_c[0:NE, 2:3], ACT.Ln, scale=2.0 ** 20).then_inc(prep_a, 1)
            act.wait_ge(prep_a, 3)
            act.activation(eps_c[0:NE, 2:3], eps_c[0:NE, 3:4], ACT.Exp, scale=-0.5, bias=eps_c[0:NE, 1:2]).then_inc(prep_a, 1)
            act.wait_ge(prep_a, 4)
            act.activation(cent[:, :], cent[:, :], ACT.Copy, scale=eps_c[0:NE, 2:3]).then_inc(prep_ok, 1)
            for i in range(3):
                a_act(act, i)
            with act.Fori(3, NB) as i:
                a_act(act, i)
            a_act(act, NB)
            a_act(act, NB + 1)
            act.wait_ge(w2_in, 16 * N_W2)
            act.activation(neg_a[:, :], hp[:, 0, :], ACT.Exp).then_inc(prep_a, 1)
            act.wait_ge(prep_a, 5)
            act.activation(neg_a[:, :], neg_a[:, :], ACT.Copy, scale=-1.0).then_inc(prep_ok, 1)
            act.preload_act_table_set("natural_log_exp_and_others")
            c_act(act, 0, 0)
            c_act(act, 1, 1)
            with act.Fori(0, (NB - 2) // 2) as j:
                c_act(act, j * 2 + 2, 0)
                c_act(act, j * 2 + 3, 1)
            c_act(act, NB, 0)
            act.preload_act_table_set("natural_log_exp_and_others")
            for i in range(-1, 4):
                b_act(act, i, i % 2)
            with act.Fori(0, (NU - 4) // 2) as j:
                b_act(act, j * 2 + 4, 0)
                b_act(act, j * 2 + 5, 1)
            for i in range(NU, NU + 3):
                b_act(act, i, i % 2)


def host_constants():
    i = np.arange(S)
    causal = np.where(i[None, :] <= i[:, None], 0.0, MASKED)
    near = np.where((i[None, :] <= i[:, None]) & (i[None, :] >= i[:, None] - WINDOW), 0.0, MASKED)

    def pack(m, span):
        return np.concatenate([m[P * t:P * t + P, k0:k0 + kn] for t, (k0, kn) in enumerate(span)], 1)

    half = np.arange(0, DH, 2, dtype=np.float32)
    freqs = i[:, None].astype(np.float32) * (1.0 / 10000.0 ** (half / DH)).astype(np.float32)[None, :]
    freqs = np.concatenate([freqs, freqs], -1)
    power = (i.astype(np.float32) - S // 2) / (WINDOW // 2)
    scale = (((half + 0.4 * DH) / (1.4 * DH))[None, :] ** power[:, None]).astype(np.float32)
    scale = np.concatenate([scale, scale], -1)
    cos, sin = np.cos(freqs), np.sin(freqs)
    sin = np.concatenate([-sin[:, :DH // 2], sin[:, DH // 2:]], -1)
    rot = np.stack([8 * cos * scale, 8 * sin * scale, cos / scale, sin / scale]).astype(np.float32)
    r = np.arange(P)
    return {
        "ident": np.eye(P, dtype=np.float32),
        "masks": np.concatenate([pack(causal, CAUSAL), pack(near, LOCAL)], 1).astype(np.float32),
        "triu": (r[:, None] <= r[None, :]).astype(np.float32),
        "later": np.where(r[None, :] >= r[:, None], 0.0, MASKED).astype(np.float32),
        "rot": rot,
    }


def layouts(i):
    t = np.ascontiguousarray
    g = {k: np.asarray(v) for k, v in i.items()}
    return {
        "x": g["L0_attn_x"],
        "w_qkv0": t(np.concatenate([g[k].reshape(INNER, D).T for k in ("L0_attn_wq", "L0_attn_wk", "L0_attn_wv")], 1)),
        "w_o0": t(g["L0_attn_wo"].T),
        "cent": g["L0_ffn_centroids"],
        "w_route": t(g["L0_ffn_w_route"].T),
        "w_moe1": t(g["L0_ffn_w1"].transpose(1, 0, 2).reshape(D, EH)),
        "w_moe2": g["L0_ffn_w2"].reshape(EH, D),
        "b_moe1": g["L0_ffn_b1"].reshape(1, EH),
        "b_moe2": g["L0_ffn_b2"],
        "w_in": t(g["L1_attn_in_proj_w"].T),
        "w_out": t(g["L1_attn_out_proj_w"].T),
        "ni_w": g["L1_attn_ni_w"], "ni_b": g["L1_attn_ni_b"],
        "ln_w": g["L1_attn_ln_w"], "ln_b": g["L1_attn_ln_b"],
        "no_w": g["L1_attn_no_w"], "no_b": g["L1_attn_no_b"],
        "A_log": g["L1_attn_A_log"], "dt_bias": g["L1_attn_dt_bias"], "Dparam": g["L1_attn_Dparam"],
        "w_qkv": g["L1_ffn_Wqkv"], "w_o": g["L1_ffn_Wo"],
        "q_scale": g["L1_ffn_q_scale"], "k_scale": g["L1_ffn_k_scale"],
        "f_g": t(g["L1_ffn_ln_g"].T), "f_b": t(g["L1_ffn_ln_b"].T),
        "w_f1": g["L1_ffn_W1"], "w_f2": g["L1_ffn_W2"],
        "b_f1": t(g["L1_ffn_b1"].T), "b_f2": g["L1_ffn_b2"],
    }


def kernel(**inputs):
    import concourse.bacc as bacc
    from concourse.bass_utils import run_bass_kernel_spmd

    arrays = {**layouts(inputs), **host_constants()}
    nc = bacc.Bacc("TRN2", target_bir_lowering=False, num_devices=1)
    a = {n: nc.dram_tensor("in_" + n, v.shape, mybir.dt.from_np(v.dtype), kind="ExternalInput").ap()
         for n, v in arrays.items()}
    out = nc.dram_tensor("out_x", (NB, S, D), F32, kind="ExternalOutput").ap()
    program(nc, a, out)
    r = run_bass_kernel_spmd(nc, [{"in_" + n: v for n, v in arrays.items()}], core_ids=[0])
    return r.results[0]["out_x"]
```
